# Optimizing a Trainium2 kernel written in Bass

```python
import numpy as np
import jax
import jax.numpy as jnp

def _softmax(x, axis=-1):
    return jax.nn.softmax(x, axis=axis)

def _gelu(x):
    return jax.nn.gelu(x, approximate=True)

def _silu(x):
    return jax.nn.silu(x)

def _sigmoid(x):
    return jax.nn.sigmoid(x)

def _layernorm(x, axis=-1, eps=1e-05):
    m = jnp.mean(x, axis=axis, keepdims=True)
    v = jnp.var(x, axis=axis, keepdims=True)
    return (x - m) / jnp.sqrt(v + eps)

def _scatter_add(tgt, idx, src, axis=0):
    return tgt.at[idx].add(src)

def _segment_sum(src, seg, n):
    return jax.ops.segment_sum(src, seg, n)
kernel_name = 'mk_decoder_postln_d1_seqx_r4_041e54'

def setup_inputs(seed: int=0):
    np.random.seed(seed)
    _w = jnp.asarray

    def _rec_inputs():
        import jax
        import jax.numpy as jnp
        _rk = jax.random.key(seed)
        x = 7.22e-05 + 1 * jax.random.normal(jax.random.fold_in(_rk, 1), (64, 128, 256), jnp.float32)
        _lenS = 128 - jax.random.randint(jax.random.fold_in(_rk, 7), (64,), 0, max(1, 128 // 4) + 1, jnp.int32)
        _lenS2 = 128 - jax.random.randint(jax.random.fold_in(_rk, 8), (64,), 0, max(1, 128 // 4) + 1, jnp.int32)
        _ctx_1024P = jax.random.normal(jax.random.fold_in(_rk, 11), (64, 16, 256), jnp.float32)
        _ctx_1024c = jax.random.dirichlet(jax.random.fold_in(_rk, 511), 0.3 * jnp.ones((16,), jnp.float32), (64, 128))
        _ctx_1024t = jnp.einsum('bsk,bkd->bsd', _ctx_1024c, _ctx_1024P)
        _ctx_1024t = _ctx_1024t * jax.lax.rsqrt(jnp.mean(jnp.square(_ctx_1024t)) + 1e-12) * 0.953939
        ctx_1024 = 4.13588e-05 + 0.999923 * (_ctx_1024t + 0.3 * jax.random.normal(jax.random.fold_in(_rk, 611), (64, 128, 256), jnp.float32))
        return (x, ctx_1024)
    x, ctx_1024 = _rec_inputs()

    def _L0_attn_setup():
        import jax, jax.numpy as jnp
        import numpy as np
        NUM_HEADS = 16
        N_EMBD = 256

        def alibi_bias(num_heads: int, seq_len: int) -> jnp.ndarray:
            pos = jnp.arange(seq_len, dtype=jnp.float32)
            dgrid = pos[None, :] - pos[:, None]
            slopes = 2.0 ** (-8.0 / num_heads * (jnp.arange(num_heads, dtype=jnp.float32) + 1.0))
            bias = slopes[:, None, None] * dgrid[None, :, :]
            return jnp.where(dgrid[None, :, :] > 0, -jnp.inf, bias)
        key = jax.random.key(seed)
        k1, k2, k3 = jax.random.split(key, 3)
        B, L, E = (2, 512, N_EMBD)
        x = jax.random.normal(k1, (B, L, E), dtype=jnp.float32)
        w_in = jax.random.normal(k2, (3 * E, E), dtype=jnp.float32) * 0.02
        w_out = jax.random.normal(k3, (E, E), dtype=jnp.float32) * 0.02
        return {'x': x, 'w_in': w_in, 'w_out': w_out}
    _L0_attn_all = _L0_attn_setup()
    _L0_attn_in = {k: v for k, v in _L0_attn_all.items() if k in ('w_in', 'w_out')}
    del _L0_attn_all

    def _L0_xattn_setup():
        import jax, jax.numpy as jnp
        import numpy as np
        B, S, D, H = (4, 512, 256, 16)
        DK = D // H

        def _split_heads(x):
            b, s, _ = x.shape
            return x.reshape(b, s, H, DK).transpose(0, 2, 1, 3)
        key = jax.random.key(seed)
        ks = jax.random.split(key, 8)
        scale = 1.0 / np.sqrt(D)
        return {'q': jax.random.normal(ks[0], (B, S, D), jnp.float32), 'k': jax.random.normal(ks[1], (B, S, D), jnp.float32), 'v': jax.random.normal(ks[2], (B, S, D), jnp.float32), 'Wq': jax.random.normal(ks[3], (D, D), jnp.float32) * scale, 'bq': jnp.zeros((D,), jnp.float32), 'Wk': jax.random.normal(ks[4], (D, D), jnp.float32) * scale, 'bk': jnp.zeros((D,), jnp.float32), 'Wv': jax.random.normal(ks[5], (D, D), jnp.float32) * scale, 'bv': jnp.zeros((D,), jnp.float32), 'Wo': jax.random.normal(ks[6], (D, D), jnp.float32) * scale, 'bo': jnp.zeros((D,), jnp.float32)}
    _L0_xattn_all = _L0_xattn_setup()
    _L0_xattn_in = {k: v for k, v in _L0_xattn_all.items() if k in ('Wq', 'bq', 'Wk', 'bk', 'Wv', 'bv', 'Wo', 'bo')}
    del _L0_xattn_all

    def _L0_ffn_setup():
        import jax, jax.numpy as jnp
        import numpy as np
        import math
        E = 8
        K = 2
        CF = 1.2
        D = 256
        H = 1024
        key = jax.random.key(seed)
        k0, k1, k2, k3 = jax.random.split(key, 4)
        B, T = (8, 512)
        x_btd = jax.random.normal(k0, (B, T, D), jnp.float32)
        Wr = jax.random.normal(k1, (D, E), jnp.float32) / np.sqrt(D)
        br = jnp.zeros((E,), jnp.float32)
        W1 = jax.random.normal(k2, (E, D, H), jnp.float32) / np.sqrt(D)
        b1 = jnp.zeros((E, H), jnp.float32)
        W2 = jax.random.normal(k3, (E, H, D), jnp.float32) / np.sqrt(H)
        b2 = jnp.zeros((E, D), jnp.float32)
        return dict(x_btd=x_btd, Wr=Wr, br=br, W1=W1, b1=b1, W2=W2, b2=b2)
    _L0_ffn_all = _L0_ffn_setup()
    _L0_ffn_in = {k: v for k, v in _L0_ffn_all.items() if k in ('Wr', 'br', 'W1', 'b1', 'W2', 'b2')}
    del _L0_ffn_all
    return {'x': x, 'ctx_1024': ctx_1024, 'L0_attn_w_in': _L0_attn_in['w_in'], 'L0_attn_w_out': _L0_attn_in['w_out'], 'L0_xattn_Wq': _L0_xattn_in['Wq'], 'L0_xattn_bq': _L0_xattn_in['bq'], 'L0_xattn_Wk': _L0_xattn_in['Wk'], 'L0_xattn_bk': _L0_xattn_in['bk'], 'L0_xattn_Wv': _L0_xattn_in['Wv'], 'L0_xattn_bv': _L0_xattn_in['bv'], 'L0_xattn_Wo': _L0_xattn_in['Wo'], 'L0_xattn_bo': _L0_xattn_in['bo'], 'L0_ffn_Wr': _L0_ffn_in['Wr'], 'L0_ffn_br': _L0_ffn_in['br'], 'L0_ffn_W1': _L0_ffn_in['W1'], 'L0_ffn_b1': _L0_ffn_in['b1'], 'L0_ffn_W2': _L0_ffn_in['W2'], 'L0_ffn_b2': _L0_ffn_in['b2']}

def reference(x, ctx_1024, L0_attn_w_in, L0_attn_w_out, L0_xattn_Wq, L0_xattn_bq, L0_xattn_Wk, L0_xattn_bk, L0_xattn_Wv, L0_xattn_bv, L0_xattn_Wo, L0_xattn_bo, L0_ffn_Wr, L0_ffn_br, L0_ffn_W1, L0_ffn_b1, L0_ffn_W2, L0_ffn_b2):
    import jax
    import jax.numpy as jnp

    def _L0_attn_ref(x, w_in, w_out):
        import jax, jax.numpy as jnp
        import numpy as np
        NUM_HEADS = 16
        N_EMBD = 256

        def alibi_bias(num_heads: int, seq_len: int) -> jnp.ndarray:
            pos = jnp.arange(seq_len, dtype=jnp.float32)
            dgrid = pos[None, :] - pos[:, None]
            slopes = 2.0 ** (-8.0 / num_heads * (jnp.arange(num_heads, dtype=jnp.float32) + 1.0))
            bias = slopes[:, None, None] * dgrid[None, :, :]
            return jnp.where(dgrid[None, :, :] > 0, -jnp.inf, bias)
        B, L, E = x.shape
        H = NUM_HEADS
        D = E // H
        qkv = jnp.einsum('ble,fe->blf', x, w_in)
        q, k, v = jnp.split(qkv, 3, axis=-1)

        def to_heads(t):
            return t.reshape(B, L, H, D).transpose(0, 2, 1, 3)
        q, k, v = (to_heads(q), to_heads(k), to_heads(v))
        scale = 1.0 / jnp.sqrt(jnp.asarray(D, dtype=x.dtype))
        scores = jnp.einsum('bhqd,bhkd->bhqk', q, k) * scale
        scores = scores + alibi_bias(H, L)[None]
        attn = jax.nn.softmax(scores, axis=-1)
        ctx = jnp.einsum('bhqk,bhkd->bhqd', attn, v)
        ctx = ctx.transpose(0, 2, 1, 3).reshape(B, L, E)
        return jnp.einsum('ble,fe->blf', ctx, w_out)

    def _L0_xattn_ref(q, k, v, Wq, bq, Wk, bk, Wv, bv, Wo, bo):
        import jax, jax.numpy as jnp
        import numpy as np
        B, S, D, H = (4, 512, 256, 16)
        DK = D // H

        def _split_heads(x):
            b, s, _ = x.shape
            return x.reshape(b, s, H, DK).transpose(0, 2, 1, 3)
        Q = _split_heads(q @ Wq + bq)
        K = _split_heads(k @ Wk + bk)
        V = _split_heads(v @ Wv + bv)
        scores = jnp.einsum('bhqd,bhkd->bhqk', Q, K)
        weights = jax.nn.softmax(scores, axis=-1)
        x = jnp.einsum('bhqk,bhkd->bhqd', weights, V)
        x = x.transpose(0, 2, 1, 3).reshape(q.shape[0], -1, D)
        return x @ Wo + bo

    def _L0_ffn_ref(x_btd, Wr, br, W1, b1, W2, b2):
        import jax, jax.numpy as jnp
        import numpy as np
        import math
        E = 8
        K = 2
        CF = 1.2
        D = 256
        H = 1024
        B, T, Dm = x_btd.shape
        N = B * T
        x = x_btd.reshape(N, Dm)
        cap = int(math.ceil(CF * N / E))
        probs = jax.nn.softmax(x @ Wr + br, axis=-1)
        gates, ids = jax.lax.top_k(probs, K)
        flat_ids = ids.reshape(-1)
        flat_g = gates.reshape(-1)
        M = N * K
        order = jnp.lexsort((-flat_g, flat_ids))
        s_ids = flat_ids[order]
        s_tok = (order // K).astype(jnp.int32)
        s_g = flat_g[order]
        counts = jnp.bincount(flat_ids, length=E)
        starts = jnp.concatenate([jnp.zeros((1,), counts.dtype), jnp.cumsum(counts)[:-1]])
        rank = jnp.arange(M) - starts[s_ids]
        valid = rank < cap
        pos = jnp.where(valid, s_ids * cap + rank, E * cap)
        disp_tok = jnp.zeros((E * cap + 1,), jnp.int32).at[pos].set(s_tok)[:E * cap]
        disp_g = jnp.zeros((E * cap + 1,), x.dtype).at[pos].set(s_g)[:E * cap]
        xg = x[disp_tok].reshape(E, cap, Dm)
        h = jax.nn.silu(jnp.einsum('ecd,edh->ech', xg, W1) + b1[:, None, :])
        out = jnp.einsum('ech,ehd->ecd', h, W2) + b2[:, None, :]
        gated = out * disp_g.reshape(E, cap, 1)
        y = jnp.zeros((N, Dm), x.dtype).at[disp_tok].add(gated.reshape(E * cap, Dm))
        return y.reshape(B, T, Dm)
    x = _layernorm(x + _L0_attn_ref(x, L0_attn_w_in, L0_attn_w_out), axis=-1)
    x = _layernorm(x + _L0_xattn_ref(x, ctx_1024, ctx_1024, L0_xattn_Wq, L0_xattn_bq, L0_xattn_Wk, L0_xattn_bk, L0_xattn_Wv, L0_xattn_bv, L0_xattn_Wo, L0_xattn_bo), axis=-1)
    x = _layernorm(x + _L0_ffn_ref(x, L0_ffn_Wr, L0_ffn_br, L0_ffn_W1, L0_ffn_b1, L0_ffn_W2, L0_ffn_b2), axis=-1)
    return x

_drawn_inputs = setup_inputs


def setup_inputs(seed=0):
    import zlib

    import numpy as np

    out = dict(_drawn_inputs(seed))
    spreads = {'L0_xattn_bq': (0.0, 0.1),
     'L0_xattn_bk': (0.0, 0.8),
     'L0_xattn_bv': (0.0, 0.1),
     'L0_xattn_bo': (0.0, 0.1),
     'L0_ffn_br': (0.0, 0.1),
     'L0_ffn_b1': (0.0, 0.317),
     'L0_ffn_b2': (0.0, 0.1)}
    factors = {}
    for name, (base, spread) in spreads.items():
        noise = np.random.default_rng([zlib.crc32(name.encode()), seed]).standard_normal(out[name].shape)
        drawn = base * np.exp(spread * noise) if base else spread * noise
        out[name] = jnp.asarray(drawn.astype(out[name].dtype))
    for name, factor in factors.items():
        out[name] = (out[name] * factor).astype(out[name].dtype)
    return out
```

```python
import concourse.bass as bass
from concourse import mybir
from contextlib import ExitStack

FP32 = mybir.dt.float32
BF16 = mybir.dt.bfloat16
ALU = mybir.AluOpType
ACT = mybir.ActivationFunctionType
AX = mybir.AxisListType.X

P = 128
D = 256
H = 16
DK = D // H
NB = 4
G = NB * P
HALVES = D // P
HEADS_HALF = H // HALVES
QUADS = H // 4
VW = 32
RING = 4
EPS = 1e-5


def wait(eng, sem, value):
    if not isinstance(value, int) or value > 0:
        eng.wait_ge(sem, value)


def wait_apart(engine, scratch, *waits):
    for sem, value in waits:
        engine.wait_ge(sem, value)
    tile, turn = scratch
    turn[0] = turn[0] % (tile.shape[1] - 1) + 1
    engine.tensor_tensor(tile[:, turn[0]:turn[0] + 1], tile[:, 0:1], tile[:, 0:1], ALU.add)


def attention_block(nc, causal, groups, x_in, ctx_in, x_out, w, consts):
    kv_own = ctx_in is not None
    n_tr = HALVES * (2 if kv_own else 1)
    n_proj = n_tr + 2 * HALVES
    n_b = n_proj + QUADS + HALVES
    n_c = 1 + QUADS + 4

    tag = "self_" if causal else "cross_"
    with ExitStack() as c:
        def sb(name, shape, dt=FP32):
            return c.enter_context(nc.sbuf_tensor(tag + name, shape, dt))

        def sem(name):
            return c.enter_context(nc.semaphore(tag + name))

        x = sb("x", [P, 2, NB, D])
        ctx = sb("ctx", [P, 2, NB, D]) if kv_own else x
        xT = sb("xT", [P, HALVES, G])
        cT = sb("cT", [P, HALVES, G]) if kv_own else xT
        q = sb("q", [P, HALVES, G])
        qm = sb("qm", [P, 2, H, G])
        k = sb("k", [P, 2, HALVES, G])
        v = sb("v", [P, 2, NB, H, VW])
        pr = sb("pr", [P, 2, 4, G])
        oq = sb("oq", [P, 2, G])
        on = sb("on", [P, NB, D])
        oT = sb("oT", [P, HALVES, G])
        y = sb("y", [P, 2, NB, D])
        wq = sb("wq", [P, HALVES, D])
        wk = sb("wk", [P, HALVES, D])
        wv = sb("wv", [P, HALVES, D])
        wo = sb("wo", [P, HALVES, D])
        sel = sb("sel", [P, H, P], BF16)
        mT = sb("mT", [P, G], BF16)
        ident = sb("ident", [P, P])
        ident_b = sb("ident_b", [P, P], BF16)
        head_mask = sb("head_mask", [P, HEADS_HALF])
        mx = sb("mx", [P, NB, H])
        m2 = sb("m2", [P, NB, 2 * H], BF16)
        rden = sb("rden", [P, NB, 4])
        stats = sb("stats", [P, NB, 6])
        mv = sb("mv", [P, NB, 2])
        rstd = sb("rstd", [P, NB])
        minus_half = sb("minus_half", [P, NB])
        scratch_v = (sb("scratch_v", [P, 9]), [0])
        scratch_p = (sb("scratch_p", [P, 65]), [0])
        if causal:
            bias_tab = sb("bias_tab", [P, H, P], BF16)
        if kv_own:
            bq = sb("bq", [P, HALVES])
            bk = sb("bk", [P, HALVES])
            bv = sb("bv", [P, D])
            bo = sb("bo", [P, D])
        A = [c.enter_context(nc.psum_tensor(f"{tag}A{i}", [P, G], FP32)) for i in range(RING)]
        B = [c.enter_context(nc.psum_tensor(f"{tag}B{i}", [P, G], FP32)) for i in range(2)]
        C = [c.enter_context(nc.psum_tensor(f"{tag}C{i}", [P, G], FP32)) for i in range(2)]

        const_in = sem("const_in")
        sel_in = sem("sel_in")
        table_in = sem("table_in")
        const_ready = sem("const_ready")
        x_loaded = [sem(f"x_loaded{i}") for i in range(2)]
        c_loaded = [sem(f"c_loaded{i}") for i in range(2)]
        y_stored = [sem(f"y_stored{i}") for i in range(2)]
        a_full = sem("a_full")
        b_full = sem("b_full")
        b_done = sem("b_done")
        c_full = sem("c_full")
        c_done = sem("c_done")
        max_done = sem("max_done")
        m2_ready = sem("m2_ready")
        exp_done = sem("exp_done")
        sel_done = sem("sel_done")
        qm_done = sem("qm_done")
        bo_added = sem("bo_added")
        stats_done = sem("stats_done")
        rstd_done = sem("rstd_done")
        y_ready = sem("y_ready")
        dve_chain = sem("dve_chain")
        pool_chain = sem("pool_chain")
        block = c.enter_context(nc.Block())

        def bx(g):
            if isinstance(g, int) and g == 0:
                return 0
            return n_proj + (g - 1) * n_b

        def b_oq(g, quad):
            last = isinstance(g, int) and g == groups - 1
            return n_proj + g * n_b + (0 if last else n_proj) + quad

        def b_ot(g, half):
            return b_oq(g, QUADS) + half

        def c_m(g):
            return 2 + g * n_c

        def c_on(g, quad):
            return c_m(g) + 1 + quad

        def c_v(g, i):
            if isinstance(g, int) and g == 0:
                return i
            return c_m(g - 1) + 1 + QUADS - 1 + i

        def c_on_last(g):
            last = isinstance(g, int) and g == groups - 1
            return c_m(g) + QUADS + (0 if last else 2)

        def c_out(g, i):
            return c_on_last(g) + 1 + i

        def c_quad(g, quad):
            return c_on(g, quad) if quad < QUADS - 1 else c_on_last(g)

        def bank(ring, g_par, index_of):
            return ring[index_of % 2]

        def steps(eng, first, body, last_first=False):
            body(0, 0)
            body(1, 1)
            with eng.Fori(1, groups // 2 - 1) as it:
                for par in range(2):
                    body(it * 2 + par, par)
            body(groups - 2, 0)
            body(groups - 1, 1)

        def par_of(fn, g, par, *a):
            gg = g if isinstance(g, int) else 2 + par
            return fn(gg, *a) % 2

        @block.sync
        def _(sp):
            n = 0
            loads = [(wq, w["wq"]), (wk, w["wk"]), (wv, w["wv"]), (wo, w["wo"])]
            for dst, src in loads:
                sp.dma_start(dst[:], src.rearrange("(t p) n -> p t n", p=P)).then_inc(const_in, 16)
                n += 16
            sp.dma_start(ident[:], consts["ident"]).then_inc(const_in, 16)
            sp.dma_start(head_mask[:], consts["head_mask"]).then_inc(const_in, 16)
            n += 32
            if kv_own:
                sp.dma_start(bq[:], w["bq"].rearrange("(t p) -> p t", p=P), allow_slow_non_contiguous=True).then_inc(const_in, 16)
                sp.dma_start(bk[:], w["bk"].rearrange("(t p) -> p t", p=P), allow_slow_non_contiguous=True).then_inc(const_in, 16)
                sp.dma_start(bv[:], w["bv"].rearrange("(a n) -> a n", a=1).to_broadcast([P, D])).then_inc(const_in, 16)
                sp.dma_start(bo[:], w["bo"].rearrange("(a n) -> a n", a=1).to_broadcast([P, D])).then_inc(const_in, 16)
                n += 64

            def load(g, par):
                rows = bass.ds(g * G, G)
                sp.dma_start(x[:, par], x_in[rows, :].rearrange("(b p) n -> p b n", p=P)).then_inc(x_loaded[par], 16)
                if kv_own:
                    sp.dma_start(ctx[:, par], ctx_in[rows, :].rearrange("(b p) n -> p b n", p=P)).then_inc(c_loaded[par], 16)

            load(0, 0)
            load(1, 1)
            sp.dma_start(qm[:, 1, 0:4, :], consts["sel_causal" if causal else "sel"]).then_inc(sel_in, 16)
            if causal:
                sp.dma_start(qm[:, 1, 4:8, :], consts["bias_tab"]).then_inc(table_in, 16)
                sp.dma_start(qm[:, 1, 8, :], consts["coarse_mask"]).then_inc(table_in, 16)

            def step(g, par):
                def store(gs, ps):
                    wait(sp, y_ready, gs + 1)
                    rows = bass.ds(gs * G, G)
                    sp.dma_start(x_out[rows, :].rearrange("(b p) n -> p b n", p=P), y[:, ps]).then_inc(y_stored[ps], 16)
                if not (isinstance(g, int) and g == 0):
                    store(g - 1, 1 - par)
                if not (isinstance(g, int) and g >= groups - 2):
                    wait(sp, c_done, c_out(g, 1) + 1)
                    load(g + 2, par)
                if isinstance(g, int) and g == groups - 1:
                    store(g, par)
            steps(sp, 0, step)
            for i in range(2):
                sp.wait_ge(y_stored[i], 16 * (groups // 2))

        CONST_N = 16 * (6 + (4 if kv_own else 0))

        @block.tensor
        def _(pe):
            pe.wait_ge(const_in, CONST_N)
            pe.wait_ge(const_ready, 1)

            def b_begin(idx):
                wait(pe, b_done, idx - 1)

            def c_begin(idx):
                wait(pe, c_done, idx - 1)

            def transposes(g, par, src, loaded, first):
                pe.wait_ge(loaded[par], (g - par) * 8 + 16)
                for half in range(HALVES):
                    idx = first + half
                    b_begin(idx)
                    b = B[(par_of(bx, g, par) + half) % 2]
                    for n in range(NB):
                        last = nc.tensor.matmul(b[:, n * P:(n + 1) * P], src[:, par, n, half * P:(half + 1) * P],
                                                ident[:], start=True, stop=True, is_transpose=True)
                    last.then_inc(b_full, 1)

            def project_qk(g, par):
                base = bx(g)
                transposes(g, par, x, x_loaded, base)
                if kv_own:
                    transposes(g, par, ctx, c_loaded, base + HALVES)
                for i, (src, wt) in enumerate(((xT, wq), (cT, wk))):
                    for half in range(HALVES):
                        idx = base + n_tr + i * HALVES + half
                        wait(pe, b_done, base + n_tr if (i, half) in ((0, 0),) else idx - 1)
                        b = B[(par_of(bx, g, par) + n_tr + i * HALVES + half) % 2]
                        for t in range(HALVES):
                            last = nc.tensor.matmul(b[:, :], wt[:, t, half * P:(half + 1) * P], src[:, t, :],
                                                    start=(t == 0), stop=(t == HALVES - 1))
                        last.then_inc(b_full, 1)

            def project_v(g, par):
                for i in range(2):
                    idx = c_v(g, i)
                    c_begin(idx)
                    b = C[(par_of(c_v, g, par, 0) + i) % 2]
                    for j in range(2):
                        n = 2 * i + j
                        for t in range(HALVES):
                            last = nc.tensor.matmul(b[:, j * D:(j + 1) * D], cT[:, t, n * P:(n + 1) * P], wv[:, t, :],
                                                    start=(t == 0), stop=(t == HALVES - 1))
                    last.then_inc(c_full, 1)

            def score_max(g, par):
                for h in range(H):
                    half = h // HEADS_HALF
                    if h == 0:
                        wait(pe, qm_done, (g + 1) * H)
                        wait(pe, b_done, bx(g) + n_proj)
                    if h < RING:
                        wait(pe, exp_done, g * H - RING + h + 1)
                    else:
                        wait(pe, max_done, g * H + h - RING + 1)
                    b = A[h % RING]
                    for n in range(NB):
                        cols = slice(n * P * 2 + 1, (n + 1) * P * 2, 2)
                        last = nc.tensor.matmul(b[:, n * P:(n + 1) * P],
                                                qm[:, par, h, :].bitcast(BF16)[:, cols],
                                                k[:, par, half, :].bitcast(BF16)[:, cols],
                                                start=(n == 0), stop=(n == NB - 1 and not causal), skip_group_check=True)
                    if causal:
                        last = nc.tensor.matmul(b[:, :], ident_b[:], bias_tab[:, h, :].unsqueeze(1).to_broadcast([P, NB, P]),
                                                start=False, stop=True, skip_group_check=True)
                    last.then_inc(a_full, 1)

            def maxima(g, par):
                c_begin(c_m(g))
                pe.wait_ge(m2_ready, g + 1)
                b = C[par_of(c_m, g, par)]
                for n in range(NB):
                    last = nc.tensor.matmul(b[0:2 * H, :].bitcast(BF16)[:, n * P:(n + 1) * P], m2[:, n, :], ident_b[:],
                                            start=True, stop=True, is_transpose=True)
                last.then_inc(c_full, 1)

            def scores(g, par, quad):
                for h in range(4 * quad, 4 * quad + 4):
                    half = h // HEADS_HALF
                    if h == 0:
                        wait(pe, c_done, c_m(g) + 1)
                    if h >= RING:
                        wait(pe, exp_done, g * H + h - RING + 1)
                    b = A[h % RING]
                    nc.tensor.matmul(b[:, :], sel[:, h, :], mT[:, :], start=True, stop=False)
                    for n in range(NB):
                        last = nc.tensor.matmul(b[:, n * P:(n + 1) * P], k[:, par, half, n * P:(n + 1) * P],
                                                qm[:, par, h, n * P:(n + 1) * P], start=False, stop=(n == NB - 1))
                    last.then_inc(a_full, 1)

            def weigh(g, par, quad):
                b_begin(b_oq(g, quad))
                wait(pe, sel_done if causal else exp_done, g * H + 4 * quad + 4)
                if quad == 0:
                    wait(pe, c_done, c_v(g, 1) + 1)
                b = B[(par_of(b_oq, g, par, 0) + quad) % 2]
                for n in range(NB):
                    for j in range(4):
                        last = nc.tensor.matmul(b[32 * j:32 * j + VW, n * P:(n + 1) * P],
                                                v[:, par, n, 4 * quad + j, :],
                                                pr[:, quad % 2, j, n * P:(n + 1) * P], start=True, stop=True)
                last.then_inc(b_full, 1)

            def quad_back(g, par, quad):
                c_begin(c_quad(g, quad))
                wait(pe, b_done, b_oq(g, quad) + 1)
                b = C[par_of(c_quad, g, par, quad)]
                for n in range(NB):
                    last = nc.tensor.matmul(b[:, n * P:(n + 1) * P], oq[:, quad % 2, n * P:(n + 1) * P], ident[:],
                                            start=True, stop=True, is_transpose=True)
                last.then_inc(c_full, 1)

            def output(g, par):
                for half in range(HALVES):
                    b_begin(b_ot(g, half))
                    if half == 0:
                        wait(pe, c_done, c_quad(g, QUADS - 1) + 1)
                    b = B[(par_of(b_ot, g, par, 0) + half) % 2]
                    for n in range(NB):
                        last = nc.tensor.matmul(b[:, n * P:(n + 1) * P], on[:, n, half * P:(half + 1) * P], ident[:],
                                                start=True, stop=True, is_transpose=True)
                    last.then_inc(b_full, 1)
                wait(pe, b_done, b_ot(g, 1) + 1)
                for i in range(2):
                    c_begin(c_out(g, i))
                    b = C[par_of(c_out, g, par, i)]
                    for j in range(2):
                        n = 2 * i + j
                        for t in range(HALVES):
                            last = nc.tensor.matmul(b[:, j * D:(j + 1) * D], oT[:, t, n * P:(n + 1) * P], wo[:, t, :],
                                                    start=(t == 0), stop=(t == HALVES - 1))
                    last.then_inc(c_full, 1)

            project_qk(0, 0)
            project_v(0, 0)

            def step(g, par):
                more = not (isinstance(g, int) and g == groups - 1)
                score_max(g, par)
                if more:
                    project_qk(g + 1, 1 - par)
                maxima(g, par)
                scores(g, par, 0)
                for quad in range(1, QUADS):
                    scores(g, par, quad)
                    weigh(g, par, quad - 1)
                    if quad >= 2:
                        quad_back(g, par, quad - 2)
                weigh(g, par, QUADS - 1)
                quad_back(g, par, QUADS - 2)
                if more:
                    project_v(g + 1, 1 - par)
                quad_back(g, par, QUADS - 1)
                output(g, par)
            steps(pe, 0, step)

        @block.scalar
        def _(act):
            act.wait_ge(const_in, CONST_N)

            def copy_in(g, par):
                base = bx(g)
                pb = par_of(bx, g, par)
                n = 0
                for dst in ((xT, cT) if kv_own else (xT,)):
                    for half in range(HALVES):
                        act.wait_ge(b_full, base + n + 1)
                        if not (isinstance(g, int) and g == 0):
                            wait(act, c_full, c_v(g - 1, 1) + 1)
                        nc.scalar.copy(dst[:, half, :], B[(pb + n) % 2][:, :]).then_inc(b_done, 1)
                        n += 1
                for half in range(HALVES):
                    act.wait_ge(b_full, base + n + 1)
                    wait(act, qm_done, g * H)
                    nc.scalar.activation(q[:, half, :], B[(pb + n) % 2][:, :], ACT.Identity,
                                         bias=bq[:, half:half + 1] if kv_own else 0.0,
                                         scale=1.0 if kv_own else DK ** -0.5).then_inc(b_done, 1)
                    n += 1
                for half in range(HALVES):
                    act.wait_ge(b_full, base + n + 1)
                    wait(act, a_full, (g - 1) * 2 * H)
                    nc.scalar.activation(k[:, par, half, :], B[(pb + n) % 2][:, :], ACT.Identity,
                                         bias=bk[:, half:half + 1] if kv_own else 0.0).then_inc(b_done, 1)
                    n += 1

            def exps(g, par, quad):
                if quad >= 2:
                    wait(act, b_full, b_oq(g, quad - 2) + 1)
                elif not (isinstance(g, int) and g == 0):
                    wait(act, b_full, b_oq(g - 1, quad + 2) + 1)
                for j in range(4):
                    h = 4 * quad + j
                    act.wait_ge(a_full, g * 2 * H + H + h + 1)
                    nc.scalar.activation(pr[:, quad % 2, j, :], A[h % RING][:, :], ACT.Exp).then_inc(exp_done, 1)

            def copy_quad(g, par, quad):
                act.wait_ge(b_full, b_oq(g, quad) + 1)
                if quad >= 2:
                    wait(act, c_full, c_quad(g, quad - 2) + 1)
                elif not (isinstance(g, int) and g == 0):
                    wait(act, c_full, c_quad(g - 1, quad + 2) + 1)
                b = B[(par_of(b_oq, g, par, 0) + quad) % 2]
                nc.scalar.copy(oq[:, quad % 2, :], b[:, :]).then_inc(b_done, 1)

            def copy_out(g, par):
                for half in range(HALVES):
                    act.wait_ge(b_full, b_ot(g, half) + 1)
                    if not (isinstance(g, int) and g == 0):
                        wait(act, c_full, c_out(g - 1, 1) + 1)
                    b = B[(par_of(b_ot, g, par, 0) + half) % 2]
                    nc.scalar.copy(oT[:, half, :], b[:, :]).then_inc(b_done, 1)

            copy_in(0, 0)

            def step(g, par):
                if not (isinstance(g, int) and g == groups - 1):
                    copy_in(g + 1, 1 - par)
                exps(g, par, 0)
                for quad in range(1, QUADS):
                    exps(g, par, quad)
                    copy_quad(g, par, quad - 1)
                copy_quad(g, par, QUADS - 1)
                copy_out(g, par)
            steps(act, 0, step)

        @block.vector
        def _(dve):
            chain = {"n": 0, "base": 0}
            def link(ins):
                chain["n"] += 1
                ins.then_inc(dve_chain, 1)
                dve.wait_ge(dve_chain, chain["base"] + chain["n"])

            if not causal:
                nc.vector.memset(mT[:, :], 0.0)
            nc.vector.memset(v[:, 0], 0.0)
            link(nc.vector.memset(v[:, 1], 0.0))
            nc.vector.memset(v[:, 0, :, :, DK:DK + 1], 1.0)
            nc.vector.memset(v[:, 1, :, :, DK:DK + 1], 1.0)
            nc.vector.memset(minus_half[:, :], -0.5)
            nc.vector.memset(scratch_v[0][:, :], 0.0)
            nc.vector.memset(scratch_p[0][:, :], 0.0)
            dve.wait_ge(const_in, CONST_N)
            nc.vector.tensor_copy(ident_b[:], ident[:])
            dve.wait_ge(sel_in, 16)
            if causal:
                dve.wait_ge(table_in, 32)
                nc.vector.tensor_copy(mT[:, :], qm[:, 1, 8, :])
                nc.vector.tensor_copy(bias_tab[:].rearrange("p h k -> p (h k)"),
                                      qm[:, 1, 4:8, :].rearrange("p a b -> p (a b)"))
            nc.vector.tensor_copy(sel[:].rearrange("p h k -> p (h k)"),
                                  qm[:, 1, 0:4, :].rearrange("p a b -> p (a b)")).then_inc(const_ready, 1)
            START = chain["n"]

            def mask_q(g, par):
                for h in range(H):
                    half = h // HEADS_HALF
                    if h % HEADS_HALF == 0:
                        dve.wait_ge(b_done, bx(g) + n_tr + half + 1)
                        if h == 0 and not (isinstance(g, int) and g < 2):
                            dve.wait_ge(a_full, (g - 1) * 2 * H)
                    nc.vector.tensor_scalar(qm[:, par, h, :], q[:, half, :],
                                            head_mask[:, h % HEADS_HALF:h % HEADS_HALF + 1], None,
                                            ALU.mult).then_inc(qm_done, 1)

            def take_v(g, par):
                for i in range(2):
                    dve.wait_ge(c_full, c_v(g, i) + 1)
                    if not (isinstance(g, int) and g < 2):
                        wait(dve, b_full, b_oq(g - 2, QUADS - 1) + 1)
                    b = C[(par_of(c_v, g, par, 0) + i) % 2]
                    out = v[:, par, 2 * i:2 * i + 2, :, 0:DK]
                    src = b[:, :].rearrange("p (n h d) -> p n h d", n=2, h=H)
                    if kv_own:
                        ins = nc.vector.tensor_tensor(
                            out, src, bv[:, :].rearrange("p (h d) -> p h d", h=H).unsqueeze(1).to_broadcast([P, 2, H, DK]), ALU.add)
                    else:
                        ins = nc.vector.tensor_copy(out, src)
                    ins.then_inc(c_done, 1)

            def maxes(g, par):
                for h in range(H):
                    dve.wait_ge(a_full, g * 2 * H + h + 1)
                    nc.vector.tensor_reduce(mx[:, :, h], A[h % RING][:, :].rearrange("p (n k) -> p n k", n=NB), AX,
                                            ALU.max).then_inc(max_done, 1)
                dve.wait_ge(max_done, (g + 1) * H)
                wait(dve, c_full, c_m(g - 1) + 1) if not (isinstance(g, int) and g == 0) else None
                link(nc.vector.tensor_copy(m2[:, :, 0:H], mx[:, :, :]))
                nc.vector.tensor_tensor(m2[:, :, H:2 * H], mx[:, :, :], m2[:, :, 0:H], ALU.subtract).then_inc(m2_ready, 1)

            def take_max(g, par):
                dve.wait_ge(c_full, c_m(g) + 1)
                b = C[par_of(c_m, g, par)]
                nc.vector.tensor_copy(mT[0:2 * H, :], b[0:2 * H, :].bitcast(BF16)[:, 0:G]).then_inc(c_done, 1)

            def normalise_quad(g, par, quad):
                dve.wait_ge(c_full, c_quad(g, quad) + 1)
                b = C[par_of(c_quad, g, par, quad)][:, :].rearrange("p (n j d) -> p n j d", n=NB, j=4)
                wait(dve, c_done, c_quad(g, quad))
                link(nc.vector.reciprocal(rden[:, :, :], b[:, :, :, DK]))
                if quad == 0 and not (isinstance(g, int) and g == 0):
                    dve.wait_ge(b_full, b_ot(g - 1, 1) + 1)
                out = on[:, :, quad * 4 * DK:(quad + 1) * 4 * DK].rearrange("p n (j d) -> p n j d", j=4)
                nc.vector.tensor_tensor(out, b[:, :, :, 0:DK], rden[:, :, :].unsqueeze(3).to_broadcast([P, NB, 4, DK]),
                                        ALU.mult).then_inc(c_done, 1)

            def residual(g, par):
                for i in range(2):
                    dve.wait_ge(c_full, c_out(g, i) + 1)
                    if i == 0:
                        if kv_own:
                            dve.wait_ge(bo_added, g + 1)
                        if not (isinstance(g, int) and g < 2):
                            dve.wait_ge(y_stored[par], (g - par) * 8)
                    b = C[par_of(c_out, g, par, i)]
                    nc.vector.tensor_tensor(y[:, par, 2 * i:2 * i + 2, :].rearrange("p n d -> p (n d)"), b[:, :],
                                            x[:, par, 2 * i:2 * i + 2, :].rearrange("p n d -> p (n d)"),
                                            ALU.add).then_inc(c_done, 1)

            def layernorm_stats(g, par):
                dve.wait_ge(c_done, c_out(g, 1) + 1)
                for n in range(NB):
                    ins = nc.vector.bn_stats(stats[:, n, :], y[:, par, n, :])
                ins.then_inc(dve_chain, 1)
                chain["n"] += 1
                waits = [(dve_chain, chain["base"] + chain["n"])]
                if not (isinstance(g, int) and g == 0):
                    waits.append((rstd_done, g))
                wait_apart(nc.vector, scratch_v, *waits)
                for n in range(NB):
                    ins = nc.vector.bn_aggr(mv[:, n, :], stats[:, n, :])
                ins.then_inc(stats_done, 1)

            def layernorm_apply(g, par):
                dve.wait_ge(stats_done, g + 1)
                dve.wait_ge(rstd_done, g + 1)
                for n in range(NB):
                    ins = nc.vector.tensor_scalar(y[:, par, n, :], y[:, par, n, :], mv[:, n, 0:1], rstd[:, n:n + 1],
                                                  ALU.subtract, ALU.mult)
                ins.then_inc(y_ready, 1)

            mask_q(0, 0)
            take_v(0, 0)

            def step(g, par):
                first = isinstance(g, int) and g == 0
                last = isinstance(g, int) and g == groups - 1
                links = 1 + QUADS + 1
                chain["base"], chain["n"] = START + g * links - (0 if first else 1), 0
                maxes(g, par)
                if not first:
                    layernorm_stats(g - 1, 1 - par)
                take_max(g, par)
                if not first:
                    layernorm_apply(g - 1, 1 - par)
                if not last:
                    mask_q(g + 1, 1 - par)
                for quad in range(QUADS - 1):
                    normalise_quad(g, par, quad)
                if not last:
                    take_v(g + 1, 1 - par)
                normalise_quad(g, par, QUADS - 1)
                residual(g, par)
                if last:
                    layernorm_stats(g, par)
                    layernorm_apply(g, par)
            steps(dve, 0, step)

        @block.gpsimd
        def _(pool):
            pool.wait_ge(const_in, CONST_N)
            pool.wait_ge(const_ready, 1)

            def clear_future(g, par):
                for h in range(H):
                    wait_apart(nc.gpsimd, scratch_p, (exp_done, g * H + h + 1))
                    t = pr[:, (h // 4) % 2, h % 4, :].rearrange("p (n k) -> p n k", n=NB)
                    nc.gpsimd.affine_select(out=t, in_=t, compare_op=ALU.is_ge, fill=0.0, base=0,
                                            pattern=[[0, NB], [1, P]], channel_multiplier=-1).then_inc(sel_done, 1)

            def add_bo(g, par):
                pool.wait_ge(b_full, bx(g) + HALVES)
                nc.gpsimd.tensor_tensor(x[:, par], x[:, par], bo[:, :].unsqueeze(1).to_broadcast([P, NB, D]),
                                        ALU.add).then_inc(bo_added, 1)

            def inverse_deviation(g, chained):
                waits = [(stats_done, g + 1)]
                if not (isinstance(g, int) and g == 0):
                    waits.append((y_ready, g))
                wait_apart(nc.gpsimd, scratch_p, *waits)
                nc.gpsimd.tensor_scalar(rstd[:, :], mv[:, :, 1], EPS, None, ALU.add).then_inc(pool_chain, 1)
                pool.wait_ge(pool_chain, g + 1)
                nc.gpsimd.tensor_tensor(rstd[:, :], rstd[:, :], minus_half[:, :], ALU.pow).then_inc(rstd_done, 1)

            def step(g, par):
                last = isinstance(g, int) and g == groups - 1
                if kv_own:
                    add_bo(g, par)
                if not (isinstance(g, int) and g == 0):
                    inverse_deviation(g - 1, 0)
                if causal:
                    clear_future(g, par)
                if last:
                    inverse_deviation(g, 0)
            steps(pool, 0, step)

I32 = mybir.dt.int32
E = 8
HID = 1024
HT = HID // P
BITS = 30


def logits_block(nc, tiles, x2_dram, x2, wr_dram, br_dram, ident_dram, logits):
    groups = tiles // NB
    with ExitStack() as c:
        ident = c.enter_context(nc.sbuf_tensor("lg_ident", [P, P], FP32))
        wr = c.enter_context(nc.sbuf_tensor("lg_wr", [P, HALVES, E], FP32))
        br = c.enter_context(nc.sbuf_tensor("lg_br", [P, E], FP32))
        xT = c.enter_context(nc.sbuf_tensor("lg_xT", [P, 2, HALVES, G], FP32))
        tb = [c.enter_context(nc.psum_tensor(f"lg_T{i}", [P, G], FP32)) for i in range(4)]
        lb = [c.enter_context(nc.psum_tensor(f"lg_L{i}", [P, NB, E], FP32)) for i in range(2)]
        const_in = c.enter_context(nc.semaphore("lg_const_in"))
        x_loaded = [c.enter_context(nc.semaphore(f"lg_x_loaded{i}")) for i in range(4)]
        t_full = c.enter_context(nc.semaphore("lg_t_full"))
        a_copied = c.enter_context(nc.semaphore("lg_a_copied"))
        d_copied = c.enter_context(nc.semaphore("lg_d_copied"))
        l_full = c.enter_context(nc.semaphore("lg_l_full"))
        l_done = c.enter_context(nc.semaphore("lg_l_done"))
        block = c.enter_context(nc.Block())

        @block.sync
        def _(sp):
            sp.dma_start(ident[:], ident_dram).then_inc(const_in, 16)
            sp.dma_start(wr[:], wr_dram.rearrange("(t p) n -> p t n", p=P)).then_inc(const_in, 16)
            sp.dma_start(br[:], br_dram.rearrange("(a n) -> a n", a=1).to_broadcast([P, E])).then_inc(const_in, 16)
            for g in range(groups):
                if g >= 4:
                    sp.wait_ge(x_loaded[g % 4], 16 * (g // 4))
                sp.dma_start(x2[:, g * NB:(g + 1) * NB, :],
                             x2_dram[g * G:(g + 1) * G, :].rearrange("(b p) n -> p b n", p=P)).then_inc(x_loaded[g % 4], 16)

        @block.tensor
        def _(pe):
            pe.wait_ge(const_in, 48)

            def logits_of(g):
                pe.wait_ge(a_copied, g + 1)
                pe.wait_ge(d_copied, g + 1)
                if g >= 2:
                    pe.wait_ge(l_done, g - 1)
                for n in range(NB):
                    for t in range(HALVES):
                        last = nc.tensor.matmul(lb[g % 2][:, n, :], xT[:, g % 2, t, n * P:(n + 1) * P], wr[:, t, :],
                                                start=(t == 0), stop=(t == HALVES - 1))
                last.then_inc(l_full, 1)

            for g in range(groups):
                pe.wait_ge(x_loaded[g % 4], 16 * (g // 4 + 1))
                if g >= 2:
                    pe.wait_ge(a_copied, g - 1)
                    pe.wait_ge(d_copied, g - 1)
                for half in range(HALVES):
                    for n in range(NB):
                        last = nc.tensor.matmul(tb[2 * (g % 2) + half][:, n * P:(n + 1) * P],
                                                x2[:, g * NB + n, half * P:(half + 1) * P], ident[:],
                                                start=True, stop=True, is_transpose=True)
                last.then_inc(t_full, 1)
                if g >= 1:
                    logits_of(g - 1)
            logits_of(groups - 1)

        @block.scalar
        def _(act):
            for g in range(groups):
                act.wait_ge(t_full, g + 1)
                if g >= 2:
                    act.wait_ge(l_full, g - 1)
                nc.scalar.copy(xT[:, g % 2, 0, :], tb[2 * (g % 2)][:, :]).then_inc(a_copied, 1)

        @block.vector
        def _(dve):
            def take(g):
                dve.wait_ge(l_full, g + 1)
                nc.vector.tensor_tensor(logits[:, g * NB:(g + 1) * NB, :], lb[g % 2][:, :, :],
                                        br[:, :].unsqueeze(1).to_broadcast([P, NB, E]), ALU.add).then_inc(l_done, 1)
            dve.wait_ge(const_in, 48)
            for g in range(groups):
                dve.wait_ge(t_full, g + 1)
                if g >= 2:
                    dve.wait_ge(l_full, g - 1)
                nc.vector.tensor_copy(xT[:, g % 2, 1, :], tb[2 * (g % 2) + 1][:, :]).then_inc(d_copied, 1)
                if g >= 1:
                    take(g - 1)
            take(groups - 1)


def route_block(nc, tiles, cap, logits, x2, xg_dram, gates, slots, consts):
    dump = E * cap
    CH = P // E
    F = tiles * P // CH
    TJ = F // P
    with ExitStack() as c:
        def sb(name, shape, dt=FP32):
            return c.enter_context(nc.sbuf_tensor("rt_" + name, shape, dt))

        def sem(name):
            return c.enter_context(nc.semaphore("rt_" + name))

        pr = sb("probs", [P, tiles, E])
        eq = sb("eq", [P, tiles, E])
        cand = sb("cand", [P, tiles, E])
        first = sb("first", [P, tiles, E])
        second = sb("second", [P, tiles, E])
        gm = sb("gm", [P, tiles, E])
        runs = sb("runs", [P, TJ, E, CH])
        st = sb("slot_t", [P, tiles, E])
        col = sb("col", [P, tiles])
        col2 = sb("col2", [P, tiles])
        ident = sb("ident", [P, P])
        same = sb("same", [P, P])
        before = sb("before", [P, P])
        ebase = sb("ebase", [P, 1])
        iota8 = sb("iota8", [P, E])
        gt = sb("gt", [P, F])
        above = sb("above", [P, F])
        equal = sb("equal", [P, F])
        ones = sb("ones", [P, F])
        sc_a = sb("sc_a", [P, F])
        sc_e = sb("sc_e", [P, F])
        junk = sb("junk", [P, F])
        thr = sb("thr", [P, 1], I32)
        tryv = sb("tryv", [P, 1], I32)
        bit = sb("bit", [P, 1], I32)
        ok = sb("ok", [P, 1], I32)
        cnt = sb("cnt", [P, 1])
        tot = sb("tot", [P, 2])
        off = sb("off", [P, 2])
        need = sb("need", [P, 1])
        bt = c.enter_context(nc.psum_tensor("rt_T", [P, G], FP32))
        bc = c.enter_context(nc.psum_tensor("rt_C", [P, 8], FP32))
        const_in, dve_done, pe_done, act_done, counted, total, scattered = (
            sem(n) for n in ("const_in", "dve_done", "pe_done", "act_done", "counted", "total", "scattered"))
        routed = sem("routed")
        block = c.enter_context(nc.Block())

        @block.sync
        def _(sp):
            for dst, name in ((ident, "ident"), (same, "same_expert"), (before, "before"), (ebase, "ebase"), (iota8, "iota8")):
                sp.dma_start(dst[:], consts[name]).then_inc(const_in, 16)

        @block.scalar
        def _(act):
            act.wait_ge(routed, 1)
            nc.scalar.activation(pr[:, :, :], pr[:, :, :], ACT.Exp).then_inc(act_done, 1)

        @block.tensor
        def _(pe):
            pe.wait_ge(const_in, 80)
            pe.wait_ge(routed, 2)
            for j in range(TJ):
                last = nc.tensor.matmul(bt[:, j * P:(j + 1) * P], runs[:, j, :, :].rearrange("p e c -> p (e c)"),
                                        ident[:], start=True, stop=True, is_transpose=True)
            last.then_inc(pe_done, 1)
            with pe.Fori(0, BITS) as i:
                pe.wait_ge(counted, i + 1)
                nc.tensor.matmul(bc[:, 0:1], same[:], cnt[:], start=True, stop=True).then_inc(total, 1)
            pe.wait_ge(routed, 3)
            nc.tensor.matmul(bc[:, 2:4], before[:], tot[:], start=True, stop=True)
            nc.tensor.matmul(bc[:, 4:6], same[:], tot[:], start=True, stop=True).then_inc(pe_done, 1)
            pe.wait_ge(routed, 4)
            for j in range(TJ):
                last = nc.tensor.matmul(bt[:, j * P:(j + 1) * P], gt[:, j * P:(j + 1) * P], ident[:],
                                        start=True, stop=True, is_transpose=True)
            last.then_inc(pe_done, 1)

        @block.vector
        def _(dve):
            n = [0]

            def link(ins):
                n[0] += 1
                ins.then_inc(dve_done, 1)
                dve.wait_ge(dve_done, n[0])

            def wide(a):
                return a.unsqueeze(2).to_broadcast([P, tiles, E])

            v = nc.vector
            v.memset(ones[:], 1.0)
            v.memset(thr[:], 0)
            link(v.memset(bit[:], 1 << (BITS - 1)))
            link(v.tensor_reduce(col[:], logits[:], AX, ALU.max))
            v.tensor_tensor(pr[:], logits[:], wide(col[:]), ALU.subtract).then_inc(routed, 1)
            dve.wait_ge(act_done, 1)
            link(v.tensor_reduce(col2[:], pr[:], AX, ALU.add))
            link(v.reciprocal(col[:], col2[:]))
            link(v.tensor_tensor(pr[:], pr[:], wide(col[:]), ALU.mult))
            dve.wait_ge(const_in, 80)
            link(v.tensor_reduce(gates[:, 0, :], pr[:], AX, ALU.max))
            lower = iota8[:].unsqueeze(1).to_broadcast([P, tiles, E])
            for kth, chosen in enumerate((first, second)):
                src = pr if kth == 0 else gm
                link(v.tensor_tensor(eq[:], src[:], wide(gates[:, kth, :]), ALU.is_equal))
                link(v.tensor_tensor(cand[:], eq[:], lower, ALU.mult))
                link(v.tensor_reduce(col[:], cand[:], AX, ALU.min))
                link(v.tensor_tensor(chosen[:], cand[:], wide(col[:]), ALU.is_equal))
                if kth == 0:
                    link(v.scalar_tensor_tensor(gm[:], chosen[:], -2.0, pr[:], ALU.mult, ALU.add))
                    link(v.tensor_reduce(gates[:, 1, :], gm[:], AX, ALU.max))
            link(v.tensor_tensor(eq[:], first[:], second[:], ALU.add))
            link(v.tensor_tensor(cand[:], pr[:], eq[:], ALU.mult))
            by_run = "p (c j) e -> p j e c"
            for j in range(TJ):
                ins = v.scalar_tensor_tensor(runs[:, j], eq[:].rearrange(by_run, j=TJ)[:, j], -1.0,
                                             cand[:].rearrange(by_run, j=TJ)[:, j], ALU.add, ALU.add)
            ins.then_inc(routed, 1)
            dve.wait_ge(pe_done, 1)
            link(v.tensor_copy(gt[:], bt[:]))
            base = n[0]
            with dve.Fori(0, BITS) as i:
                v.tensor_tensor(tryv[:], thr[:], bit[:], ALU.bitwise_or).then_inc(dve_done, 1)
                dve.wait_ge(dve_done, i * 4 + (base + 1))
                v.tensor_scalar(junk[:], gt[:], tryv[:].bitcast(FP32), 0.0, ALU.is_ge, ALU.add,
                                accum_out=cnt[:]).then_inc(counted, 1)
                dve.wait_ge(total, i + 1)
                v.tensor_scalar(ok[:], bc[:, 0:1], float(cap), bit[:, 0:1], ALU.is_ge, ALU.mult).then_inc(dve_done, 1)
                dve.wait_ge(dve_done, i * 4 + (base + 2))
                v.tensor_tensor(thr[:], thr[:], ok[:], ALU.bitwise_or).then_inc(dve_done, 1)
                v.tensor_scalar(bit[:], bit[:], 1, None, ALU.logical_shift_right).then_inc(dve_done, 1)
                dve.wait_ge(dve_done, i * 4 + (base + 4))
            n[0] = base + 4 * BITS
            dve.wait_ge(counted, BITS)
            t = thr[:].bitcast(FP32)
            link(v.tensor_scalar(above[:], gt[:], t, None, ALU.is_gt))
            link(v.tensor_scalar(equal[:], gt[:], t, None, ALU.is_equal))
            link(v.tensor_tensor_scan(sc_a[:], ones[:], above[:], 0.0, ALU.mult, ALU.add))
            link(v.tensor_tensor_scan(sc_e[:], ones[:], equal[:], 0.0, ALU.mult, ALU.add))
            v.tensor_copy(tot[:, 0:1], sc_a[:, F - 1:F])
            link(v.tensor_copy(tot[:, 1:2], sc_e[:, F - 1:F]))
            v.engine_nop().then_inc(routed, 1) if False else v.memset(junk[:, 0:1], 0.0).then_inc(routed, 1)
            dve.wait_ge(pe_done, 2)
            link(v.tensor_copy(off[:], bc[:, 2:4]))
            link(v.tensor_scalar(need[:], bc[:, 4:5], -1.0, float(cap), ALU.mult, ALU.add))
            link(v.scalar_tensor_tensor(sc_e[:], sc_e[:], off[:, 1:2], equal[:], ALU.add, ALU.subtract))
            link(v.scalar_tensor_tensor(sc_a[:], sc_a[:], off[:, 0:1], above[:], ALU.add, ALU.subtract))
            link(v.scalar_tensor_tensor(equal[:], sc_e[:], need[:, 0:1], equal[:], ALU.is_lt, ALU.mult))
            link(v.scalar_tensor_tensor(sc_a[:], sc_e[:], need[:, 0:1], sc_a[:], ALU.min, ALU.add))
            link(v.tensor_tensor(equal[:], equal[:], above[:], ALU.add))
            v.scalar_tensor_tensor(gt[:], sc_a[:], ebase[:, 0:1], equal[:], ALU.add, ALU.mult).then_inc(routed, 1)
            dve.wait_ge(pe_done, 3)
            for j in range(TJ):
                ins = v.tensor_copy(st[:].rearrange(by_run, j=TJ)[:, j], bt[:].rearrange("p (j e c) -> p j e c", j=TJ, e=E)[:, j])
            link(ins)
            for kth, chosen in enumerate((first, second)):
                link(v.tensor_tensor(cand[:], chosen[:], st[:], ALU.mult))
                link(v.tensor_reduce(col[:], cand[:], AX, ALU.add))
                link(v.tensor_scalar(slots[:, kth, :], col[:], float(dump), None, ALU.add))
            v.memset(junk[:, 0:1], 0.0).then_inc(routed, 1)

        @block.gpsimd
        def _(pool):
            pool.wait_ge(routed, 5)
            for t in range(tiles):
                for kth in range(2):
                    nc.gpsimd.indirect_dma_start(xg_dram, bass.IndirectOffsetOnAxis(ap=slots[:, kth, t:t + 1], axis=0),
                                                 x2[:, t, :], None, bounds_check=dump - 1,
                                                 oob_is_err=False).then_inc(scattered, 16)
            pool.wait_ge(scattered, 32 * tiles)


def experts_block(nc, cap, xg_dram, og_dram, w, ident_dram):
    CHUNK = 4 * P
    chunks = [(s, min(CHUNK, cap - s)) for s in range(0, cap, CHUNK)]
    NC = len(chunks)
    UP = 4
    tiles_of = [[(o, min(P, n - o)) for o in range(0, n, P)] for _, n in chunks]
    per_e = sum(len(t) for t in tiles_of)
    before = [sum(len(t) for t in tiles_of[:c]) for c in range(NC)]
    pairs = E // 2
    assert per_e % 2 == 0 or True
    with ExitStack() as c:
        def sb(name, shape, dt=FP32):
            return c.enter_context(nc.sbuf_tensor("ex_" + name, shape, dt))

        def sem(name):
            return c.enter_context(nc.semaphore("ex_" + name))

        w1 = sb("w1", [P, 2, HALVES, HID])
        w2 = sb("w2", [P, 2, HT, D])
        b1 = sb("b1", [P, 2, HT])
        b2 = sb("b2", [P, 2, D])
        xg = sb("xg", [P, 2, NB, D])
        xT = sb("xT", [P, 2, HALVES, G])
        hT = sb("hT", [P, 2, HT, G])
        o = sb("o", [P, 2, NB, D])
        ident = sb("ident", [P, P])
        T = [c.enter_context(nc.psum_tensor(f"ex_T{i}", [P, G], FP32)) for i in range(2)]
        U = [c.enter_context(nc.psum_tensor(f"ex_U{i}", [P, G], FP32)) for i in range(UP)]
        Dn = [c.enter_context(nc.psum_tensor(f"ex_D{i}", [P, D], FP32)) for i in range(2)]
        ident_in = sem("ident_in")
        w_loaded = [sem(f"w_loaded{i}") for i in range(2)]
        x_loaded = [sem(f"x_loaded{i}") for i in range(2)]
        o_stored = [sem(f"o_stored{i}") for i in range(2)]
        t_full, t_done, u_full, u_done, d_full, d_done, o_ready = (
            sem(n) for n in ("t_full", "t_done", "u_full", "u_done", "d_full", "d_done", "o_ready"))
        block = c.enter_context(nc.Block())

        def pairwise(eng, body):
            def pair(e0):
                for j in range(2):
                    for ch in range(NC):
                        body(e0 + j, j, ch)
            pair(0)
            with eng.Fori(1, pairs - 1) as it:
                pair(it * 2)
            pair(E - 2)

        def par(j, ch):
            return (NC * j + ch) % 2

        def o_before(e, ch):
            return e * per_e + before[ch]

        def dmas(e, j, ch, pr):
            def of(ch2):
                n = chunks[ch2][1]
                return 16 * ((n >= P) + (n % P > 0))
            per_pair = sum(of(ch2) for j2 in range(2) for ch2 in range(NC) if par(j2, ch2) == pr)
            inside = sum(of(ch2) for j2 in range(2) for ch2 in range(NC)
                         if par(j2, ch2) == pr and NC * j2 + ch2 < NC * j + ch)
            assert per_pair % 2 == 0
            return (e - j) * (per_pair // 2) + inside

        def after(e, j, ch, pr):
            n = chunks[ch][1]
            return dmas(e, j, ch, pr) + 16 * ((n >= P) + (n % P > 0))

        @block.sync
        def _(sp):
            sp.dma_start(ident[:], ident_dram).then_inc(ident_in, 16)

            def load_w(e, j):
                ix = bass.ds(e, 1)
                sp.dma_start(w1[:, j], w["w1"][ix].rearrange("a (t p) n -> p (a t) n", p=P)).then_inc(w_loaded[j], 16)
                sp.dma_start(w2[:, j], w["w2"][ix].rearrange("a (t p) n -> p (a t) n", p=P)).then_inc(w_loaded[j], 16)
                sp.dma_start(b1[:, j], w["b1"][ix].rearrange("a (t p) -> p (a t)", p=P), allow_slow_non_contiguous=True).then_inc(w_loaded[j], 16)
                sp.dma_start(b2[:, j], w["b2"][ix].to_broadcast([P, D])).then_inc(w_loaded[j], 16)

            def load_x(e, j, ch):
                s, n = chunks[ch]
                pr = par(j, ch)
                full = n // P
                if full:
                    sp.dma_start(xg[:, pr, 0:full, :], xg_dram[bass.ds(e * cap + s, full * P), :]
                                 .rearrange("(b p) n -> p b n", p=P)).then_inc(x_loaded[pr], 16)
                if n % P:
                    sp.dma_start(xg[0:n % P, pr, full, :], xg_dram[bass.ds(e * cap + s + full * P, n % P), :]).then_inc(x_loaded[pr], 16)

            load_w(0, 0)
            load_x(0, 0, 0)
            load_x(0, 0, 1)
            load_w(1, 1)

            def body(e, j, ch):
                s = e * NC + ch
                if not (isinstance(e, int) and s + 2 >= E * NC):
                    wait(sp, t_full, (s + 1) * 2)
                    load_x(e + (ch + 2) // NC, (j + (ch + 2) // NC) % 2, (ch + 2) % NC)
                if not (isinstance(e, int) and s == 0):
                    pj, pc = ((j, ch - 1) if ch else (1 - j, NC - 1))
                    store(e if ch else e - 1, pj, pc)
                if ch == 0 and not (isinstance(e, int) and (e < 1 or e + 1 >= E)):
                    load_w(e + 1, 1 - j)

            def store(e, j, ch):
                s, n = chunks[ch]
                pr = par(j, ch)
                sp.wait_ge(d_done, o_before(e, ch) + len(tiles_of[ch]))
                full = n // P
                if full:
                    sp.dma_start(og_dram[bass.ds(e * cap + s, full * P), :].rearrange("(b p) n -> p b n", p=P),
                                 o[:, pr, 0:full, :]).then_inc(o_stored[pr], 16)
                if n % P:
                    sp.dma_start(og_dram[bass.ds(e * cap + s + full * P, n % P), :], o[0:n % P, pr, full, :]).then_inc(o_stored[pr], 16)
            pairwise(sp, body)
            store(E - 1, 1, NC - 1)
            for pr in range(2):
                sp.wait_ge(o_stored[pr], dmas(E, 0, 0, pr))

        @block.tensor
        def _(pe):
            pe.wait_ge(ident_in, 16)

            def transpose_x(e, j, ch):
                s = e * NC + ch
                pr = par(j, ch)
                pe.wait_ge(x_loaded[pr], after(e, j, ch, pr))
                for half in range(HALVES):
                    wait(pe, t_done, s * 2 + half - 1)
                    for b, (off, n) in enumerate(tiles_of[ch]):
                        last = nc.tensor.matmul(T[half][:, off:off + n], xg[0:n, pr, b, half * P:(half + 1) * P],
                                                ident[0:n, 0:n], start=True, stop=True, is_transpose=True)
                    last.then_inc(t_full, 1)

            def up(e, j, ch):
                s = e * NC + ch
                n = chunks[ch][1]
                if ch == 0:
                    pe.wait_ge(w_loaded[j], ((e - j) // 2 + 1) * 64 if isinstance(e, int) else (e - j) * 32 + 64)
                pe.wait_ge(t_done, (s + 1) * 2)
                for m in range(HT):
                    wait(pe, u_done, s * HT + m - UP + 1)
                    for t in range(HALVES):
                        last = nc.tensor.matmul(U[m % UP][:, 0:n], w1[:, j, t, m * P:(m + 1) * P],
                                                xT[:, par(j, ch), t, 0:n], start=(t == 0), stop=(t == HALVES - 1))
                    last.then_inc(u_full, 1)

            def down(e, j, ch):
                s = e * NC + ch
                pe.wait_ge(u_done, (s + 1) * HT)
                for b, (off, n) in enumerate(tiles_of[ch]):
                    idx = o_before(e, ch) + b
                    wait(pe, d_done, idx - 1)
                    for t in range(HT):
                        last = nc.tensor.matmul(Dn[(j * per_e + before[ch] + b) % 2][0:n, :], hT[:, par(j, ch), t, off:off + n],
                                                w2[:, j, t, :], start=(t == 0), stop=(t == HT - 1))
                    last.then_inc(d_full, 1)

            transpose_x(0, 0, 0)

            def body(e, j, ch):
                last = isinstance(e, int) and e == E - 1 and ch == NC - 1
                if not last:
                    nx = ch + 1
                    transpose_x(e + nx // NC, (j + nx // NC) % 2, nx % NC)
                up(e, j, ch)
                if not (isinstance(e, int) and e == 0 and ch == 0):
                    down(*((e, j, ch - 1) if ch else (e - 1, 1 - j, NC - 1)))
            pairwise(pe, body)
            down(E - 1, 1, NC - 1)

        @block.scalar
        def _(act):
            def body(e, j, ch):
                s = e * NC + ch
                n = chunks[ch][1]
                if ch == 0:
                    act.wait_ge(w_loaded[j], ((e - j) // 2 + 1) * 64 if isinstance(e, int) else (e - j) * 32 + 64)
                for m in range(HT):
                    act.wait_ge(u_full, s * HT + m + 1)
                    if m == 0 and not (isinstance(e, int) and s < 2):
                        act.wait_ge(d_full, o_before(e, ch - 1) if ch else o_before(e, 0) - len(tiles_of[NC - 1]))
                    nc.scalar.activation(hT[:, par(j, ch), m, 0:n], U[m % UP][:, 0:n], ACT.Silu,
                                         bias=b1[:, j, m:m + 1]).then_inc(u_done, 1)
            pairwise(act, body)

        @block.vector
        def _(dve):
            def take_x(e, j, ch):
                s = e * NC + ch
                n = chunks[ch][1]
                for half in range(HALVES):
                    dve.wait_ge(t_full, s * 2 + half + 1)
                    if half == 0 and not (isinstance(e, int) and s < 2):
                        dve.wait_ge(u_full, (s - 1) * HT)
                    nc.vector.tensor_copy(xT[:, par(j, ch), half, 0:n], T[half][:, 0:n]).then_inc(t_done, 1)

            def take_o(e, j, ch):
                pr = par(j, ch)
                s = e * NC + ch
                if not (isinstance(e, int) and s < 2):
                    dve.wait_ge(o_stored[pr], dmas(e, j, ch, pr))
                if ch == 0:
                    dve.wait_ge(w_loaded[j], ((e - j) // 2 + 1) * 64 if isinstance(e, int) else (e - j) * 32 + 64)
                for b, (off, n) in enumerate(tiles_of[ch]):
                    idx = o_before(e, ch) + b
                    dve.wait_ge(d_full, idx + 1)
                    nc.vector.tensor_tensor(o[0:n, pr, b, :], Dn[(j * per_e + before[ch] + b) % 2][0:n, :],
                                            b2[0:n, j, :], ALU.add).then_inc(d_done, 1)

            take_x(0, 0, 0)

            def body(e, j, ch):
                last = isinstance(e, int) and e == E - 1 and ch == NC - 1
                if not last:
                    nx = ch + 1
                    take_x(e + nx // NC, (j + nx // NC) % 2, nx % NC)
                if not (isinstance(e, int) and e == 0 and ch == 0):
                    take_o(*((e, j, ch - 1) if ch else (e - 1, 1 - j, NC - 1)))
            pairwise(dve, body)
            take_o(E - 1, 1, NC - 1)


def combine_block(nc, tiles, cap, x2, gates, slots, og_dram, out_dram):
    dump = E * cap
    groups = tiles // NB
    R = 3
    with ExitStack() as c:
        def sb(name, shape, dt=FP32):
            return c.enter_context(nc.sbuf_tensor("cb_" + name, shape, dt))

        def sem(name):
            return c.enter_context(nc.semaphore("cb_" + name))

        r = sb("rows", [P, R, 2, NB, D])
        zero = sb("zero", [1, D])
        stats = sb("stats", [P, 2, NB, 6])
        mv = sb("mv", [P, 2, NB, 2])
        rstd = sb("rstd", [P, 2, NB])
        shift = sb("shift", [P, 2, NB])
        minus_half = sb("minus_half", [P, NB])
        zeroed, ready = sem("zeroed"), sem("ready")
        gathered = [sem(f"gathered{i}") for i in range(R)]
        summed, stats_done, rstd_done, y_ready, dve_chain, pool_chain = (
            sem(n) for n in ("summed", "stats_done", "rstd_done", "y_ready", "dve_chain", "pool_chain"))
        stored = sem("stored")
        block = c.enter_context(nc.Block())

        @block.sync
        def _(sp):
            sp.wait_ge(ready, 1)
            sp.dma_start(og_dram[dump:dump + 1, :], zero[:]).then_inc(zeroed, 16)
            for g in range(groups):
                sp.wait_ge(y_ready, g + 1)
                sp.dma_start(out_dram[g * G:(g + 1) * G, :].rearrange("(b p) n -> p b n", p=P),
                             x2[:, g * NB:(g + 1) * NB, :]).then_inc(stored, 16)
            sp.wait_ge(stored, 16 * groups)

        @block.gpsimd
        def _(pool):
            nc.gpsimd.memset(minus_half[:], -0.5)
            nc.gpsimd.memset(zero[:], 0.0).then_inc(ready, 1)
            pool.wait_ge(zeroed, 16)

            def gather(g):
                if g >= R:
                    pool.wait_ge(summed, g - R + 1)
                for n in range(NB):
                    for kth in range(2):
                        t = g * NB + n
                        nc.gpsimd.indirect_dma_start(r[:, g % R, kth, n, :], None, og_dram,
                                                     bass.IndirectOffsetOnAxis(ap=slots[:, kth, t:t + 1], axis=0),
                                                     bounds_check=dump).then_inc(gathered[g % R], 16)

            def inverse_deviation(g):
                pool.wait_ge(stats_done, g + 1)
                if g >= 2:
                    pool.wait_ge(y_ready, g - 1)
                nc.gpsimd.tensor_scalar(shift[:, g % 2], mv[:, g % 2, :, 0], -1.0, None, ALU.mult)
                nc.gpsimd.tensor_scalar(rstd[:, g % 2], mv[:, g % 2, :, 1], EPS, None, ALU.add).then_inc(pool_chain, 1)
                pool.wait_ge(pool_chain, 2 * g + 1)
                pool.wait_ge(ready, 1)
                nc.gpsimd.tensor_tensor(rstd[:, g % 2], rstd[:, g % 2], minus_half[:], ALU.pow).then_inc(pool_chain, 1)
                pool.wait_ge(pool_chain, 2 * g + 2)
                nc.gpsimd.tensor_tensor(shift[:, g % 2], shift[:, g % 2], rstd[:, g % 2], ALU.mult).then_inc(rstd_done, 1)
            for g in range(groups):
                gather(g)
                if g >= 2:
                    inverse_deviation(g - 2)
            inverse_deviation(groups - 2)
            inverse_deviation(groups - 1)

        @block.vector
        def _(dve):
            n_links = [0]

            def link(ins):
                n_links[0] += 1
                ins.then_inc(dve_chain, 1)
                dve.wait_ge(dve_chain, n_links[0])
            for g in range(groups):
                dve.wait_ge(gathered[g % R], 16 * 2 * NB * (g // R + 1))
                for kth in range(2):
                    for n in range(NB):
                        t = g * NB + n
                        ins = nc.vector.scalar_tensor_tensor(x2[:, t, :], r[:, g % R, kth, n, :], gates[:, kth, t:t + 1],
                                                             x2[:, t, :], ALU.mult, ALU.add)
                    if kth == 0:
                        link(ins)
                    else:
                        ins.then_inc(summed, 1)
                dve.wait_ge(summed, g + 1)
                for n in range(NB):
                    ins = nc.vector.bn_stats(stats[:, g % 2, n, :], x2[:, g * NB + n, :])
                link(ins)
                if g >= 2:
                    dve.wait_ge(y_ready, g - 1)
                for n in range(NB):
                    ins = nc.vector.bn_aggr(mv[:, g % 2, n, :], stats[:, g % 2, n, :])
                ins.then_inc(stats_done, 1)

        @block.scalar
        def _(act):
            for g in range(groups):
                act.wait_ge(rstd_done, g + 1)
                act.wait_ge(summed, g + 1)
                for n in range(NB):
                    t = g * NB + n
                    ins = nc.scalar.activation(x2[:, t, :], x2[:, t, :], ACT.Identity,
                                               bias=shift[:, g % 2, n:n + 1], scale=rstd[:, g % 2, n:n + 1])
                ins.then_inc(y_ready, 1)


def fill_block(nc, dram, rows):
    with ExitStack() as c:
        n = 8
        z = c.enter_context(nc.sbuf_tensor("fill_z", [P, n * D], FP32))
        made = c.enter_context(nc.semaphore("fill_made"))
        filled = c.enter_context(nc.semaphore("fill_filled"))
        block = c.enter_context(nc.Block())

        @block.vector
        def _(dve):
            nc.vector.memset(z[:], 0.0).then_inc(made, 1)

        @block.sync
        def _(sp):
            sp.wait_ge(made, 1)
            count = 0
            for at in range(0, rows - n * P + 1, n * P):
                sp.dma_start(dram[at:at + n * P, :].rearrange("(p b) n -> p (b n)", p=P), z[:]).then_inc(filled, 16)
                count += 1
            rest = rows % (n * P)
            at = rows - rest
            while rest:
                k = min(P, rest)
                sp.dma_start(dram[at:at + k, :], z[0:k, 0:D]).then_inc(filled, 16)
                at, rest, count = at + k, rest - k, count + 1
            sp.wait_ge(filled, 16 * count)


def decoder_layer(nc, ins, out):
    tokens = ins["x"].shape[0]
    cap = -(-tokens * 12 // (10 * E))
    tiles = tokens // P
    groups = tokens // G
    x1 = nc.dram_tensor("x1", [tokens, D], FP32, kind="Internal").ap()
    x2d = nc.dram_tensor("x2", [tokens, D], FP32, kind="Internal").ap()
    xg = nc.dram_tensor("xg", [E * cap, D], FP32, kind="Internal").ap()
    og = nc.dram_tensor("og", [E * cap + 1, D], FP32, kind="Internal").ap()
    fill_block(nc, xg, E * cap)
    attention_block(nc, True, groups, ins["x"], None, x1,
                    {k: ins["attn_" + k] for k in ("wq", "wk", "wv", "wo")}, ins)
    attention_block(nc, False, groups, x1, ins["ctx"], x2d,
                    {k: ins["xattn_" + k] for k in ("wq", "wk", "wv", "wo", "bq", "bk", "bv", "bo")}, ins)
    with ExitStack() as c:
        x2 = c.enter_context(nc.sbuf_tensor("x2_sb", [P, tiles, D], FP32))
        logits = c.enter_context(nc.sbuf_tensor("logits", [P, tiles, E], FP32))
        gates = c.enter_context(nc.sbuf_tensor("gates", [P, 2, tiles], FP32))
        slots = c.enter_context(nc.sbuf_tensor("slots", [P, 2, tiles], I32))
        logits_block(nc, tiles, x2d, x2, ins["wr"], ins["br"], ins["ident"], logits)
        route_block(nc, tiles, cap, logits, x2, xg, gates, slots, ins)
        experts_block(nc, cap, xg, og, {k: ins[k] for k in ("w1", "w2", "b1", "b2")}, ins["ident"])
        combine_block(nc, tiles, cap, x2, gates, slots, og, out)


def tables(tokens):
    import numpy as np
    cap = -(-tokens * 12 // (10 * E))
    pos = np.arange(P)
    slopes = (2.0 ** (-8.0 / H * (np.arange(H, dtype=np.float32) + 1.0))).astype(np.float32)
    head_mask = (pos[:, None] // DK == np.arange(HEADS_HALF)[None, :]).astype(np.float32)
    sel = np.zeros((P, H, P), np.float32)
    for h in range(H):
        sel[h, h, :] = sel[H + h, h, :] = -1.0
    sel_causal = sel.copy()
    for h in range(H):
        rest = slopes[h] * pos.astype(np.float32)
        for j in range(3):
            bits = rest.astype(np.float32).view(np.uint32)
            part = (bits & np.uint32(0xFFFF0000)).view(np.float32)
            sel_causal[2 * H + j, h, :] = part
            rest = rest - part
    coarse_mask = np.zeros((P, NB, P), np.float32)
    coarse_mask[2 * H:2 * H + 3] = 1.0
    for j in range(P // 2):
        sel_causal[P // 2 + j, :, 2 * j:2 * j + 2] = 1.0
        coarse_mask[P // 2 + j] = np.where(j > pos // 2, -1e30, 0.0)
    bias_tab = np.where(pos[None, None, :] > pos[:, None, None], -1e30,
                        slopes[None, :, None] * pos[None, None, :]).astype(np.float32)
    ch = P // E
    same = (pos[:, None] // ch == pos[None, :] // ch).astype(np.float32)
    before = same * (pos[:, None] < pos[None, :])
    ebase = (pos // ch * cap - E * cap).astype(np.float32).reshape(P, 1)
    iota8 = np.tile(np.arange(E, dtype=np.float32) - E, (P, 1))
    return {"ident": np.eye(P, dtype=np.float32), "head_mask": head_mask, "sel": sel.reshape(P, 4, G),
            "sel_causal": sel_causal.reshape(P, 4, G), "coarse_mask": coarse_mask.reshape(P, G),
            "bias_tab": bias_tab.astype(np.float32).reshape(P, 4, G), "same_expert": same,
            "before": before.astype(np.float32), "ebase": ebase, "iota8": iota8.astype(np.float32)}


def kernel(**inputs):
    import numpy as _np
    import concourse.bacc as _bacc
    from concourse import mybir as _mybir
    from concourse.bass_utils import run_bass_kernel_spmd as _run

    a = {n: _np.asarray(v) for n, v in inputs.items()}
    b, s, d = a["x"].shape
    w_in = a["L0_attn_w_in"]
    arrays = {
        "x": a["x"].reshape(b * s, d), "ctx": a["ctx_1024"].reshape(b * s, d),
        "attn_wq": w_in[0:d].T, "attn_wk": w_in[d:2 * d].T, "attn_wv": w_in[2 * d:3 * d].T,
        "attn_wo": a["L0_attn_w_out"].T,
        "xattn_wq": a["L0_xattn_Wq"], "xattn_wk": a["L0_xattn_Wk"], "xattn_wv": a["L0_xattn_Wv"],
        "xattn_wo": a["L0_xattn_Wo"], "xattn_bq": a["L0_xattn_bq"], "xattn_bk": a["L0_xattn_bk"],
        "xattn_bv": a["L0_xattn_bv"], "xattn_bo": a["L0_xattn_bo"],
        "wr": a["L0_ffn_Wr"], "br": a["L0_ffn_br"], "w1": a["L0_ffn_W1"], "b1": a["L0_ffn_b1"],
        "w2": a["L0_ffn_W2"], "b2": a["L0_ffn_b2"], **tables(b * s)}
    nc = _bacc.Bacc("TRN2", target_bir_lowering=False, num_devices=1)
    ins, feed = {}, {}
    for name, v in arrays.items():
        v = _np.ascontiguousarray(v)
        feed["in_" + name] = v
        ins[name] = nc.dram_tensor("in_" + name, v.shape, _mybir.dt.from_np(v.dtype), kind="ExternalInput").ap()
    out = nc.dram_tensor("out", (b * s, d), _mybir.dt.float32, kind="ExternalOutput").ap()
    decoder_layer(nc, ins, out)
    r = _run(nc, [feed], core_ids=[0])
    return _np.asarray(r.results[0]["out"]).reshape(b, s, d)
```

```python
import concourse.bass as bass
from concourse import mybir
from contextlib import ExitStack

FP32 = mybir.dt.float32
BF16 = mybir.dt.bfloat16
FP32R = mybir.dt.float32r
ALU = mybir.AluOpType
ACT = mybir.ActivationFunctionType
AX = mybir.AxisListType.X

P = 128
D = 256
H = 16
DK = D // H
NB = 4
G = NB * P
HALVES = D // P
HEADS_HALF = H // HALVES
QUADS = H // 4
VW = 32
RING = 4
EPS = 1e-5


def wait(eng, sem, value):
    if not isinstance(value, int) or value > 0:
        eng.wait_ge(sem, value)


def wait_apart(engine, scratch, *waits):
    for sem, value in waits:
        engine.wait_ge(sem, value)
    tile, turn = scratch
    turn[0] = turn[0] % (tile.shape[1] - 1) + 1
    engine.tensor_tensor(tile[:, turn[0]:turn[0] + 1], tile[:, 0:1], tile[:, 0:1], ALU.add)


def matmul3(nc, out, left, right, start, stop, pick_l, pick_r):
    for n, (a, b) in enumerate(((0, 0), (0, 1), (1, 0))):
        last = nc.tensor.matmul(out, pick_l(left, a), pick_r(right, b), start=(start and n == 0), stop=(stop and n == 2))
    return last


def attention_block(nc, causal, groups, x_in, ctx_in, x_out, w, consts):
    kv_own = ctx_in is not None
    n_tr = HALVES * (2 if kv_own else 1)
    n_proj = n_tr + 2 * HALVES
    n_b = n_proj + QUADS + HALVES
    n_c = 1 + QUADS + 4

    tag = "self_" if causal else "cross_"
    with ExitStack() as c:
        def sb(name, shape, dt=FP32):
            return c.enter_context(nc.sbuf_tensor(tag + name, shape, dt))

        def sem(name):
            return c.enter_context(nc.semaphore(tag + name))

        x = sb("x", [P, 2, NB, D])
        ctx = sb("ctx", [P, 2, NB, D]) if kv_own else x
        xr = sb("xr", [P, 2, NB, D])
        xT = sb("xT", [P, 2, HALVES, G], FP32R)
        cT = sb("cT", [P, 2, HALVES, G], FP32R) if kv_own else xT
        q = sb("q", [P, 2, HALVES, G])
        qm = sb("qm", [P, 2, H, G], FP32R)
        k = sb("k", [P, 2, 2, HALVES, G], FP32R)
        v = sb("v", [P, NB, H, VW])
        pr = sb("pr", [P, 2, NB, G])
        oq = sb("oq", [P, 2, G])
        on = sb("on", [P, NB, D])
        oT = sb("oT", [P, 2, HALVES, G], FP32R)
        y = sb("y", [P, 2, NB, D])
        wq = sb("wq", [P, 2, HALVES, D], FP32R)
        wk = sb("wk", [P, 2, HALVES, D], FP32R)
        wv = sb("wv", [P, 2, HALVES, D], FP32R)
        wo = sb("wo", [P, 2, HALVES, D], FP32R)
        sel = sb("sel", [P, H, P], BF16)
        mT = sb("mT", [P, G], BF16)
        ident = sb("ident", [P, P])
        ident_b = sb("ident_b", [P, P], BF16)
        head_mask = sb("head_mask", [P, HEADS_HALF])
        mx = sb("mx", [P, NB, H])
        m2 = sb("m2", [P, NB, 2 * H], BF16)
        rden = sb("rden", [P, NB, 4])
        stats = sb("stats", [P, NB, 6])
        mv = sb("mv", [P, NB, 2])
        rstd = sb("rstd", [P, NB])
        minus_half = sb("minus_half", [P, NB])
        scratch_v = (sb("scratch_v", [P, 9]), [0])
        scratch_p = (sb("scratch_p", [P, 65]), [0])
        if causal:
            bias_tab = sb("bias_tab", [P, H, P], BF16)
        if kv_own:
            bq = sb("bq", [P, HALVES])
            bk = sb("bk", [P, HALVES])
            bv = sb("bv", [P, D])
            bo = sb("bo", [P, D])
        A = [c.enter_context(nc.psum_tensor(f"{tag}A{i}", [P, G], FP32)) for i in range(RING)]
        B = [c.enter_context(nc.psum_tensor(f"{tag}B{i}", [P, G], FP32)) for i in range(2)]
        C = [c.enter_context(nc.psum_tensor(f"{tag}C{i}", [P, G], FP32)) for i in range(2)]

        const_in = sem("const_in")
        sel_in = sem("sel_in")
        table_in = sem("table_in")
        const_ready = sem("const_ready")
        x_loaded = [sem(f"x_loaded{i}") for i in range(2)]
        c_loaded = [sem(f"c_loaded{i}") for i in range(2)]
        y_stored = [sem(f"y_stored{i}") for i in range(2)]
        a_full = sem("a_full")
        b_full = sem("b_full")
        b_done = sem("b_done")
        lo_done = sem("lo_done")
        c_full = sem("c_full")
        c_done = sem("c_done")
        max_done = sem("max_done")
        m2_ready = sem("m2_ready")
        exp_done = sem("exp_done")
        sel_done = sem("sel_done")
        qm_done = sem("qm_done")
        xr_ready = sem("xr_ready")
        lo_masked = sem("lo_masked")
        stats_done = sem("stats_done")
        rstd_done = sem("rstd_done")
        y_ready = sem("y_ready")
        dve_chain = sem("dve_chain")
        pool_chain = sem("pool_chain")
        block = c.enter_context(nc.Block())
        y_stage = y[:].rearrange("p a n d -> p (a n d)").rearrange("p (w t d) -> p w t d", w=4, t=HALVES)
        on_stage = on[:].rearrange("p n d -> p (n d)")[:, 0:G]

        def is_last(g):
            return isinstance(g, int) and g == groups - 1

        def is_first(g):
            return isinstance(g, int) and g == 0

        def in_step(g, first, per_step, without_output):
            return first if is_first(g) else first + without_output + (g - 1) * per_step

        def b_step(g):
            return in_step(g, n_proj, n_b, n_proj + QUADS)

        def b_p(g, i):
            if is_first(g):
                return i
            late = HALVES if i >= HALVES and not (isinstance(g, int) and g == 1) else 0
            return b_step(g - 1) + i + late

        def b_oq(g, quad):
            return b_step(g) + (0 if is_last(g) else n_proj) + (0 if is_first(g) else HALVES) + quad

        def b_ot(g, half):
            if is_last(g):
                return b_oq(g, QUADS) + half
            return b_step(g + 1) + (0 if is_last(g + 1) else HALVES) + half

        n_lo = n_proj + HALVES

        def lo_step(g):
            return in_step(g, n_proj, n_lo, n_proj)

        def lo_p(g, i):
            if is_first(g):
                return i
            late = HALVES if i >= HALVES and not (isinstance(g, int) and g == 1) else 0
            return lo_step(g - 1) + i + late

        def lo_o(g, half):
            if is_last(g):
                return lo_step(g) + HALVES + half
            return lo_step(g + 1) + (0 if is_last(g + 1) else HALVES) + half

        def c_step(g):
            return in_step(g, 2, n_c, n_c - 2)

        def c_out(g, i):
            if is_last(g):
                return c_m(g) + 1 + QUADS + i
            return c_step(g + 1) + i

        def c_m(g):
            return c_step(g) + (0 if is_first(g) else 2)

        def c_v(g, i):
            return i if is_first(g) else c_m(g - 1) + QUADS + i

        def c_quad(g, quad):
            return c_m(g) + 1 + quad + (2 if quad == QUADS - 1 and not is_last(g) else 0)

        def steps(eng, first, body, last_first=False):
            body(0, 0)
            body(1, 1)
            with eng.Fori(1, groups // 2 - 1) as it:
                for par in range(2):
                    body(it * 2 + par, par)
            body(groups - 2, 0)
            body(groups - 1, 1)

        def par_of(fn, g, par, *a):
            gg = g if isinstance(g, int) else 4 + par
            return fn(gg, *a) % 2

        @block.sync
        def _(sp):
            n = 0
            for i, name in enumerate(("wq", "wk", "wv", "wo")):
                sp.dma_start(y_stage[:, i], w[name].rearrange("(t p) n -> p t n", p=P)).then_inc(const_in, 16)
                n += 16
            sp.dma_start(ident[:], consts["ident"]).then_inc(const_in, 16)
            sp.dma_start(head_mask[:], consts["head_mask"]).then_inc(const_in, 16)
            n += 32
            if kv_own:
                sp.dma_start(bq[:], w["bq"].rearrange("(t p) -> p t", p=P), allow_slow_non_contiguous=True).then_inc(const_in, 16)
                sp.dma_start(bk[:], w["bk"].rearrange("(t p) -> p t", p=P), allow_slow_non_contiguous=True).then_inc(const_in, 16)
                sp.dma_start(bv[:], w["bv"].rearrange("(a n) -> a n", a=1).to_broadcast([P, D])).then_inc(const_in, 16)
                sp.dma_start(bo[:], w["bo"].rearrange("(a n) -> a n", a=1).to_broadcast([P, D])).then_inc(const_in, 16)
                n += 64

            def load(g, par):
                rows = bass.ds(g * G, G)
                sp.dma_start(x[:, par], x_in[rows, :].rearrange("(b p) n -> p b n", p=P)).then_inc(x_loaded[par], 16)
                if kv_own:
                    sp.dma_start(ctx[:, par], ctx_in[rows, :].rearrange("(b p) n -> p b n", p=P)).then_inc(c_loaded[par], 16)

            load(0, 0)
            load(1, 1)
            sp.dma_start(pr[:, 0], consts["sel_causal" if causal else "sel"]).then_inc(sel_in, 16)
            if causal:
                sp.dma_start(pr[:, 1], consts["bias_tab"]).then_inc(table_in, 16)
                sp.dma_start(on_stage, consts["coarse_mask"]).then_inc(table_in, 16)

            def step(g, par):
                def store(gs, ps):
                    wait(sp, y_ready, gs + 1)
                    rows = bass.ds(gs * G, G)
                    sp.dma_start(x_out[rows, :].rearrange("(b p) n -> p b n", p=P), y[:, ps]).then_inc(y_stored[ps], 16)
                if not (isinstance(g, int) and g >= groups - 2):
                    wait(sp, c_full, c_v(g, 1) + 1)
                    load(g + 2, par)
                if not (isinstance(g, int) and g == 0):
                    store(g - 1, 1 - par)
                if isinstance(g, int) and g == groups - 1:
                    store(g, par)
            steps(sp, 0, step)
            for i in range(2):
                sp.wait_ge(y_stored[i], 16 * (groups // 2))

        CONST_N = 16 * (6 + (4 if kv_own else 0))

        @block.tensor
        def _(pe):
            pe.wait_ge(const_in, CONST_N)
            pe.wait_ge(const_ready, 1)

            def c_begin(idx):
                wait(pe, c_done, idx - 1)

            def after_projection(g, i):
                pe.wait_ge(lo_done, lo_p(g, i) + 1)

            def transposes(g, par, src, loaded, first):
                pe.wait_ge(loaded[par], (g - par) * 8 + 16)
                for half in range(HALVES):
                    i = first + half
                    if i < HALVES and isinstance(g, int) and g == 1:
                        after_projection(0, n_proj - 2 + half)
                    elif i < HALVES and not is_first(g):
                        wait(pe, b_done, b_oq(g - 2, 2 + half) + 1)
                    elif i >= HALVES and (isinstance(g, int) and g < 2):
                        after_projection(g, half)
                    elif i >= HALVES:
                        pe.wait_ge(lo_done, lo_o(g - 2, half) + 1)
                    b = B[par_of(b_p, g, par, i)]
                    for n in range(NB):
                        last = nc.tensor.matmul(b[:, n * P:(n + 1) * P], src[:, par, n, half * P:(half + 1) * P],
                                                ident[:], start=True, stop=True, is_transpose=True)
                    last.then_inc(b_full, 1)

            def project_qk(g, par):
                for i, (src, wt) in enumerate(((xT, wq), (cT, wk))):
                    for half in range(HALVES):
                        place = n_tr + i * HALVES + half
                        needed = (HALVES - 1) if i == 0 else n_tr - 1
                        after_projection(g, max(needed, place - 2))
                        if i == 0 and not kv_own and not (isinstance(g, int) and g < 2):
                            pe.wait_ge(lo_done, lo_o(g - 2, half) + 1)
                        b = B[par_of(b_p, g, par, place)]
                        for t in range(HALVES):
                            last = matmul3(nc, b[:, :], wt, src, t == 0, t == HALVES - 1,
                                           lambda w_, a, t=t, half=half: w_[:, a, t, half * P:(half + 1) * P],
                                           lambda x_, a, t=t: x_[:, a, t, :])
                        last.then_inc(b_full, 1)

            def project_v(g, par):
                pe.wait_ge(xr_ready, g + 1)
                for i in range(2):
                    idx = c_v(g, i)
                    c_begin(idx)
                    b = C[(par_of(c_v, g, par, 0) + i) % 2]
                    for j in range(2):
                        n = 2 * i + j
                        for t in range(HALVES):
                            last = matmul3(nc, b[:, j * D:(j + 1) * D], cT, wv, t == 0, t == HALVES - 1,
                                           lambda x_, a, t=t, n=n: x_[:, a, t, n * P:(n + 1) * P],
                                           lambda w_, a, t=t: w_[:, a, t, :])
                    last.then_inc(c_full, 1)

            def score_max(g, par, heads):
                for h in heads:
                    half = h // HEADS_HALF
                    if h == 0:
                        wait(pe, qm_done, (g + 1) * H)
                        after_projection(g, n_proj - 1)
                    if h < RING:
                        wait(pe, exp_done, g * H - RING + h + 1)
                    else:
                        wait(pe, max_done, g * H + h - RING + 1)
                    b = A[h % RING]
                    for n in range(NB):
                        cols = slice(n * P * 2 + 1, (n + 1) * P * 2, 2)
                        last = nc.tensor.matmul(b[:, n * P:(n + 1) * P],
                                                qm[:, 0, h, :].bitcast(BF16)[:, cols],
                                                k[:, par, 0, half, :].bitcast(BF16)[:, cols],
                                                start=(n == 0), stop=(n == NB - 1 and not causal), skip_group_check=True)
                    if causal:
                        last = nc.tensor.matmul(b[:, :], ident_b[:], bias_tab[:, h, :].unsqueeze(1).to_broadcast([P, NB, P]),
                                                start=False, stop=True, skip_group_check=True)
                    last.then_inc(a_full, 1)

            def maxima(g, par):
                c_begin(c_m(g))
                pe.wait_ge(m2_ready, g + 1)
                b = C[par_of(c_m, g, par)]
                for n in range(NB):
                    last = nc.tensor.matmul(b[0:2 * H, :].bitcast(BF16)[:, n * P:(n + 1) * P], m2[:, n, :], ident_b[:],
                                            start=True, stop=True, is_transpose=True)
                last.then_inc(c_full, 1)

            def scores(g, par, quad):
                half = quad * 4 // HEADS_HALF
                heads = slice(4 * quad, 4 * quad + 4)
                for n in range(NB):
                    turn = 4 * quad + n
                    if turn == 0:
                        wait(pe, c_done, c_m(g) + 1)
                    if n == 0:
                        wait(pe, lo_masked, g * H + 4 * quad + 4)
                    if turn >= RING:
                        wait(pe, exp_done, g * H + turn - RING + 1)
                    b = A[turn % RING]
                    cols = slice(n * P, (n + 1) * P)
                    for j in range(4):
                        nc.tensor.matmul(b[:, j * P:(j + 1) * P], sel[:, 4 * quad + j, :], mT[:, cols],
                                         start=(j == 0), stop=False)
                    last = matmul3(nc, b[:, :].rearrange("p (j q) -> p j q", j=4), k, qm, False, True,
                                   lambda k_, a: k_[:, par, a, half, cols], lambda q_, a: q_[:, a, heads, cols])
                    last.then_inc(a_full, 1)

            def weigh(g, par, quad):
                if quad >= 2:
                    wait(pe, b_done, b_oq(g, quad - 2) + 1)
                elif is_last(g):
                    pe.wait_ge(lo_done, lo_o(g - 1, quad) + 1)
                else:
                    after_projection(g + 1, n_proj - 2 + quad)
                wait(pe, sel_done if causal else exp_done, g * H + 4 * quad + 4)
                if quad == 0:
                    wait(pe, c_done, c_v(g, 1) + 1)
                b = B[par_of(b_oq, g, par, quad)]
                for n in range(NB):
                    for j in range(4):
                        last = nc.tensor.matmul(b[32 * j:32 * j + VW, n * P:(n + 1) * P],
                                                v[:, n, 4 * quad + j, :],
                                                pr[:, quad % 2, n, j * P:(j + 1) * P], start=True, stop=True)
                last.then_inc(b_full, 1)

            def quad_back(g, par, quad):
                c_begin(c_quad(g, quad))
                wait(pe, b_done, b_oq(g, quad) + 1)
                b = C[par_of(c_quad, g, par, quad)]
                for n in range(NB):
                    last = nc.tensor.matmul(b[:, n * P:(n + 1) * P], oq[:, quad % 2, n * P:(n + 1) * P], ident[:],
                                            start=True, stop=True, is_transpose=True)
                last.then_inc(c_full, 1)

            def output_back(g, par):
                for half in range(HALVES):
                    if isinstance(g, int) and g >= groups - 2:
                        wait(pe, b_done, b_oq(g, 2 + half) + 1)
                    else:
                        after_projection(g + 2, half)
                    if half == 0:
                        wait(pe, c_done, c_quad(g, QUADS - 1) + 1)
                    b = B[par_of(b_ot, g, par, half)]
                    for n in range(NB):
                        last = nc.tensor.matmul(b[:, n * P:(n + 1) * P], on[:, n, half * P:(half + 1) * P], ident[:],
                                                start=True, stop=True, is_transpose=True)
                    last.then_inc(b_full, 1)

            def output(g, par):
                pe.wait_ge(lo_done, lo_o(g, 1) + 1)
                for i in range(2):
                    c_begin(c_out(g, i))
                    b = C[par_of(c_out, g, par, i)]
                    for j in range(2):
                        n = 2 * i + j
                        for t in range(HALVES):
                            last = matmul3(nc, b[:, j * D:(j + 1) * D], oT, wo, t == 0, t == HALVES - 1,
                                           lambda o_, a, t=t, n=n: o_[:, a, t, n * P:(n + 1) * P],
                                           lambda w_, a, t=t: w_[:, a, t, :])
                    last.then_inc(c_full, 1)

            transposes(0, 0, x, x_loaded, 0)
            if kv_own:
                transposes(0, 0, ctx, c_loaded, HALVES)
            project_qk(0, 0)
            project_v(0, 0)

            def step(g, par):
                more = not is_last(g)
                if more:
                    transposes(g + 1, 1 - par, x, x_loaded, 0)
                score_max(g, par, range(H // 2))
                if not is_first(g):
                    output_back(g - 1, 1 - par)
                score_max(g, par, range(H // 2, H * 3 // 4))
                if not is_first(g):
                    output(g - 1, 1 - par)
                score_max(g, par, range(H * 3 // 4, H))
                if more:
                    if kv_own:
                        transposes(g + 1, 1 - par, ctx, c_loaded, HALVES)
                    project_qk(g + 1, 1 - par)
                maxima(g, par)
                scores(g, par, 0)
                for quad in range(1, QUADS):
                    scores(g, par, quad)
                    weigh(g, par, quad - 1)
                    if quad >= 2:
                        quad_back(g, par, quad - 2)
                weigh(g, par, QUADS - 1)
                quad_back(g, par, QUADS - 2)
                if more:
                    project_v(g + 1, 1 - par)
                quad_back(g, par, QUADS - 1)
                if not more:
                    output_back(g, par)
                    output(g, par)
            steps(pe, 0, step)

        @block.scalar
        def _(act):
            act.wait_ge(const_in, CONST_N)

            def copy_in(g, par, banks):
                for i in banks:
                    what = "x" if i < HALVES else "c" if i < n_tr else "q" if i < n_tr + HALVES else "k"
                    half = i % HALVES
                    b = B[par_of(b_p, g, par, i)][:, :]
                    act.wait_ge(b_full, b_p(g, i) + 1)
                    if what in "xc":
                        if not is_first(g):
                            wait(act, c_full, c_v(g - 1, 1) + 1)
                        ins = nc.scalar.copy((xT if what == "x" else cT)[:, 0, half, :], b)
                    elif what == "q":
                        wait(act, qm_done, g * H)
                        ins = nc.scalar.activation(q[:, 0, half, :].bitcast(FP32R), b, ACT.Identity,
                                                   bias=bq[:, half:half + 1] if kv_own else 0.0,
                                                   scale=1.0 if kv_own else DK ** -0.5)
                    else:
                        wait(act, a_full, (g - 1) * 2 * H)
                        ins = nc.scalar.activation(k[:, par, 0, half, :], b, ACT.Identity,
                                                   bias=bk[:, half:half + 1] if kv_own else 0.0)
                    ins.then_inc(b_done, 1)

            def mask_rest(g, par, quad):
                if quad == 0:
                    act.wait_ge(lo_done, lo_p(g, n_tr + HALVES - 1) + 1)
                if not is_first(g):
                    act.wait_ge(a_full, (g - 1) * 2 * H + H + 4 * quad + 4)
                for h in range(4 * quad, 4 * quad + 4):
                    nc.scalar.mul(qm[:, 1, h, :], q[:, 1, h // HEADS_HALF, :],
                                  head_mask[:, h % HEADS_HALF:h % HEADS_HALF + 1]).then_inc(lo_masked, 1)

            def exps(g, par, quad):
                if quad >= 2:
                    wait(act, b_full, b_oq(g, quad - 2) + 1)
                elif not (isinstance(g, int) and g == 0):
                    wait(act, b_full, b_oq(g - 1, quad + 2) + 1)
                for n in range(NB):
                    turn = 4 * quad + n
                    act.wait_ge(a_full, g * 2 * H + H + turn + 1)
                    nc.scalar.activation(pr[:, quad % 2, n, :], A[turn % RING][:, :], ACT.Exp).then_inc(exp_done, 1)

            def copy_quad(g, par, quad):
                act.wait_ge(b_full, b_oq(g, quad) + 1)
                if quad >= 2:
                    wait(act, c_full, c_quad(g, quad - 2) + 1)
                elif not (isinstance(g, int) and g == 0):
                    wait(act, c_full, c_quad(g - 1, quad + 2) + 1)
                b = B[par_of(b_oq, g, par, quad)]
                nc.scalar.copy(oq[:, quad % 2, :], b[:, :]).then_inc(b_done, 1)

            def copy_out(g, par):
                for half in range(HALVES):
                    act.wait_ge(b_full, b_ot(g, half) + 1)
                    if not (isinstance(g, int) and g == 0):
                        wait(act, c_full, c_out(g - 1, 1) + 1)
                    b = B[par_of(b_ot, g, par, half)]
                    nc.scalar.copy(oT[:, 0, half, :], b[:, :]).then_inc(b_done, 1)

            copy_in(0, 0, range(n_proj))
            for quad in range(QUADS):
                mask_rest(0, 0, quad)

            def step(g, par):
                more = not is_last(g)
                if more:
                    copy_in(g + 1, 1 - par, range(HALVES))
                if not is_first(g):
                    copy_out(g - 1, 1 - par)
                if more:
                    copy_in(g + 1, 1 - par, range(HALVES, n_proj))
                exps(g, par, 0)
                for quad in range(1, QUADS):
                    exps(g, par, quad)
                    if more:
                        mask_rest(g + 1, 1 - par, quad - 1)
                    copy_quad(g, par, quad - 1)
                if more:
                    mask_rest(g + 1, 1 - par, QUADS - 1)
                copy_quad(g, par, QUADS - 1)
                if not more:
                    copy_out(g, par)
            steps(act, 0, step)

        @block.vector
        def _(dve):
            chain = {"n": 0, "base": 0}
            def link(ins):
                chain["n"] += 1
                ins.then_inc(dve_chain, 1)
                dve.wait_ge(dve_chain, chain["base"] + chain["n"])

            if not causal:
                nc.vector.memset(mT[:, :], 0.0)
            link(nc.vector.memset(v[:, :, :, :], 0.0))
            nc.vector.memset(v[:, :, :, DK:DK + 1], 1.0)
            nc.vector.memset(minus_half[:, :], -0.5)
            nc.vector.memset(scratch_v[0][:, :], 0.0)
            nc.vector.memset(scratch_p[0][:, :], 0.0)
            dve.wait_ge(const_in, CONST_N)
            nc.vector.tensor_copy(ident_b[:], ident[:])
            dve.wait_ge(sel_in, 16)
            if causal:
                dve.wait_ge(table_in, 32)
                nc.vector.tensor_copy(mT[:, :], on_stage)
                nc.vector.tensor_copy(bias_tab[:].rearrange("p h k -> p (h k)"),
                                      pr[:, 1].rearrange("p a b -> p (a b)"))
            nc.vector.tensor_copy(sel[:].rearrange("p h k -> p (h k)"),
                                  pr[:, 0].rearrange("p a b -> p (a b)"))
            for i, wt in enumerate((wq, wk, wv, wo)):
                ins = nc.vector.tensor_copy(wt[:, 0], y_stage[:, i])
            link(ins)
            for i, wt in enumerate((wq, wk, wv, wo)):
                ins = nc.vector.tensor_tensor(wt[:, 1], y_stage[:, i], wt[:, 0].bitcast(FP32), ALU.subtract)
            ins.then_inc(const_ready, 1)
            START = chain["n"]

            def rest(g, par, i):
                idx = b_p(g, i)
                b = B[par_of(b_p, g, par, i)][:, :]
                half = i % HALVES
                what = "x" if i < HALVES else "c" if i < n_tr else "q" if i < n_tr + HALVES else "k"
                dve.wait_ge(b_done, idx + 1)
                if what in "xc":
                    t = xT if what == "x" else cT
                    ins = nc.vector.tensor_tensor(t[:, 1, half, :], b, t[:, 0, half, :].bitcast(FP32), ALU.subtract)
                elif what == "q":
                    if not is_first(g):
                        dve.wait_ge(lo_masked, g * H)
                    out, hi = q[:, 1, half, :], q[:, 0, half, :]
                    if kv_own:
                        ins = nc.vector.scalar_tensor_tensor(out, b, bq[:, half:half + 1], hi, ALU.add, ALU.subtract)
                    else:
                        ins = nc.vector.scalar_tensor_tensor(out, b, DK ** -0.5, hi, ALU.mult, ALU.subtract)
                else:
                    out, hi = k[:, par, 1, half, :], k[:, par, 0, half, :].bitcast(FP32)
                    if kv_own:
                        ins = nc.vector.scalar_tensor_tensor(out, b, bk[:, half:half + 1], hi, ALU.add, ALU.subtract)
                    else:
                        ins = nc.vector.tensor_tensor(out, b, hi, ALU.subtract)
                ins.then_inc(lo_done, 1)

            def rest_o(g, par, half):
                dve.wait_ge(b_done, b_ot(g, half) + 1)
                b = B[par_of(b_ot, g, par, half)]
                nc.vector.tensor_tensor(oT[:, 1, half, :], b[:, :], oT[:, 0, half, :].bitcast(FP32),
                                        ALU.subtract).then_inc(lo_done, 1)

            def mask_q(g, par, quad):
                if quad == 0:
                    dve.wait_ge(b_done, b_p(g, n_tr + HALVES - 1) + 1)
                if not (isinstance(g, int) and g == 0):
                    dve.wait_ge(a_full, (g - 1) * 2 * H + H + 4 * quad + 4)
                for h in range(4 * quad, 4 * quad + 4):
                    half = h // HEADS_HALF
                    mask = head_mask[:, h % HEADS_HALF:h % HEADS_HALF + 1]
                    nc.vector.tensor_scalar(qm[:, 0, h, :], q[:, 0, half, :], mask, None, ALU.mult).then_inc(qm_done, 1)

            def take_v(g, par):
                for i in range(2):
                    dve.wait_ge(c_full, c_v(g, i) + 1)
                    if not (isinstance(g, int) and g == 0):
                        wait(dve, b_full, b_oq(g - 1, QUADS - 1) + 1)
                    b = C[(par_of(c_v, g, par, 0) + i) % 2]
                    out = v[:, 2 * i:2 * i + 2, :, 0:DK]
                    src = b[:, :].rearrange("p (n h d) -> p n h d", n=2, h=H)
                    if kv_own:
                        ins = nc.vector.tensor_tensor(
                            out, src, bv[:, :].rearrange("p (h d) -> p h d", h=H).unsqueeze(1).to_broadcast([P, 2, H, DK]), ALU.add)
                    else:
                        ins = nc.vector.tensor_copy(out, src)
                    ins.then_inc(c_done, 1)

            def maxes(g, par, heads):
                for h in heads:
                    dve.wait_ge(a_full, g * 2 * H + h + 1)
                    nc.vector.tensor_reduce(mx[:, :, h], A[h % RING][:, :].rearrange("p (n k) -> p n k", n=NB), AX,
                                            ALU.max).then_inc(max_done, 1)

            def split_max(g, par):
                dve.wait_ge(max_done, (g + 1) * H)
                wait(dve, c_full, c_m(g - 1) + 1) if not (isinstance(g, int) and g == 0) else None
                link(nc.vector.tensor_copy(m2[:, :, 0:H], mx[:, :, :]))
                nc.vector.tensor_tensor(m2[:, :, H:2 * H], mx[:, :, :], m2[:, :, 0:H], ALU.subtract).then_inc(m2_ready, 1)

            def take_max(g, par):
                dve.wait_ge(c_full, c_m(g) + 1)
                b = C[par_of(c_m, g, par)]
                nc.vector.tensor_copy(mT[0:2 * H, :], b[0:2 * H, :].bitcast(BF16)[:, 0:G]).then_inc(c_done, 1)

            def normalise_quad(g, par, quad):
                dve.wait_ge(c_full, c_quad(g, quad) + 1)
                b = C[par_of(c_quad, g, par, quad)][:, :].rearrange("p (n j d) -> p n j d", n=NB, j=4)
                wait(dve, c_done, c_quad(g, quad))
                link(nc.vector.reciprocal(rden[:, :, :], b[:, :, :, DK]))
                if quad == 0 and not (isinstance(g, int) and g == 0):
                    dve.wait_ge(b_full, b_ot(g - 1, 1) + 1)
                out = on[:, :, quad * 4 * DK:(quad + 1) * 4 * DK].rearrange("p n (j d) -> p n j d", j=4)
                nc.vector.tensor_tensor(out, b[:, :, :, 0:DK], rden[:, :, :].unsqueeze(3).to_broadcast([P, NB, 4, DK]),
                                        ALU.mult).then_inc(c_done, 1)

            def residual(g, par):
                for i in range(2):
                    dve.wait_ge(c_full, c_out(g, i) + 1)
                    if i == 0:
                        dve.wait_ge(xr_ready, g + 1)
                        if not (isinstance(g, int) and g < 2):
                            dve.wait_ge(y_stored[par], (g - par) * 8)
                    b = C[par_of(c_out, g, par, i)]
                    nc.vector.tensor_tensor(y[:, par, 2 * i:2 * i + 2, :].rearrange("p n d -> p (n d)"), b[:, :],
                                            xr[:, par, 2 * i:2 * i + 2, :].rearrange("p n d -> p (n d)"),
                                            ALU.add).then_inc(c_done, 1)

            def layernorm_stats(g, par):
                dve.wait_ge(c_done, c_out(g, 1) + 1)
                for n in range(NB):
                    ins = nc.vector.bn_stats(stats[:, n, :], y[:, par, n, :])
                ins.then_inc(dve_chain, 1)
                chain["n"] += 1
                waits = [(dve_chain, chain["base"] + chain["n"])]
                if not (isinstance(g, int) and g == 0):
                    waits.append((rstd_done, g))
                wait_apart(nc.vector, scratch_v, *waits)
                for n in range(NB):
                    ins = nc.vector.bn_aggr(mv[:, n, :], stats[:, n, :])
                ins.then_inc(stats_done, 1)

            def layernorm_apply(g, par):
                dve.wait_ge(stats_done, g + 1)
                dve.wait_ge(rstd_done, g + 1)
                for n in range(NB):
                    ins = nc.vector.tensor_scalar(y[:, par, n, :], y[:, par, n, :], mv[:, n, 0:1], rstd[:, n:n + 1],
                                                  ALU.subtract, ALU.mult)
                ins.then_inc(y_ready, 1)

            for i in range(n_proj):
                rest(0, 0, i)
            for quad in range(QUADS):
                mask_q(0, 0, quad)
            take_v(0, 0)

            def step(g, par):
                first = isinstance(g, int) and g == 0
                last = isinstance(g, int) and g == groups - 1
                links = 1 + QUADS + 1
                chain["base"], chain["n"] = START + g * links - (0 if first else 1), 0
                if not last:
                    for i in range(HALVES):
                        rest(g + 1, 1 - par, i)
                maxes(g, par, range(H // 2))
                if not first:
                    for half in range(HALVES):
                        rest_o(g - 1, 1 - par, half)
                maxes(g, par, range(H // 2, H * 3 // 4))
                if not first:
                    residual(g - 1, 1 - par)
                maxes(g, par, range(H * 3 // 4, H))
                split_max(g, par)
                if not last:
                    for i in range(HALVES, n_tr + HALVES):
                        rest(g + 1, 1 - par, i)
                if not first:
                    layernorm_stats(g - 1, 1 - par)
                if not last:
                    for i in range(n_tr + HALVES, n_proj):
                        rest(g + 1, 1 - par, i)
                take_max(g, par)
                if not first:
                    layernorm_apply(g - 1, 1 - par)
                for quad in range(QUADS):
                    if not last:
                        mask_q(g + 1, 1 - par, quad)
                    if quad >= 1:
                        normalise_quad(g, par, quad - 1)
                if not last:
                    take_v(g + 1, 1 - par)
                normalise_quad(g, par, QUADS - 1)
                if last:
                    for half in range(HALVES):
                        rest_o(g, par, half)
                    residual(g, par)
                    layernorm_stats(g, par)
                    layernorm_apply(g, par)
            steps(dve, 0, step)

        @block.gpsimd
        def _(pool):
            pool.wait_ge(const_in, CONST_N)
            pool.wait_ge(const_ready, 1)

            def clear_future(g, par):
                for h in range(H):
                    wait_apart(nc.gpsimd, scratch_p, (exp_done, g * H + h + 1))
                    t = pr[:, (h // 4) % 2, h % 4, :].rearrange("p (n k) -> p n k", n=NB)
                    nc.gpsimd.affine_select(out=t, in_=t, compare_op=ALU.is_ge, fill=0.0, base=0,
                                            pattern=[[0, NB], [1, P]], channel_multiplier=-1).then_inc(sel_done, 1)

            def keep_residual(g, par):
                waits = [(x_loaded[par], (g - par) * 8 + 16)]
                if not (isinstance(g, int) and g < 2):
                    waits.append((c_done, c_out(g - 2, 1) + 1))
                wait_apart(nc.gpsimd, scratch_p, *waits)
                if kv_own:
                    ins = nc.gpsimd.tensor_tensor(xr[:, par], x[:, par], bo[:, :].unsqueeze(1).to_broadcast([P, NB, D]), ALU.add)
                else:
                    ins = nc.gpsimd.tensor_copy(xr[:, par], x[:, par])
                ins.then_inc(xr_ready, 1)

            def inverse_deviation(g, chained):
                waits = [(stats_done, g + 1)]
                if not (isinstance(g, int) and g == 0):
                    waits.append((y_ready, g))
                wait_apart(nc.gpsimd, scratch_p, *waits)
                nc.gpsimd.tensor_scalar(rstd[:, :], mv[:, :, 1], EPS, None, ALU.add).then_inc(pool_chain, 1)
                pool.wait_ge(pool_chain, g + 1)
                nc.gpsimd.tensor_tensor(rstd[:, :], rstd[:, :], minus_half[:, :], ALU.pow).then_inc(rstd_done, 1)

            keep_residual(0, 0)

            def step(g, par):
                last = isinstance(g, int) and g == groups - 1
                if not last:
                    keep_residual(g + 1, 1 - par)
                if not (isinstance(g, int) and g == 0):
                    inverse_deviation(g - 1, 0)
                if causal:
                    clear_future(g, par)
                if last:
                    inverse_deviation(g, 0)
            steps(pool, 0, step)

I32 = mybir.dt.int32
E = 8
HID = 1024
HT = HID // P
BITS = 30


def logits_block(nc, tiles, x2_dram, x2, wr_dram, br_dram, ident_dram, logits):
    groups = tiles // NB
    with ExitStack() as c:
        ident = c.enter_context(nc.sbuf_tensor("lg_ident", [P, P], FP32))
        wr = c.enter_context(nc.sbuf_tensor("lg_wr", [P, HALVES, E], FP32))
        br = c.enter_context(nc.sbuf_tensor("lg_br", [P, E], FP32))
        xT = c.enter_context(nc.sbuf_tensor("lg_xT", [P, 2, HALVES, G], FP32))
        tb = [c.enter_context(nc.psum_tensor(f"lg_T{i}", [P, G], FP32)) for i in range(4)]
        lb = [c.enter_context(nc.psum_tensor(f"lg_L{i}", [P, NB, E], FP32)) for i in range(2)]
        const_in = c.enter_context(nc.semaphore("lg_const_in"))
        x_loaded = [c.enter_context(nc.semaphore(f"lg_x_loaded{i}")) for i in range(4)]
        t_full = c.enter_context(nc.semaphore("lg_t_full"))
        a_copied = c.enter_context(nc.semaphore("lg_a_copied"))
        d_copied = c.enter_context(nc.semaphore("lg_d_copied"))
        l_full = c.enter_context(nc.semaphore("lg_l_full"))
        l_done = c.enter_context(nc.semaphore("lg_l_done"))
        block = c.enter_context(nc.Block())

        @block.sync
        def _(sp):
            sp.dma_start(ident[:], ident_dram).then_inc(const_in, 16)
            sp.dma_start(wr[:], wr_dram.rearrange("(t p) n -> p t n", p=P)).then_inc(const_in, 16)
            sp.dma_start(br[:], br_dram.rearrange("(a n) -> a n", a=1).to_broadcast([P, E])).then_inc(const_in, 16)
            for g in range(groups):
                if g >= 4:
                    sp.wait_ge(x_loaded[g % 4], 16 * (g // 4))
                sp.dma_start(x2[:, g * NB:(g + 1) * NB, :],
                             x2_dram[g * G:(g + 1) * G, :].rearrange("(b p) n -> p b n", p=P)).then_inc(x_loaded[g % 4], 16)

        @block.tensor
        def _(pe):
            pe.wait_ge(const_in, 48)

            def logits_of(g):
                pe.wait_ge(a_copied, g + 1)
                pe.wait_ge(d_copied, g + 1)
                if g >= 2:
                    pe.wait_ge(l_done, g - 1)
                for n in range(NB):
                    for t in range(HALVES):
                        last = nc.tensor.matmul(lb[g % 2][:, n, :], xT[:, g % 2, t, n * P:(n + 1) * P], wr[:, t, :],
                                                start=(t == 0), stop=(t == HALVES - 1))
                last.then_inc(l_full, 1)

            for g in range(groups):
                pe.wait_ge(x_loaded[g % 4], 16 * (g // 4 + 1))
                if g >= 2:
                    pe.wait_ge(a_copied, g - 1)
                    pe.wait_ge(d_copied, g - 1)
                for half in range(HALVES):
                    for n in range(NB):
                        last = nc.tensor.matmul(tb[2 * (g % 2) + half][:, n * P:(n + 1) * P],
                                                x2[:, g * NB + n, half * P:(half + 1) * P], ident[:],
                                                start=True, stop=True, is_transpose=True)
                last.then_inc(t_full, 1)
                if g >= 1:
                    logits_of(g - 1)
            logits_of(groups - 1)

        @block.scalar
        def _(act):
            for g in range(groups):
                act.wait_ge(t_full, g + 1)
                if g >= 2:
                    act.wait_ge(l_full, g - 1)
                nc.scalar.copy(xT[:, g % 2, 0, :], tb[2 * (g % 2)][:, :]).then_inc(a_copied, 1)

        @block.vector
        def _(dve):
            def take(g):
                dve.wait_ge(l_full, g + 1)
                nc.vector.tensor_tensor(logits[:, g * NB:(g + 1) * NB, :], lb[g % 2][:, :, :],
                                        br[:, :].unsqueeze(1).to_broadcast([P, NB, E]), ALU.add).then_inc(l_done, 1)
            dve.wait_ge(const_in, 48)
            for g in range(groups):
                dve.wait_ge(t_full, g + 1)
                if g >= 2:
                    dve.wait_ge(l_full, g - 1)
                nc.vector.tensor_copy(xT[:, g % 2, 1, :], tb[2 * (g % 2) + 1][:, :]).then_inc(d_copied, 1)
                if g >= 1:
                    take(g - 1)
            take(groups - 1)


def route_block(nc, tiles, cap, logits, x2, xg_dram, gates, slots, consts):
    dump = E * cap
    CH = P // E
    F = tiles * P // CH
    TJ = F // P
    with ExitStack() as c:
        def sb(name, shape, dt=FP32):
            return c.enter_context(nc.sbuf_tensor("rt_" + name, shape, dt))

        def sem(name):
            return c.enter_context(nc.semaphore("rt_" + name))

        pr = sb("probs", [P, tiles, E])
        eq = sb("eq", [P, tiles, E])
        cand = sb("cand", [P, tiles, E])
        first = sb("first", [P, tiles, E])
        second = sb("second", [P, tiles, E])
        gm = sb("gm", [P, tiles, E])
        runs = sb("runs", [P, TJ, E, CH])
        st = sb("slot_t", [P, tiles, E])
        col = sb("col", [P, tiles])
        col2 = sb("col2", [P, tiles])
        ident = sb("ident", [P, P])
        same = sb("same", [P, P])
        before = sb("before", [P, P])
        ebase = sb("ebase", [P, 1])
        iota8 = sb("iota8", [P, E])
        gt = sb("gt", [P, F])
        above = sb("above", [P, F])
        equal = sb("equal", [P, F])
        ones = sb("ones", [P, F])
        sc_a = sb("sc_a", [P, F])
        sc_e = sb("sc_e", [P, F])
        junk = sb("junk", [P, F])
        thr = sb("thr", [P, 1], I32)
        tryv = sb("tryv", [P, 1], I32)
        bit = sb("bit", [P, 1], I32)
        ok = sb("ok", [P, 1], I32)
        cnt = sb("cnt", [P, 1])
        tot = sb("tot", [P, 2])
        off = sb("off", [P, 2])
        need = sb("need", [P, 1])
        bt = c.enter_context(nc.psum_tensor("rt_T", [P, G], FP32))
        bc = c.enter_context(nc.psum_tensor("rt_C", [P, 8], FP32))
        const_in, dve_done, pe_done, act_done, counted, total, scattered = (
            sem(n) for n in ("const_in", "dve_done", "pe_done", "act_done", "counted", "total", "scattered"))
        routed = sem("routed")
        block = c.enter_context(nc.Block())

        @block.sync
        def _(sp):
            for dst, name in ((ident, "ident"), (same, "same_expert"), (before, "before"), (ebase, "ebase"), (iota8, "iota8")):
                sp.dma_start(dst[:], consts[name]).then_inc(const_in, 16)

        @block.scalar
        def _(act):
            act.wait_ge(routed, 1)
            nc.scalar.activation(pr[:, :, :], pr[:, :, :], ACT.Exp).then_inc(act_done, 1)

        @block.tensor
        def _(pe):
            pe.wait_ge(const_in, 80)
            pe.wait_ge(routed, 2)
            for j in range(TJ):
                last = nc.tensor.matmul(bt[:, j * P:(j + 1) * P], runs[:, j, :, :].rearrange("p e c -> p (e c)"),
                                        ident[:], start=True, stop=True, is_transpose=True)
            last.then_inc(pe_done, 1)
            with pe.Fori(0, BITS) as i:
                pe.wait_ge(counted, i + 1)
                nc.tensor.matmul(bc[:, 0:1], same[:], cnt[:], start=True, stop=True).then_inc(total, 1)
            pe.wait_ge(routed, 3)
            nc.tensor.matmul(bc[:, 2:4], before[:], tot[:], start=True, stop=True)
            nc.tensor.matmul(bc[:, 4:6], same[:], tot[:], start=True, stop=True).then_inc(pe_done, 1)
            pe.wait_ge(routed, 4)
            for j in range(TJ):
                last = nc.tensor.matmul(bt[:, j * P:(j + 1) * P], gt[:, j * P:(j + 1) * P], ident[:],
                                        start=True, stop=True, is_transpose=True)
            last.then_inc(pe_done, 1)

        @block.vector
        def _(dve):
            n = [0]

            def link(ins):
                n[0] += 1
                ins.then_inc(dve_done, 1)
                dve.wait_ge(dve_done, n[0])

            def wide(a):
                return a.unsqueeze(2).to_broadcast([P, tiles, E])

            v = nc.vector
            v.memset(ones[:], 1.0)
            v.memset(thr[:], 0)
            link(v.memset(bit[:], 1 << (BITS - 1)))
            link(v.tensor_reduce(col[:], logits[:], AX, ALU.max))
            v.tensor_tensor(pr[:], logits[:], wide(col[:]), ALU.subtract).then_inc(routed, 1)
            dve.wait_ge(act_done, 1)
            link(v.tensor_reduce(col2[:], pr[:], AX, ALU.add))
            link(v.reciprocal(col[:], col2[:]))
            link(v.tensor_tensor(pr[:], pr[:], wide(col[:]), ALU.mult))
            dve.wait_ge(const_in, 80)
            link(v.tensor_reduce(gates[:, 0, :], pr[:], AX, ALU.max))
            lower = iota8[:].unsqueeze(1).to_broadcast([P, tiles, E])
            for kth, chosen in enumerate((first, second)):
                src = pr if kth == 0 else gm
                link(v.tensor_tensor(eq[:], src[:], wide(gates[:, kth, :]), ALU.is_equal))
                link(v.tensor_tensor(cand[:], eq[:], lower, ALU.mult))
                link(v.tensor_reduce(col[:], cand[:], AX, ALU.min))
                link(v.tensor_tensor(chosen[:], cand[:], wide(col[:]), ALU.is_equal))
                if kth == 0:
                    link(v.scalar_tensor_tensor(gm[:], chosen[:], -2.0, pr[:], ALU.mult, ALU.add))
                    link(v.tensor_reduce(gates[:, 1, :], gm[:], AX, ALU.max))
            link(v.tensor_tensor(eq[:], first[:], second[:], ALU.add))
            link(v.tensor_tensor(cand[:], pr[:], eq[:], ALU.mult))
            by_run = "p (c j) e -> p j e c"
            for j in range(TJ):
                ins = v.scalar_tensor_tensor(runs[:, j], eq[:].rearrange(by_run, j=TJ)[:, j], -1.0,
                                             cand[:].rearrange(by_run, j=TJ)[:, j], ALU.add, ALU.add)
            ins.then_inc(routed, 1)
            dve.wait_ge(pe_done, 1)
            link(v.tensor_copy(gt[:], bt[:]))
            base = n[0]
            with dve.Fori(0, BITS) as i:
                v.tensor_tensor(tryv[:], thr[:], bit[:], ALU.bitwise_or).then_inc(dve_done, 1)
                dve.wait_ge(dve_done, i * 4 + (base + 1))
                v.tensor_scalar(junk[:], gt[:], tryv[:].bitcast(FP32), 0.0, ALU.is_ge, ALU.add,
                                accum_out=cnt[:]).then_inc(counted, 1)
                dve.wait_ge(total, i + 1)
                v.tensor_scalar(ok[:], bc[:, 0:1], float(cap), bit[:, 0:1], ALU.is_ge, ALU.mult).then_inc(dve_done, 1)
                dve.wait_ge(dve_done, i * 4 + (base + 2))
                v.tensor_tensor(thr[:], thr[:], ok[:], ALU.bitwise_or).then_inc(dve_done, 1)
                v.tensor_scalar(bit[:], bit[:], 1, None, ALU.logical_shift_right).then_inc(dve_done, 1)
                dve.wait_ge(dve_done, i * 4 + (base + 4))
            n[0] = base + 4 * BITS
            dve.wait_ge(counted, BITS)
            t = thr[:].bitcast(FP32)
            link(v.tensor_scalar(above[:], gt[:], t, None, ALU.is_gt))
            link(v.tensor_scalar(equal[:], gt[:], t, None, ALU.is_equal))
            link(v.tensor_tensor_scan(sc_a[:], ones[:], above[:], 0.0, ALU.mult, ALU.add))
            link(v.tensor_tensor_scan(sc_e[:], ones[:], equal[:], 0.0, ALU.mult, ALU.add))
            v.tensor_copy(tot[:, 0:1], sc_a[:, F - 1:F])
            link(v.tensor_copy(tot[:, 1:2], sc_e[:, F - 1:F]))
            v.engine_nop().then_inc(routed, 1) if False else v.memset(junk[:, 0:1], 0.0).then_inc(routed, 1)
            dve.wait_ge(pe_done, 2)
            link(v.tensor_copy(off[:], bc[:, 2:4]))
            link(v.tensor_scalar(need[:], bc[:, 4:5], -1.0, float(cap), ALU.mult, ALU.add))
            link(v.scalar_tensor_tensor(sc_e[:], sc_e[:], off[:, 1:2], equal[:], ALU.add, ALU.subtract))
            link(v.scalar_tensor_tensor(sc_a[:], sc_a[:], off[:, 0:1], above[:], ALU.add, ALU.subtract))
            link(v.scalar_tensor_tensor(equal[:], sc_e[:], need[:, 0:1], equal[:], ALU.is_lt, ALU.mult))
            link(v.scalar_tensor_tensor(sc_a[:], sc_e[:], need[:, 0:1], sc_a[:], ALU.min, ALU.add))
            link(v.tensor_tensor(equal[:], equal[:], above[:], ALU.add))
            v.scalar_tensor_tensor(gt[:], sc_a[:], ebase[:, 0:1], equal[:], ALU.add, ALU.mult).then_inc(routed, 1)
            dve.wait_ge(pe_done, 3)
            for j in range(TJ):
                ins = v.tensor_copy(st[:].rearrange(by_run, j=TJ)[:, j], bt[:].rearrange("p (j e c) -> p j e c", j=TJ, e=E)[:, j])
            link(ins)
            for kth, chosen in enumerate((first, second)):
                link(v.tensor_tensor(cand[:], chosen[:], st[:], ALU.mult))
                link(v.tensor_reduce(col[:], cand[:], AX, ALU.add))
                link(v.tensor_scalar(slots[:, kth, :], col[:], float(dump), None, ALU.add))
            v.memset(junk[:, 0:1], 0.0).then_inc(routed, 1)

        @block.gpsimd
        def _(pool):
            pool.wait_ge(routed, 5)
            for t in range(tiles):
                for kth in range(2):
                    nc.gpsimd.indirect_dma_start(xg_dram, bass.IndirectOffsetOnAxis(ap=slots[:, kth, t:t + 1], axis=0),
                                                 x2[:, t, :], None, bounds_check=dump - 1,
                                                 oob_is_err=False).then_inc(scattered, 16)
            pool.wait_ge(scattered, 32 * tiles)


def experts_block(nc, cap, xg_dram, og_dram, w, ident_dram):
    CHUNK = 4 * P
    chunks = [(s, min(CHUNK, cap - s)) for s in range(0, cap, CHUNK)]
    NC = len(chunks)
    UP = 4
    tiles_of = [[(o, min(P, n - o)) for o in range(0, n, P)] for _, n in chunks]
    per_e = sum(len(t) for t in tiles_of)
    before = [sum(len(t) for t in tiles_of[:c]) for c in range(NC)]
    pairs = E // 2
    assert per_e % 2 == 0 or True
    with ExitStack() as c:
        def sb(name, shape, dt=FP32):
            return c.enter_context(nc.sbuf_tensor("ex_" + name, shape, dt))

        def sem(name):
            return c.enter_context(nc.semaphore("ex_" + name))

        w1 = sb("w1", [P, 2, HALVES, HID])
        w2 = sb("w2", [P, 2, HT, D])
        b1 = sb("b1", [P, 2, HT])
        b2 = sb("b2", [P, 2, D])
        xg = sb("xg", [P, 2, NB, D])
        xT = sb("xT", [P, 2, HALVES, G])
        hT = sb("hT", [P, 2, HT, G])
        o = sb("o", [P, 2, NB, D])
        ident = sb("ident", [P, P])
        T = [c.enter_context(nc.psum_tensor(f"ex_T{i}", [P, G], FP32)) for i in range(2)]
        U = [c.enter_context(nc.psum_tensor(f"ex_U{i}", [P, G], FP32)) for i in range(UP)]
        Dn = [c.enter_context(nc.psum_tensor(f"ex_D{i}", [P, D], FP32)) for i in range(2)]
        ident_in = sem("ident_in")
        w_loaded = [sem(f"w_loaded{i}") for i in range(2)]
        x_loaded = [sem(f"x_loaded{i}") for i in range(2)]
        o_stored = [sem(f"o_stored{i}") for i in range(2)]
        t_full, t_done, u_full, u_done, d_full, d_done, o_ready = (
            sem(n) for n in ("t_full", "t_done", "u_full", "u_done", "d_full", "d_done", "o_ready"))
        block = c.enter_context(nc.Block())

        def pairwise(eng, body):
            def pair(e0):
                for j in range(2):
                    for ch in range(NC):
                        body(e0 + j, j, ch)
            pair(0)
            with eng.Fori(1, pairs - 1) as it:
                pair(it * 2)
            pair(E - 2)

        def par(j, ch):
            return (NC * j + ch) % 2

        def o_before(e, ch):
            return e * per_e + before[ch]

        def dmas(e, j, ch, pr):
            def of(ch2):
                n = chunks[ch2][1]
                return 16 * ((n >= P) + (n % P > 0))
            per_pair = sum(of(ch2) for j2 in range(2) for ch2 in range(NC) if par(j2, ch2) == pr)
            inside = sum(of(ch2) for j2 in range(2) for ch2 in range(NC)
                         if par(j2, ch2) == pr and NC * j2 + ch2 < NC * j + ch)
            assert per_pair % 2 == 0
            return (e - j) * (per_pair // 2) + inside

        def after(e, j, ch, pr):
            n = chunks[ch][1]
            return dmas(e, j, ch, pr) + 16 * ((n >= P) + (n % P > 0))

        @block.sync
        def _(sp):
            sp.dma_start(ident[:], ident_dram).then_inc(ident_in, 16)

            def load_w(e, j):
                ix = bass.ds(e, 1)
                sp.dma_start(w1[:, j], w["w1"][ix].rearrange("a (t p) n -> p (a t) n", p=P)).then_inc(w_loaded[j], 16)
                sp.dma_start(w2[:, j], w["w2"][ix].rearrange("a (t p) n -> p (a t) n", p=P)).then_inc(w_loaded[j], 16)
                sp.dma_start(b1[:, j], w["b1"][ix].rearrange("a (t p) -> p (a t)", p=P), allow_slow_non_contiguous=True).then_inc(w_loaded[j], 16)
                sp.dma_start(b2[:, j], w["b2"][ix].to_broadcast([P, D])).then_inc(w_loaded[j], 16)

            def load_x(e, j, ch):
                s, n = chunks[ch]
                pr = par(j, ch)
                full = n // P
                if full:
                    sp.dma_start(xg[:, pr, 0:full, :], xg_dram[bass.ds(e * cap + s, full * P), :]
                                 .rearrange("(b p) n -> p b n", p=P)).then_inc(x_loaded[pr], 16)
                if n % P:
                    sp.dma_start(xg[0:n % P, pr, full, :], xg_dram[bass.ds(e * cap + s + full * P, n % P), :]).then_inc(x_loaded[pr], 16)

            load_w(0, 0)
            load_x(0, 0, 0)
            load_x(0, 0, 1)
            load_w(1, 1)

            def body(e, j, ch):
                s = e * NC + ch
                if not (isinstance(e, int) and s + 2 >= E * NC):
                    wait(sp, t_full, (s + 1) * 2)
                    load_x(e + (ch + 2) // NC, (j + (ch + 2) // NC) % 2, (ch + 2) % NC)
                if not (isinstance(e, int) and s == 0):
                    pj, pc = ((j, ch - 1) if ch else (1 - j, NC - 1))
                    store(e if ch else e - 1, pj, pc)
                if ch == 0 and not (isinstance(e, int) and (e < 1 or e + 1 >= E)):
                    load_w(e + 1, 1 - j)

            def store(e, j, ch):
                s, n = chunks[ch]
                pr = par(j, ch)
                sp.wait_ge(d_done, o_before(e, ch) + len(tiles_of[ch]))
                full = n // P
                if full:
                    sp.dma_start(og_dram[bass.ds(e * cap + s, full * P), :].rearrange("(b p) n -> p b n", p=P),
                                 o[:, pr, 0:full, :]).then_inc(o_stored[pr], 16)
                if n % P:
                    sp.dma_start(og_dram[bass.ds(e * cap + s + full * P, n % P), :], o[0:n % P, pr, full, :]).then_inc(o_stored[pr], 16)
            pairwise(sp, body)
            store(E - 1, 1, NC - 1)
            for pr in range(2):
                sp.wait_ge(o_stored[pr], dmas(E, 0, 0, pr))

        @block.tensor
        def _(pe):
            pe.wait_ge(ident_in, 16)

            def transpose_x(e, j, ch):
                s = e * NC + ch
                pr = par(j, ch)
                pe.wait_ge(x_loaded[pr], after(e, j, ch, pr))
                for half in range(HALVES):
                    wait(pe, t_done, s * 2 + half - 1)
                    for b, (off, n) in enumerate(tiles_of[ch]):
                        last = nc.tensor.matmul(T[half][:, off:off + n], xg[0:n, pr, b, half * P:(half + 1) * P],
                                                ident[0:n, 0:n], start=True, stop=True, is_transpose=True)
                    last.then_inc(t_full, 1)

            def up(e, j, ch):
                s = e * NC + ch
                n = chunks[ch][1]
                if ch == 0:
                    pe.wait_ge(w_loaded[j], ((e - j) // 2 + 1) * 64 if isinstance(e, int) else (e - j) * 32 + 64)
                pe.wait_ge(t_done, (s + 1) * 2)
                for m in range(HT):
                    wait(pe, u_done, s * HT + m - UP + 1)
                    for t in range(HALVES):
                        last = nc.tensor.matmul(U[m % UP][:, 0:n], w1[:, j, t, m * P:(m + 1) * P],
                                                xT[:, par(j, ch), t, 0:n], start=(t == 0), stop=(t == HALVES - 1))
                    last.then_inc(u_full, 1)

            def down(e, j, ch):
                s = e * NC + ch
                pe.wait_ge(u_done, (s + 1) * HT)
                for b, (off, n) in enumerate(tiles_of[ch]):
                    idx = o_before(e, ch) + b
                    wait(pe, d_done, idx - 1)
                    for t in range(HT):
                        last = nc.tensor.matmul(Dn[(j * per_e + before[ch] + b) % 2][0:n, :], hT[:, par(j, ch), t, off:off + n],
                                                w2[:, j, t, :], start=(t == 0), stop=(t == HT - 1))
                    last.then_inc(d_full, 1)

            transpose_x(0, 0, 0)

            def body(e, j, ch):
                last = isinstance(e, int) and e == E - 1 and ch == NC - 1
                if not last:
                    nx = ch + 1
                    transpose_x(e + nx // NC, (j + nx // NC) % 2, nx % NC)
                up(e, j, ch)
                if not (isinstance(e, int) and e == 0 and ch == 0):
                    down(*((e, j, ch - 1) if ch else (e - 1, 1 - j, NC - 1)))
            pairwise(pe, body)
            down(E - 1, 1, NC - 1)

        @block.scalar
        def _(act):
            def body(e, j, ch):
                s = e * NC + ch
                n = chunks[ch][1]
                if ch == 0:
                    act.wait_ge(w_loaded[j], ((e - j) // 2 + 1) * 64 if isinstance(e, int) else (e - j) * 32 + 64)
                for m in range(HT):
                    act.wait_ge(u_full, s * HT + m + 1)
                    if m == 0 and not (isinstance(e, int) and s < 2):
                        act.wait_ge(d_full, o_before(e, ch - 1) if ch else o_before(e, 0) - len(tiles_of[NC - 1]))
                    nc.scalar.activation(hT[:, par(j, ch), m, 0:n], U[m % UP][:, 0:n], ACT.Silu,
                                         bias=b1[:, j, m:m + 1]).then_inc(u_done, 1)
            pairwise(act, body)

        @block.vector
        def _(dve):
            def take_x(e, j, ch):
                s = e * NC + ch
                n = chunks[ch][1]
                for half in range(HALVES):
                    dve.wait_ge(t_full, s * 2 + half + 1)
                    if half == 0 and not (isinstance(e, int) and s < 2):
                        dve.wait_ge(u_full, (s - 1) * HT)
                    nc.vector.tensor_copy(xT[:, par(j, ch), half, 0:n], T[half][:, 0:n]).then_inc(t_done, 1)

            def take_o(e, j, ch):
                pr = par(j, ch)
                s = e * NC + ch
                if not (isinstance(e, int) and s < 2):
                    dve.wait_ge(o_stored[pr], dmas(e, j, ch, pr))
                if ch == 0:
                    dve.wait_ge(w_loaded[j], ((e - j) // 2 + 1) * 64 if isinstance(e, int) else (e - j) * 32 + 64)
                for b, (off, n) in enumerate(tiles_of[ch]):
                    idx = o_before(e, ch) + b
                    dve.wait_ge(d_full, idx + 1)
                    nc.vector.tensor_tensor(o[0:n, pr, b, :], Dn[(j * per_e + before[ch] + b) % 2][0:n, :],
                                            b2[0:n, j, :], ALU.add).then_inc(d_done, 1)

            take_x(0, 0, 0)

            def body(e, j, ch):
                last = isinstance(e, int) and e == E - 1 and ch == NC - 1
                if not last:
                    nx = ch + 1
                    take_x(e + nx // NC, (j + nx // NC) % 2, nx % NC)
                if not (isinstance(e, int) and e == 0 and ch == 0):
                    take_o(*((e, j, ch - 1) if ch else (e - 1, 1 - j, NC - 1)))
            pairwise(dve, body)
            take_o(E - 1, 1, NC - 1)


def combine_block(nc, tiles, cap, x2, gates, slots, og_dram, out_dram):
    dump = E * cap
    groups = tiles // NB
    R = 3
    with ExitStack() as c:
        def sb(name, shape, dt=FP32):
            return c.enter_context(nc.sbuf_tensor("cb_" + name, shape, dt))

        def sem(name):
            return c.enter_context(nc.semaphore("cb_" + name))

        r = sb("rows", [P, R, 2, NB, D])
        zero = sb("zero", [1, D])
        stats = sb("stats", [P, 2, NB, 6])
        mv = sb("mv", [P, 2, NB, 2])
        rstd = sb("rstd", [P, 2, NB])
        shift = sb("shift", [P, 2, NB])
        minus_half = sb("minus_half", [P, NB])
        zeroed, ready = sem("zeroed"), sem("ready")
        gathered = [sem(f"gathered{i}") for i in range(R)]
        summed, stats_done, rstd_done, y_ready, dve_chain, pool_chain = (
            sem(n) for n in ("summed", "stats_done", "rstd_done", "y_ready", "dve_chain", "pool_chain"))
        stored = sem("stored")
        block = c.enter_context(nc.Block())

        @block.sync
        def _(sp):
            sp.wait_ge(ready, 1)
            sp.dma_start(og_dram[dump:dump + 1, :], zero[:]).then_inc(zeroed, 16)
            for g in range(groups):
                sp.wait_ge(y_ready, g + 1)
                sp.dma_start(out_dram[g * G:(g + 1) * G, :].rearrange("(b p) n -> p b n", p=P),
                             x2[:, g * NB:(g + 1) * NB, :]).then_inc(stored, 16)
            sp.wait_ge(stored, 16 * groups)

        @block.gpsimd
        def _(pool):
            nc.gpsimd.memset(minus_half[:], -0.5)
            nc.gpsimd.memset(zero[:], 0.0).then_inc(ready, 1)
            pool.wait_ge(zeroed, 16)

            def gather(g):
                if g >= R:
                    pool.wait_ge(summed, g - R + 1)
                for n in range(NB):
                    for kth in range(2):
                        t = g * NB + n
                        nc.gpsimd.indirect_dma_start(r[:, g % R, kth, n, :], None, og_dram,
                                                     bass.IndirectOffsetOnAxis(ap=slots[:, kth, t:t + 1], axis=0),
                                                     bounds_check=dump).then_inc(gathered[g % R], 16)

            def inverse_deviation(g):
                pool.wait_ge(stats_done, g + 1)
                if g >= 2:
                    pool.wait_ge(y_ready, g - 1)
                nc.gpsimd.tensor_scalar(shift[:, g % 2], mv[:, g % 2, :, 0], -1.0, None, ALU.mult)
                nc.gpsimd.tensor_scalar(rstd[:, g % 2], mv[:, g % 2, :, 1], EPS, None, ALU.add).then_inc(pool_chain, 1)
                pool.wait_ge(pool_chain, 2 * g + 1)
                pool.wait_ge(ready, 1)
                nc.gpsimd.tensor_tensor(rstd[:, g % 2], rstd[:, g % 2], minus_half[:], ALU.pow).then_inc(pool_chain, 1)
                pool.wait_ge(pool_chain, 2 * g + 2)
                nc.gpsimd.tensor_tensor(shift[:, g % 2], shift[:, g % 2], rstd[:, g % 2], ALU.mult).then_inc(rstd_done, 1)
            for g in range(groups):
                gather(g)
                if g >= 2:
                    inverse_deviation(g - 2)
            inverse_deviation(groups - 2)
            inverse_deviation(groups - 1)

        @block.vector
        def _(dve):
            n_links = [0]

            def link(ins):
                n_links[0] += 1
                ins.then_inc(dve_chain, 1)
                dve.wait_ge(dve_chain, n_links[0])
            for g in range(groups):
                dve.wait_ge(gathered[g % R], 16 * 2 * NB * (g // R + 1))
                for kth in range(2):
                    for n in range(NB):
                        t = g * NB + n
                        ins = nc.vector.scalar_tensor_tensor(x2[:, t, :], r[:, g % R, kth, n, :], gates[:, kth, t:t + 1],
                                                             x2[:, t, :], ALU.mult, ALU.add)
                    if kth == 0:
                        link(ins)
                    else:
                        ins.then_inc(summed, 1)
                dve.wait_ge(summed, g + 1)
                for n in range(NB):
                    ins = nc.vector.bn_stats(stats[:, g % 2, n, :], x2[:, g * NB + n, :])
                link(ins)
                if g >= 2:
                    dve.wait_ge(y_ready, g - 1)
                for n in range(NB):
                    ins = nc.vector.bn_aggr(mv[:, g % 2, n, :], stats[:, g % 2, n, :])
                ins.then_inc(stats_done, 1)

        @block.scalar
        def _(act):
            for g in range(groups):
                act.wait_ge(rstd_done, g + 1)
                act.wait_ge(summed, g + 1)
                for n in range(NB):
                    t = g * NB + n
                    ins = nc.scalar.activation(x2[:, t, :], x2[:, t, :], ACT.Identity,
                                               bias=shift[:, g % 2, n:n + 1], scale=rstd[:, g % 2, n:n + 1])
                ins.then_inc(y_ready, 1)


def fill_block(nc, dram, rows):
    with ExitStack() as c:
        n = 8
        z = c.enter_context(nc.sbuf_tensor("fill_z", [P, n * D], FP32))
        made = c.enter_context(nc.semaphore("fill_made"))
        filled = c.enter_context(nc.semaphore("fill_filled"))
        block = c.enter_context(nc.Block())

        @block.vector
        def _(dve):
            nc.vector.memset(z[:], 0.0).then_inc(made, 1)

        @block.sync
        def _(sp):
            sp.wait_ge(made, 1)
            count = 0
            for at in range(0, rows - n * P + 1, n * P):
                sp.dma_start(dram[at:at + n * P, :].rearrange("(p b) n -> p (b n)", p=P), z[:]).then_inc(filled, 16)
                count += 1
            rest = rows % (n * P)
            at = rows - rest
            while rest:
                k = min(P, rest)
                sp.dma_start(dram[at:at + k, :], z[0:k, 0:D]).then_inc(filled, 16)
                at, rest, count = at + k, rest - k, count + 1
            sp.wait_ge(filled, 16 * count)


def decoder_layer(nc, ins, out):
    tokens = ins["x"].shape[0]
    cap = -(-tokens * 12 // (10 * E))
    tiles = tokens // P
    groups = tokens // G
    x1 = nc.dram_tensor("x1", [tokens, D], FP32, kind="Internal").ap()
    x2d = nc.dram_tensor("x2", [tokens, D], FP32, kind="Internal").ap()
    xg = nc.dram_tensor("xg", [E * cap, D], FP32, kind="Internal").ap()
    og = nc.dram_tensor("og", [E * cap + 1, D], FP32, kind="Internal").ap()
    fill_block(nc, xg, E * cap)
    attention_block(nc, True, groups, ins["x"], None, x1,
                    {k: ins["attn_" + k] for k in ("wq", "wk", "wv", "wo")}, ins)
    attention_block(nc, False, groups, x1, ins["ctx"], x2d,
                    {k: ins["xattn_" + k] for k in ("wq", "wk", "wv", "wo", "bq", "bk", "bv", "bo")}, ins)
    with ExitStack() as c:
        x2 = c.enter_context(nc.sbuf_tensor("x2_sb", [P, tiles, D], FP32))
        logits = c.enter_context(nc.sbuf_tensor("logits", [P, tiles, E], FP32))
        gates = c.enter_context(nc.sbuf_tensor("gates", [P, 2, tiles], FP32))
        slots = c.enter_context(nc.sbuf_tensor("slots", [P, 2, tiles], I32))
        logits_block(nc, tiles, x2d, x2, ins["wr"], ins["br"], ins["ident"], logits)
        route_block(nc, tiles, cap, logits, x2, xg, gates, slots, ins)
        experts_block(nc, cap, xg, og, {k: ins[k] for k in ("w1", "w2", "b1", "b2")}, ins["ident"])
        combine_block(nc, tiles, cap, x2, gates, slots, og, out)


def tables(tokens):
    import numpy as np
    cap = -(-tokens * 12 // (10 * E))
    pos = np.arange(P)
    slopes = (2.0 ** (-8.0 / H * (np.arange(H, dtype=np.float32) + 1.0))).astype(np.float32)
    head_mask = (pos[:, None] // DK == np.arange(HEADS_HALF)[None, :]).astype(np.float32)
    sel = np.zeros((P, H, P), np.float32)
    for h in range(H):
        sel[h, h, :] = sel[H + h, h, :] = -1.0
    sel_causal = sel.copy()
    for h in range(H):
        rest = slopes[h] * pos.astype(np.float32)
        for j in range(3):
            bits = rest.astype(np.float32).view(np.uint32)
            part = (bits & np.uint32(0xFFFF0000)).view(np.float32)
            sel_causal[2 * H + j, h, :] = part
            rest = rest - part
    coarse_mask = np.zeros((P, NB, P), np.float32)
    coarse_mask[2 * H:2 * H + 3] = 1.0
    for j in range(P // 2):
        sel_causal[P // 2 + j, :, 2 * j:2 * j + 2] = 1.0
        coarse_mask[P // 2 + j] = np.where(j > pos // 2, -1e30, 0.0)
    bias_tab = np.where(pos[None, None, :] > pos[:, None, None], -1e30,
                        slopes[None, :, None] * pos[None, None, :]).astype(np.float32)
    ch = P // E
    same = (pos[:, None] // ch == pos[None, :] // ch).astype(np.float32)
    before = same * (pos[:, None] < pos[None, :])
    ebase = (pos // ch * cap - E * cap).astype(np.float32).reshape(P, 1)
    iota8 = np.tile(np.arange(E, dtype=np.float32) - E, (P, 1))
    return {"ident": np.eye(P, dtype=np.float32), "head_mask": head_mask, "sel": sel.reshape(P, 4, G),
            "sel_causal": sel_causal.reshape(P, 4, G), "coarse_mask": coarse_mask.reshape(P, G),
            "bias_tab": bias_tab.astype(np.float32).reshape(P, 4, G), "same_expert": same,
            "before": before.astype(np.float32), "ebase": ebase, "iota8": iota8.astype(np.float32)}


def kernel(**inputs):
    import numpy as _np
    import concourse.bacc as _bacc
    from concourse import mybir as _mybir
    from concourse.bass_utils import run_bass_kernel_spmd as _run

    a = {n: _np.asarray(v) for n, v in inputs.items()}
    b, s, d = a["x"].shape
    w_in = a["L0_attn_w_in"]
    arrays = {
        "x": a["x"].reshape(b * s, d), "ctx": a["ctx_1024"].reshape(b * s, d),
        "attn_wq": w_in[0:d].T, "attn_wk": w_in[d:2 * d].T, "attn_wv": w_in[2 * d:3 * d].T,
        "attn_wo": a["L0_attn_w_out"].T,
        "xattn_wq": a["L0_xattn_Wq"], "xattn_wk": a["L0_xattn_Wk"], "xattn_wv": a["L0_xattn_Wv"],
        "xattn_wo": a["L0_xattn_Wo"], "xattn_bq": a["L0_xattn_bq"], "xattn_bk": a["L0_xattn_bk"],
        "xattn_bv": a["L0_xattn_bv"], "xattn_bo": a["L0_xattn_bo"],
        "wr": a["L0_ffn_Wr"], "br": a["L0_ffn_br"], "w1": a["L0_ffn_W1"], "b1": a["L0_ffn_b1"],
        "w2": a["L0_ffn_W2"], "b2": a["L0_ffn_b2"], **tables(b * s)}
    nc = _bacc.Bacc("TRN2", target_bir_lowering=False, num_devices=1)
    ins, feed = {}, {}
    for name, v in arrays.items():
        v = _np.ascontiguousarray(v)
        feed["in_" + name] = v
        ins[name] = nc.dram_tensor("in_" + name, v.shape, _mybir.dt.from_np(v.dtype), kind="ExternalInput").ap()
    out = nc.dram_tensor("out", (b * s, d), _mybir.dt.float32, kind="ExternalOutput").ap()
    decoder_layer(nc, ins, out)
    r = _run(nc, [feed], core_ids=[0])
    return _np.asarray(r.results[0]["out"]).reshape(b, s, d)
```

```python
import concourse.bass as bass
from concourse import mybir
from contextlib import ExitStack

FP32 = mybir.dt.float32
BF16 = mybir.dt.bfloat16
FP32R = mybir.dt.float32r
ALU = mybir.AluOpType
ACT = mybir.ActivationFunctionType
AX = mybir.AxisListType.X

P = 128
D = 256
H = 16
DK = D // H
NB = 4
G = NB * P
HALVES = D // P
HEADS_HALF = H // HALVES
QUADS = H // 4
PAIRS = H // 2
PAIR = 2 * DK
EXTRA = 3 * PAIR
QK_LOADS = 9
VW = 32
RING = 4
EPS = 1e-5


def wait(eng, sem, value):
    if not isinstance(value, int) or value > 0:
        eng.wait_ge(sem, value)


def wait_apart(engine, scratch, *waits):
    for sem, value in waits:
        engine.wait_ge(sem, value)
    tile, turn = scratch
    turn[0] = turn[0] % (tile.shape[1] - 1) + 1
    engine.tensor_tensor(tile[:, turn[0]:turn[0] + 1], tile[:, 0:1], tile[:, 0:1], ALU.add)


def matmul3(nc, out, left, right, start, stop, pick_l, pick_r):
    for n, (a, b) in enumerate(((0, 0), (0, 1), (1, 0))):
        last = nc.tensor.matmul(out, pick_l(left, a), pick_r(right, b), start=(start and n == 0), stop=(stop and n == 2))
    return last


def attention_block(nc, causal, groups, x_in, ctx_in, x_outs, qk_dram, w, consts):
    kv_own = ctx_in is not None
    n_tr = HALVES * (2 if kv_own else 1)
    n_proj = n_tr + 2 * HALVES
    n_b = n_proj + QUADS + HALVES
    n_c = 1 + QUADS + 4

    tag = "self_" if causal else "cross_"
    with ExitStack() as c:
        def sb(name, shape, dt=FP32):
            return c.enter_context(nc.sbuf_tensor(tag + name, shape, dt))

        def sem(name):
            return c.enter_context(nc.semaphore(tag + name))

        x = sb("x", [P, 2, NB, D])
        ctx = sb("ctx", [P, 2, NB, D]) if kv_own else x
        xr = sb("xr", [P, 2, NB, D])
        xT = sb("xT", [P, 2, HALVES, G], FP32R)
        cT = sb("cT", [P, 2, HALVES, G], FP32R) if kv_own else xT
        qk = sb("qk", [P, 2, 2, HALVES, G], FP32R)
        qq = sb("qq", [P, H, G], FP32R)
        kk = sb("kk", [P, PAIRS, G], FP32R)
        v = sb("v", [P, NB, H, VW])
        pr = sb("pr", [P, 2, NB, G])
        oq = sb("oq", [P, 2, G])
        on = sb("on", [P, NB, D])
        oT = sb("oT", [P, 2, HALVES, G], FP32R)
        y = sb("y", [P, 2, NB, D])
        wq = sb("wq", [P, 2, HALVES, D], FP32R)
        wk = sb("wk", [P, 2, HALVES, D], FP32R)
        wv = sb("wv", [P, 2, HALVES, D], FP32R)
        wo = sb("wo", [P, 2, HALVES, D], FP32R)
        sel = sb("sel", [P, H, P], BF16)
        mT = sb("mT", [P, G], BF16)
        ident = sb("ident", [P, P])
        ident_b = sb("ident_b", [P, P], BF16)
        mx = sb("mx", [P, NB, H])
        m2 = sb("m2", [P, NB, 2 * H], BF16)
        rden = sb("rden", [P, NB, 4])
        stats = sb("stats", [P, NB, 6])
        mv = sb("mv", [P, NB, 2])
        rstd = sb("rstd", [P, NB])
        minus_half = sb("minus_half", [P, NB])
        scratch_v = (sb("scratch_v", [P, 9]), [0])
        scratch_p = (sb("scratch_p", [P, 65]), [0])
        if causal:
            bias_tab = sb("bias_tab", [P, H, P], BF16)
        if kv_own:
            bq = sb("bq", [P, HALVES])
            bk = sb("bk", [P, HALVES])
            bv = sb("bv", [P, D])
            bo = sb("bo", [P, D])
        A = [c.enter_context(nc.psum_tensor(f"{tag}A{i}", [P, G], FP32)) for i in range(RING)]
        B = [c.enter_context(nc.psum_tensor(f"{tag}B{i}", [P, G], FP32)) for i in range(2)]
        C = [c.enter_context(nc.psum_tensor(f"{tag}C{i}", [P, G], FP32)) for i in range(2)]

        ident_in = sem("ident_in")
        const_in = sem("const_in")
        sel_in = sem("sel_in")
        table_in = sem("table_in")
        const_ready = sem("const_ready")
        scratch_ready = sem("scratch_ready")
        x_loaded = [sem(f"x_loaded{i}") for i in range(2)]
        c_loaded = [sem(f"c_loaded{i}") for i in range(2)]
        y_stored = [sem(f"y_stored{i}") for i in range(2)]
        a_full = sem("a_full")
        b_full = sem("b_full")
        b_done = sem("b_done")
        lo_done = sem("lo_done")
        c_full = sem("c_full")
        c_done = sem("c_done")
        max_done = sem("max_done")
        m2_ready = sem("m2_ready")
        exp_done = sem("exp_done")
        sel_done = sem("sel_done")
        cleared = sem("cleared")
        q_stored = sem("q_stored")
        k_stored = sem("k_stored")
        qk_loaded = [sem(f"qk_loaded{i}") for i in range(HALVES)]
        xr_ready = sem("xr_ready")
        stats_done = sem("stats_done")
        rstd_done = sem("rstd_done")
        y_ready = sem("y_ready")
        dve_chain = sem("dve_chain")
        pool_chain = sem("pool_chain")
        block = c.enter_context(nc.Block())
        y_stage = y[:].rearrange("p a n d -> p (a n d)").rearrange("p (w t d) -> p w t d", w=4, t=HALVES)
        on_stage = on[:].rearrange("p n d -> p (n d)")[:, 0:G]

        def is_last(g):
            return isinstance(g, int) and g == groups - 1

        def is_first(g):
            return isinstance(g, int) and g == 0

        def in_step(g, first, per_step, without_output):
            return first if is_first(g) else first + without_output + (g - 1) * per_step

        def b_step(g):
            return in_step(g, n_proj, n_b, n_proj + QUADS)

        def b_p(g, i):
            if is_first(g):
                return i
            late = HALVES if i >= HALVES and not (isinstance(g, int) and g == 1) else 0
            return b_step(g - 1) + i + late

        def b_oq(g, quad):
            return b_step(g) + (0 if is_last(g) else n_proj) + (0 if is_first(g) else HALVES) + quad

        def b_ot(g, half):
            if is_last(g):
                return b_oq(g, QUADS) + half
            return b_step(g + 1) + (0 if is_last(g + 1) else HALVES) + half

        n_lo = n_proj + HALVES

        def lo_step(g):
            return in_step(g, n_proj, n_lo, n_proj)

        def lo_p(g, i):
            if is_first(g):
                return i
            late = HALVES if i >= HALVES and not (isinstance(g, int) and g == 1) else 0
            return lo_step(g - 1) + i + late

        def lo_o(g, half):
            if is_last(g):
                return lo_step(g) + HALVES + half
            return lo_step(g + 1) + (0 if is_last(g + 1) else HALVES) + half

        def c_step(g):
            return in_step(g, 2, n_c, n_c - 2)

        def c_out(g, i):
            if is_last(g):
                return c_m(g) + 1 + QUADS + i
            return c_step(g + 1) + i

        def c_m(g):
            return c_step(g) + (0 if is_first(g) else 2)

        def c_v(g, i):
            return i if is_first(g) else c_m(g - 1) + QUADS + i

        def c_quad(g, quad):
            return c_m(g) + 1 + quad + (2 if quad == QUADS - 1 and not is_last(g) else 0)

        def steps(eng, body):
            body(0, 0)
            body(1, 1)
            with eng.Fori(1, groups // 2 - 1) as it:
                for par in range(2):
                    body(it * 2 + par, par)
            body(groups - 2, 0)
            body(groups - 1, 1)

        def par_of(fn, g, par, *a):
            gg = g if isinstance(g, int) else 4 + par
            return fn(gg, *a) % 2

        @block.sync
        def _(sp):
            sp.dma_start(ident[:], consts["ident"]).then_inc(ident_in, 16)

            def load(g, par):
                rows = bass.ds(g * G, G)
                sp.dma_start(x[:, par], x_in[rows, :].rearrange("(b p) n -> p b n", p=P)).then_inc(x_loaded[par], 16)
                if kv_own:
                    sp.dma_start(ctx[:, par], ctx_in[rows, :].rearrange("(b p) n -> p b n", p=P)).then_inc(c_loaded[par], 16)

            load(0, 0)
            for i, name in enumerate(("wq", "wk", "wv", "wo")):
                sp.dma_start(y_stage[:, i], w[name].rearrange("(t p) n -> p t n", p=P)).then_inc(const_in, 16)
            if kv_own:
                sp.dma_start(bq[:], w["bq"].rearrange("(t p) -> p t", p=P), allow_slow_non_contiguous=True).then_inc(const_in, 16)
                sp.dma_start(bk[:], w["bk"].rearrange("(t p) -> p t", p=P), allow_slow_non_contiguous=True).then_inc(const_in, 16)
                sp.dma_start(bv[:], w["bv"].rearrange("(a n) -> a n", a=1).to_broadcast([P, D])).then_inc(const_in, 16)
                sp.dma_start(bo[:], w["bo"].rearrange("(a n) -> a n", a=1).to_broadcast([P, D])).then_inc(const_in, 16)
            load(1, 1)
            sp.dma_start(pr[:, 0], consts["sel_causal" if causal else "sel"]).then_inc(sel_in, 16)
            if causal:
                sp.dma_start(pr[:, 1], consts["bias_tab"]).then_inc(table_in, 16)
                sp.dma_start(on_stage, consts["coarse_mask"]).then_inc(table_in, 16)

            def store_qk(g, par):
                for i, stored in enumerate((q_stored, k_stored)):
                    wait(sp, lo_done, lo_p(g, n_tr + i * HALVES + 1) + 1)
                    sp.dma_start(qk_dram[par, i].rearrange("a t p n -> p (a t) n"),
                                 qk[:, i].rearrange("p a t n -> p (a t) n").bitcast(FP32)).then_inc(stored, 16)

            BLOCKS = tuple(enumerate(((0, 0), (0, 1), (1, 0))))

            def load_q(par, half):
                heads = half * HEADS_HALF
                for block, (part, _) in BLOCKS:
                    for a in range(2):
                        row = block * PAIR + a * DK
                        src = qk_dram[par, 0, part, half].rearrange("(j a d) n -> a d j n", a=2, d=DK)[a]
                        sp.dma_start(qq[row:row + DK, heads + a:heads + HEADS_HALF:2, :].bitcast(FP32), src).then_inc(qk_loaded[half], 16)

            def load_k(par, half):
                pairs = slice(half * PAIRS // HALVES, (half + 1) * PAIRS // HALVES)
                for block, (_, part) in BLOCKS:
                    src = qk_dram[par, 1, part, half].rearrange("(j r) n -> r j n", r=PAIR)
                    sp.dma_start(kk[block * PAIR:(block + 1) * PAIR, pairs, :].bitcast(FP32), src).then_inc(qk_loaded[half], 16)

            sp.wait_ge(cleared, 2)
            store_qk(0, 0)
            sp.wait_ge(q_stored, 16)
            sp.wait_ge(k_stored, 16)
            for half in range(HALVES):
                load_q(0, half)
                load_k(0, half)

            def step(g, par):
                def store(gs, ps):
                    wait(sp, y_ready, gs + 1)
                    rows = bass.ds(gs * G, G)
                    for x_out in x_outs:
                        sp.dma_start(x_out[rows, :].rearrange("(b p) n -> p b n", p=P), y[:, ps]).then_inc(y_stored[ps], 16)
                if not (isinstance(g, int) and g >= groups - 2):
                    wait(sp, c_full, c_v(g, 1) + 1)
                    load(g + 2, par)
                if not is_last(g):
                    store_qk(g + 1, 1 - par)
                if not is_last(g):
                    wait(sp, b_full, b_oq(g, 0) + 1)
                    load_q(1 - par, 0)
                    wait(sp, b_full, b_oq(g, 1) + 1)
                    load_k(1 - par, 0)
                    wait(sp, b_full, b_oq(g, 2) + 1)
                    load_q(1 - par, 1)
                    load_k(1 - par, 1)
                if not is_first(g):
                    store(g - 1, 1 - par)
                if is_last(g):
                    store(g, par)
            steps(sp, step)
            for i in range(2):
                sp.wait_ge(y_stored[i], 16 * len(x_outs) * (groups // 2))

        CONST_N = 16 * (4 + (4 if kv_own else 0))

        @block.tensor
        def _(pe):
            pe.wait_ge(ident_in, 16)

            def c_begin(idx):
                wait(pe, c_done, idx - 1)

            def after_projection(g, i):
                pe.wait_ge(lo_done, lo_p(g, i) + 1)

            def transposes(g, par, src, loaded, first):
                pe.wait_ge(loaded[par], (g - par) * 8 + 16)
                for half in range(HALVES):
                    i = first + half
                    if i < HALVES and isinstance(g, int) and g == 1:
                        after_projection(0, n_proj - 2 + half)
                    elif i < HALVES and not is_first(g):
                        wait(pe, b_done, b_oq(g - 2, 2 + half) + 1)
                    elif i >= HALVES and (isinstance(g, int) and g < 2):
                        after_projection(g, half)
                    elif i >= HALVES:
                        pe.wait_ge(lo_done, lo_o(g - 2, half) + 1)
                    b = B[par_of(b_p, g, par, i)]
                    for n in range(NB):
                        last = nc.tensor.matmul(b[:, n * P:(n + 1) * P], src[:, par, n, half * P:(half + 1) * P],
                                                ident[:], start=True, stop=True, is_transpose=True)
                    last.then_inc(b_full, 1)

            def project_qk(g, par, which):
                for i, (src, wt) in which:
                    for half in range(HALVES):
                        place = n_tr + i * HALVES + half
                        needed = (HALVES - 1) if i == 0 else n_tr - 1
                        after_projection(g, max(needed, place - 2))
                        if i == 0 and not kv_own and not (isinstance(g, int) and g < 2):
                            pe.wait_ge(lo_done, lo_o(g - 2, half) + 1)
                        b = B[par_of(b_p, g, par, place)]
                        for t in range(HALVES):
                            last = matmul3(nc, b[:, :], wt, src, t == 0, t == HALVES - 1,
                                           lambda w_, a, t=t, half=half: w_[:, a, t, half * P:(half + 1) * P],
                                           lambda x_, a, t=t: x_[:, a, t, :])
                        last.then_inc(b_full, 1)

            def project_v(g, par):
                pe.wait_ge(xr_ready, g + 1)
                for i in range(2):
                    idx = c_v(g, i)
                    c_begin(idx)
                    b = C[(par_of(c_v, g, par, 0) + i) % 2]
                    for j in range(2):
                        n = 2 * i + j
                        for t in range(HALVES):
                            last = matmul3(nc, b[:, j * D:(j + 1) * D], cT, wv, t == 0, t == HALVES - 1,
                                           lambda x_, a, t=t, n=n: x_[:, a, t, n * P:(n + 1) * P],
                                           lambda w_, a, t=t: w_[:, a, t, :])
                    last.then_inc(c_full, 1)

            def score_max(g, par, heads):
                for h in heads:
                    half = h // HEADS_HALF
                    if h % HEADS_HALF == 0:
                        wait(pe, qk_loaded[half], (g + 1) * 16 * QK_LOADS)
                    if h < RING:
                        wait(pe, exp_done, g * H - RING + h + 1)
                    else:
                        wait(pe, max_done, g * H + h - RING + 1)
                    b = A[h % RING]
                    for n in range(NB):
                        cols = slice(n * P * 2 + 1, (n + 1) * P * 2, 2)
                        last = nc.tensor.matmul(b[:, n * P:(n + 1) * P],
                                                qq[:, h, :].bitcast(BF16)[:, cols],
                                                kk[:, h // 2, :].bitcast(BF16)[:, cols],
                                                start=(n == 0), stop=(n == NB - 1 and not causal), skip_group_check=True)
                    if causal:
                        last = nc.tensor.matmul(b[:, :], ident_b[:], bias_tab[:, h, :].unsqueeze(1).to_broadcast([P, NB, P]),
                                                start=False, stop=True, skip_group_check=True)
                    last.then_inc(a_full, 1)

            def maxima(g, par):
                c_begin(c_m(g))
                pe.wait_ge(m2_ready, g + 1)
                b = C[par_of(c_m, g, par)]
                for n in range(NB):
                    last = nc.tensor.matmul(b[0:2 * H, :].bitcast(BF16)[:, n * P:(n + 1) * P], m2[:, n, :], ident_b[:],
                                            start=True, stop=True, is_transpose=True)
                last.then_inc(c_full, 1)

            def scores(g, par, quad):
                for n in range(NB):
                    turn = 4 * quad + n
                    if turn == 0:
                        wait(pe, c_done, c_m(g) + 1)
                    if turn >= RING:
                        wait(pe, exp_done, g * H + turn - RING + 1)
                    b = A[turn % RING]
                    cols = slice(n * P, (n + 1) * P)
                    for j in range(4):
                        nc.tensor.matmul(b[:, j * P:(j + 1) * P], sel[:, 4 * quad + j, :], mT[:, cols],
                                         start=(j == 0), stop=False)
                    for j in range(2):
                        pair = 2 * quad + j
                        last = nc.tensor.matmul(b[:, j * 2 * P:(j + 1) * 2 * P].rearrange("p (j q) -> p j q", j=2),
                                                kk[:, pair, cols], qq[:, 2 * pair:2 * pair + 2, cols],
                                                start=False, stop=(j == 1))
                    last.then_inc(a_full, 1)

            def weigh(g, par, quad):
                if quad >= 2:
                    wait(pe, b_done, b_oq(g, quad - 2) + 1)
                elif is_last(g):
                    pe.wait_ge(lo_done, lo_o(g - 1, quad) + 1)
                else:
                    after_projection(g + 1, n_proj - 2 + quad)
                wait(pe, sel_done if causal else exp_done, g * H + 4 * quad + 4)
                if quad == 0:
                    wait(pe, c_done, c_v(g, 1) + 1)
                b = B[par_of(b_oq, g, par, quad)]
                for n in range(NB):
                    for j in range(4):
                        last = nc.tensor.matmul(b[32 * j:32 * j + VW, n * P:(n + 1) * P],
                                                v[:, n, 4 * quad + j, :],
                                                pr[:, quad % 2, n, j * P:(j + 1) * P], start=True, stop=True)
                last.then_inc(b_full, 1)

            def quad_back(g, par, quad):
                c_begin(c_quad(g, quad))
                wait(pe, b_done, b_oq(g, quad) + 1)
                b = C[par_of(c_quad, g, par, quad)]
                for n in range(NB):
                    last = nc.tensor.matmul(b[:, n * P:(n + 1) * P], oq[:, quad % 2, n * P:(n + 1) * P], ident[:],
                                            start=True, stop=True, is_transpose=True)
                last.then_inc(c_full, 1)

            def output_back(g, par):
                for half in range(HALVES):
                    if isinstance(g, int) and g >= groups - 2:
                        wait(pe, b_done, b_oq(g, 2 + half) + 1)
                    else:
                        after_projection(g + 2, half)
                    if half == 0:
                        wait(pe, c_done, c_quad(g, QUADS - 1) + 1)
                    b = B[par_of(b_ot, g, par, half)]
                    for n in range(NB):
                        last = nc.tensor.matmul(b[:, n * P:(n + 1) * P], on[:, n, half * P:(half + 1) * P], ident[:],
                                                start=True, stop=True, is_transpose=True)
                    last.then_inc(b_full, 1)

            def output(g, par):
                pe.wait_ge(lo_done, lo_o(g, 1) + 1)
                for i in range(2):
                    c_begin(c_out(g, i))
                    b = C[par_of(c_out, g, par, i)]
                    for j in range(2):
                        n = 2 * i + j
                        for t in range(HALVES):
                            last = matmul3(nc, b[:, j * D:(j + 1) * D], oT, wo, t == 0, t == HALVES - 1,
                                           lambda o_, a, t=t, n=n: o_[:, a, t, n * P:(n + 1) * P],
                                           lambda w_, a, t=t: w_[:, a, t, :])
                    last.then_inc(c_full, 1)

            transposes(0, 0, x, x_loaded, 0)
            if kv_own:
                transposes(0, 0, ctx, c_loaded, HALVES)
            pe.wait_ge(const_ready, 1)
            of_q, of_k = (0, (xT, wq)), (1, (cT, wk))
            project_qk(0, 0, (of_q, of_k))
            project_v(0, 0)
            pe.wait_ge(const_ready, 2)
            score_max(0, 0, range(0, H // 2))

            def step(g, par):
                more = not is_last(g)
                if more:
                    transposes(g + 1, 1 - par, x, x_loaded, 0)
                score_max(g, par, range(8, 10))
                if not is_first(g):
                    output_back(g - 1, 1 - par)
                score_max(g, par, range(10, 14))
                if not is_first(g):
                    output(g - 1, 1 - par)
                if more and kv_own:
                    transposes(g + 1, 1 - par, ctx, c_loaded, HALVES)
                score_max(g, par, range(14, H))
                if more:
                    project_qk(g + 1, 1 - par, (of_q,))
                maxima(g, par)
                if more:
                    project_qk(g + 1, 1 - par, (of_k,))
                scores(g, par, 0)
                for quad in range(1, QUADS):
                    scores(g, par, quad)
                    if quad <= 2 and more:
                        pe.wait_ge((q_stored, k_stored)[quad - 1], 16 * (g + 2))
                    weigh(g, par, quad - 1)
                    if quad >= 2:
                        quad_back(g, par, quad - 2)
                if more:
                    score_max(g + 1, 1 - par, range(0, 2))
                weigh(g, par, QUADS - 1)
                if more:
                    score_max(g + 1, 1 - par, range(2, 4))
                quad_back(g, par, QUADS - 2)
                if more:
                    score_max(g + 1, 1 - par, range(4, 6))
                    project_v(g + 1, 1 - par)
                    score_max(g + 1, 1 - par, range(6, 8))
                quad_back(g, par, QUADS - 1)
                if not more:
                    output_back(g, par)
                    output(g, par)
            steps(pe, step)

        @block.scalar
        def _(act):
            act.wait_ge(const_in, CONST_N)

            def copy_in(g, par, banks):
                for i in banks:
                    what = "x" if i < HALVES else "c" if i < n_tr else "q" if i < n_tr + HALVES else "k"
                    half = i % HALVES
                    b = B[par_of(b_p, g, par, i)][:, :]
                    act.wait_ge(b_full, b_p(g, i) + 1)
                    if what in "xc":
                        if not is_first(g):
                            wait(act, c_full, c_v(g - 1, 1) + 1)
                        ins = nc.scalar.copy((xT if what == "x" else cT)[:, 0, half, :], b)
                    elif what == "q":
                        wait(act, q_stored, g * 16)
                        ins = nc.scalar.activation(qk[:, 0, 0, half, :], b, ACT.Identity,
                                                   bias=bq[:, half:half + 1] if kv_own else 0.0,
                                                   scale=1.0 if kv_own else DK ** -0.5)
                    else:
                        wait(act, k_stored, g * 16)
                        ins = nc.scalar.activation(qk[:, 1, 0, half, :], b, ACT.Identity,
                                                   bias=bk[:, half:half + 1] if kv_own else 0.0)
                    ins.then_inc(b_done, 1)

            def exps(g, par, quad):
                if quad >= 2:
                    wait(act, b_full, b_oq(g, quad - 2) + 1)
                elif not is_first(g):
                    wait(act, b_full, b_oq(g - 1, quad + 2) + 1)
                for n in range(NB):
                    turn = 4 * quad + n
                    act.wait_ge(a_full, g * 2 * H + H + turn + 1)
                    nc.scalar.activation(pr[:, quad % 2, n, :], A[turn % RING][:, :], ACT.Exp).then_inc(exp_done, 1)

            def copy_quad(g, par, quad):
                act.wait_ge(b_full, b_oq(g, quad) + 1)
                if quad >= 2:
                    wait(act, c_full, c_quad(g, quad - 2) + 1)
                elif not is_first(g):
                    wait(act, c_full, c_quad(g - 1, quad + 2) + 1)
                b = B[par_of(b_oq, g, par, quad)]
                nc.scalar.copy(oq[:, quad % 2, :], b[:, :]).then_inc(b_done, 1)

            def copy_out(g, par):
                for half in range(HALVES):
                    act.wait_ge(b_full, b_ot(g, half) + 1)
                    if not is_first(g):
                        wait(act, c_full, c_out(g - 1, 1) + 1)
                    b = B[par_of(b_ot, g, par, half)]
                    nc.scalar.copy(oT[:, 0, half, :], b[:, :]).then_inc(b_done, 1)

            copy_in(0, 0, range(n_proj))

            def step(g, par):
                more = not is_last(g)
                if more:
                    copy_in(g + 1, 1 - par, range(HALVES))
                if not is_first(g):
                    copy_out(g - 1, 1 - par)
                if more:
                    copy_in(g + 1, 1 - par, range(HALVES, n_proj))
                exps(g, par, 0)
                for quad in range(1, QUADS):
                    exps(g, par, quad)
                    copy_quad(g, par, quad - 1)
                copy_quad(g, par, QUADS - 1)
                if not more:
                    copy_out(g, par)
            steps(act, step)

        @block.vector
        def _(dve):
            chain = {"n": 0, "base": 0}
            def link(ins):
                chain["n"] += 1
                ins.then_inc(dve_chain, 1)
                dve.wait_ge(dve_chain, chain["base"] + chain["n"])

            if not causal:
                nc.vector.memset(mT[:, :], 0.0)
            nc.vector.memset(scratch_v[0][:, :], 0.0)
            nc.vector.memset(scratch_p[0][:, :], 0.0).then_inc(scratch_ready, 1)
            dve.wait_ge(const_in, CONST_N)
            for i, wt in enumerate((wq, wk, wv, wo)):
                ins = nc.vector.tensor_copy(wt[:, 0], y_stage[:, i])
            link(ins)
            for i, wt in enumerate((wq, wk, wv, wo)):
                ins = nc.vector.tensor_tensor(wt[:, 1], y_stage[:, i], wt[:, 0].bitcast(FP32), ALU.subtract)
            ins.then_inc(const_ready, 1)
            START = chain["n"]

            def rest(g, par, i):
                idx = b_p(g, i)
                b = B[par_of(b_p, g, par, i)][:, :]
                half = i % HALVES
                what = "x" if i < HALVES else "c" if i < n_tr else "q" if i < n_tr + HALVES else "k"
                dve.wait_ge(b_done, idx + 1)
                if what in "xc":
                    t = xT if what == "x" else cT
                    ins = nc.vector.tensor_tensor(t[:, 1, half, :], b, t[:, 0, half, :].bitcast(FP32), ALU.subtract)
                elif what == "q":
                    out, hi = qk[:, 0, 1, half, :], qk[:, 0, 0, half, :].bitcast(FP32)
                    if kv_own:
                        ins = nc.vector.scalar_tensor_tensor(out, b, bq[:, half:half + 1], hi, ALU.add, ALU.subtract)
                    else:
                        ins = nc.vector.scalar_tensor_tensor(out, b, DK ** -0.5, hi, ALU.mult, ALU.subtract)
                else:
                    out, hi = qk[:, 1, 1, half, :], qk[:, 1, 0, half, :].bitcast(FP32)
                    if kv_own:
                        ins = nc.vector.scalar_tensor_tensor(out, b, bk[:, half:half + 1], hi, ALU.add, ALU.subtract)
                    else:
                        ins = nc.vector.tensor_tensor(out, b, hi, ALU.subtract)
                ins.then_inc(lo_done, 1)

            def rest_o(g, par, half):
                dve.wait_ge(b_done, b_ot(g, half) + 1)
                b = B[par_of(b_ot, g, par, half)]
                nc.vector.tensor_tensor(oT[:, 1, half, :], b[:, :], oT[:, 0, half, :].bitcast(FP32),
                                        ALU.subtract).then_inc(lo_done, 1)

            def take_v(g, par):
                for i in range(2):
                    dve.wait_ge(c_full, c_v(g, i) + 1)
                    if not is_first(g):
                        wait(dve, b_full, b_oq(g - 1, QUADS - 1) + 1)
                    b = C[(par_of(c_v, g, par, 0) + i) % 2]
                    out = v[:, 2 * i:2 * i + 2, :, 0:DK]
                    src = b[:, :].rearrange("p (n h d) -> p n h d", n=2, h=H)
                    if kv_own:
                        ins = nc.vector.tensor_tensor(
                            out, src, bv[:, :].rearrange("p (h d) -> p h d", h=H).unsqueeze(1).to_broadcast([P, 2, H, DK]), ALU.add)
                    else:
                        ins = nc.vector.tensor_copy(out, src)
                    ins.then_inc(c_done, 1)

            def maxes(g, par, heads):
                for h in heads:
                    dve.wait_ge(a_full, g * 2 * H + h + 1)
                    nc.vector.tensor_reduce(mx[:, :, h], A[h % RING][:, :].rearrange("p (n k) -> p n k", n=NB), AX,
                                            ALU.max).then_inc(max_done, 1)

            def split_max(g, par):
                dve.wait_ge(max_done, (g + 1) * H)
                if not is_first(g):
                    dve.wait_ge(c_full, c_m(g - 1) + 1)
                link(nc.vector.tensor_copy(m2[:, :, 0:H], mx[:, :, :]))
                nc.vector.tensor_tensor(m2[:, :, H:2 * H], mx[:, :, :], m2[:, :, 0:H], ALU.subtract).then_inc(m2_ready, 1)

            def take_max(g, par):
                dve.wait_ge(c_full, c_m(g) + 1)
                b = C[par_of(c_m, g, par)]
                nc.vector.tensor_copy(mT[0:2 * H, :], b[0:2 * H, :].bitcast(BF16)[:, 0:G]).then_inc(c_done, 1)

            def normalise_quad(g, par, quad):
                dve.wait_ge(c_full, c_quad(g, quad) + 1)
                b = C[par_of(c_quad, g, par, quad)][:, :].rearrange("p (n j d) -> p n j d", n=NB, j=4)
                wait(dve, c_done, c_quad(g, quad))
                link(nc.vector.reciprocal(rden[:, :, :], b[:, :, :, DK]))
                if quad == 0 and not is_first(g):
                    dve.wait_ge(b_full, b_ot(g - 1, 1) + 1)
                out = on[:, :, quad * 4 * DK:(quad + 1) * 4 * DK].rearrange("p n (j d) -> p n j d", j=4)
                nc.vector.tensor_tensor(out, b[:, :, :, 0:DK], rden[:, :, :].unsqueeze(3).to_broadcast([P, NB, 4, DK]),
                                        ALU.mult).then_inc(c_done, 1)

            def residual(g, par):
                for i in range(2):
                    dve.wait_ge(c_full, c_out(g, i) + 1)
                    if i == 0:
                        dve.wait_ge(xr_ready, g + 1)
                        if not (isinstance(g, int) and g < 2):
                            dve.wait_ge(y_stored[par], (g - par) * (8 * len(x_outs)))
                    b = C[par_of(c_out, g, par, i)]
                    nc.vector.tensor_tensor(y[:, par, 2 * i:2 * i + 2, :].rearrange("p n d -> p (n d)"), b[:, :],
                                            xr[:, par, 2 * i:2 * i + 2, :].rearrange("p n d -> p (n d)"),
                                            ALU.add).then_inc(c_done, 1)

            def layernorm_stats(g, par):
                dve.wait_ge(c_done, c_out(g, 1) + 1)
                for n in range(NB):
                    ins = nc.vector.bn_stats(stats[:, n, :], y[:, par, n, :])
                ins.then_inc(dve_chain, 1)
                chain["n"] += 1
                waits = [(dve_chain, chain["base"] + chain["n"])]
                if not is_first(g):
                    waits.append((rstd_done, g))
                wait_apart(nc.vector, scratch_v, *waits)
                for n in range(NB):
                    ins = nc.vector.bn_aggr(mv[:, n, :], stats[:, n, :])
                ins.then_inc(stats_done, 1)

            def layernorm_apply(g, par):
                dve.wait_ge(stats_done, g + 1)
                dve.wait_ge(rstd_done, g + 1)
                for n in range(NB):
                    ins = nc.vector.tensor_scalar(y[:, par, n, :], y[:, par, n, :], mv[:, n, 0:1], rstd[:, n:n + 1],
                                                  ALU.subtract, ALU.mult)
                ins.then_inc(y_ready, 1)

            for i in range(n_proj):
                rest(0, 0, i)
            nc.vector.memset(v[:, :, :, DK + 1:VW], 0.0)
            nc.vector.memset(v[:, :, :, DK:DK + 1], 1.0)
            dve.wait_ge(ident_in, 16)
            nc.vector.tensor_copy(ident_b[:], ident[:])
            dve.wait_ge(sel_in, 16)
            if causal:
                dve.wait_ge(table_in, 32)
                nc.vector.tensor_copy(mT[:, :], on_stage)
                nc.vector.tensor_copy(bias_tab[:].rearrange("p h k -> p (h k)"),
                                      pr[:, 1].rearrange("p a b -> p (a b)"))
            nc.vector.tensor_copy(sel[:].rearrange("p h k -> p (h k)"),
                                  pr[:, 0].rearrange("p a b -> p (a b)")).then_inc(const_ready, 1)
            take_v(0, 0)
            maxes(0, 0, range(0, H // 2))

            def step(g, par):
                first = is_first(g)
                last = is_last(g)
                links = 1 + QUADS + 1
                chain["base"], chain["n"] = START + g * links - (0 if first else 1), 0
                if not last:
                    for i in range(HALVES):
                        rest(g + 1, 1 - par, i)
                maxes(g, par, range(8, 10))
                if not first:
                    for half in range(HALVES):
                        rest_o(g - 1, 1 - par, half)
                maxes(g, par, range(10, 14))
                if not first:
                    residual(g - 1, 1 - par)
                if not last and kv_own:
                    for i in range(HALVES, n_tr):
                        rest(g + 1, 1 - par, i)
                maxes(g, par, range(14, H))
                split_max(g, par)
                if not last:
                    for i in range(n_tr, n_tr + HALVES):
                        rest(g + 1, 1 - par, i)
                take_max(g, par)
                if not last:
                    for i in range(n_tr + HALVES, n_proj):
                        rest(g + 1, 1 - par, i)
                if not first:
                    layernorm_stats(g - 1, 1 - par)
                normalise_quad(g, par, 0)
                if not first:
                    layernorm_apply(g - 1, 1 - par)
                normalise_quad(g, par, 1)
                if not last:
                    maxes(g + 1, 1 - par, range(0, 4))
                normalise_quad(g, par, QUADS - 2)
                if not last:
                    maxes(g + 1, 1 - par, range(4, 6))
                    take_v(g + 1, 1 - par)
                    maxes(g + 1, 1 - par, range(6, 8))
                normalise_quad(g, par, QUADS - 1)
                if last:
                    for half in range(HALVES):
                        rest_o(g, par, half)
                    residual(g, par)
                    layernorm_stats(g, par)
                    layernorm_apply(g, par)
            steps(dve, step)

        @block.gpsimd
        def _(pool):
            nc.gpsimd.memset(kk[EXTRA:P, :, :].bitcast(FP32), 0.0).then_inc(cleared, 1)
            pool.wait_ge(cleared, 1)
            nc.gpsimd.memset(qq[:, :, :].bitcast(FP32), 0.0).then_inc(cleared, 1)
            pool.wait_ge(const_in, CONST_N)
            pool.wait_ge(scratch_ready, 1)
            nc.gpsimd.memset(minus_half[:, :], -0.5).then_inc(pool_chain, 1)
            pool.wait_ge(pool_chain, 1)

            def clear_future(g, par, heads):
                for h in heads:
                    wait_apart(nc.gpsimd, scratch_p, (exp_done, g * H + h + 1))
                    t = pr[:, (h // 4) % 2, h % 4, :].rearrange("p (n k) -> p n k", n=NB)
                    nc.gpsimd.affine_select(out=t, in_=t, compare_op=ALU.is_ge, fill=0.0, base=0,
                                            pattern=[[0, NB], [1, P]], channel_multiplier=-1).then_inc(sel_done, 1)

            def keep_residual(g, par):
                waits = [(x_loaded[par], (g - par) * 8 + 16)]
                if not (isinstance(g, int) and g < 2):
                    waits.append((c_done, c_out(g - 2, 1) + 1))
                wait_apart(nc.gpsimd, scratch_p, *waits)
                if kv_own:
                    ins = nc.gpsimd.tensor_tensor(xr[:, par], x[:, par], bo[:, :].unsqueeze(1).to_broadcast([P, NB, D]), ALU.add)
                else:
                    ins = nc.gpsimd.tensor_copy(xr[:, par], x[:, par])
                ins.then_inc(xr_ready, 1)

            def inverse_deviation(g):
                waits = [(stats_done, g + 1)]
                if not is_first(g):
                    waits.append((y_ready, g))
                wait_apart(nc.gpsimd, scratch_p, *waits)
                nc.gpsimd.tensor_scalar(rstd[:, :], mv[:, :, 1], EPS, None, ALU.add).then_inc(pool_chain, 1)
                pool.wait_ge(pool_chain, g + 2)
                nc.gpsimd.tensor_tensor(rstd[:, :], rstd[:, :], minus_half[:, :], ALU.pow).then_inc(rstd_done, 1)

            keep_residual(0, 0)

            def step(g, par):
                last = is_last(g)
                if not last:
                    keep_residual(g + 1, 1 - par)
                if causal:
                    clear_future(g, par, range(0, 4))
                if not is_first(g):
                    inverse_deviation(g - 1)
                if causal:
                    clear_future(g, par, range(4, H))
                if last:
                    inverse_deviation(g)
            steps(pool, step)

I32 = mybir.dt.int32
E = 8
HID = 1024
HT = HID // P
BITS = 30
BITS_TURN = 5


def logits_block(nc, tiles, rows_dram, sum_dram, wr_dram, br_dram, ident_dram, logits):
    groups = tiles // NB
    LOADS = 4
    with ExitStack() as c:
        ident = c.enter_context(nc.sbuf_tensor("lg_ident", [P, P], FP32))
        wr = c.enter_context(nc.sbuf_tensor("lg_wr", [P, HALVES, E], FP32))
        br = c.enter_context(nc.sbuf_tensor("lg_br", [E, 1], FP32))
        zero = c.enter_context(nc.sbuf_tensor("lg_zero", [P, D + E], FP32))
        x2 = c.enter_context(nc.sbuf_tensor("lg_x2", [P, LOADS, NB, D], FP32))
        xT = c.enter_context(nc.sbuf_tensor("lg_xT", [P, 2, HALVES, G], FP32))
        lT = c.enter_context(nc.sbuf_tensor("lg_lT", [E, 2, G], FP32))
        tb = [c.enter_context(nc.psum_tensor(f"lg_T{i}", [P, G], FP32)) for i in range(4)]
        lb = [c.enter_context(nc.psum_tensor(f"lg_L{i}", [E, G], FP32)) for i in range(2)]
        bb = [c.enter_context(nc.psum_tensor(f"lg_B{i}", [P, NB, E], FP32)) for i in range(2)]
        const_in = c.enter_context(nc.semaphore("lg_const_in"))
        x_loaded = [c.enter_context(nc.semaphore(f"lg_x_loaded{i}")) for i in range(LOADS)]
        zero_made = c.enter_context(nc.semaphore("lg_zero_made"))
        zeroed = c.enter_context(nc.semaphore("lg_zeroed"))
        t_full = c.enter_context(nc.semaphore("lg_t_full"))
        a_copied = c.enter_context(nc.semaphore("lg_a_copied"))
        d_copied = c.enter_context(nc.semaphore("lg_d_copied"))
        l_full = c.enter_context(nc.semaphore("lg_l_full"))
        l_done = c.enter_context(nc.semaphore("lg_l_done"))
        b_full = c.enter_context(nc.semaphore("lg_b_full"))
        b_done = c.enter_context(nc.semaphore("lg_b_done"))
        block = c.enter_context(nc.Block())

        @block.sync
        def _(sp):
            sp.dma_start(ident[:], ident_dram).then_inc(const_in, 16)
            sp.dma_start(wr[:], wr_dram.rearrange("(t p) n -> p t n", p=P)).then_inc(const_in, 16)
            sp.dma_start(br[:], br_dram.rearrange("(p a) -> p a", a=1)).then_inc(const_in, 16)
            for g in range(groups):
                if g >= LOADS:
                    sp.wait_ge(t_full, g - LOADS + 1)
                sp.dma_start(x2[:, g % LOADS], rows_dram[g * G:(g + 1) * G, 0:D]
                             .rearrange("(b p) n -> p b n", p=P)).then_inc(x_loaded[g % LOADS], 16)
            sp.wait_ge(zero_made, 1)
            sp.dma_start(rows_dram[groups * G:groups * G + P, :], zero[:]).then_inc(zeroed, 16)
            sp.dma_start(sum_dram[groups * G:groups * G + P, :], zero[:, 0:D]).then_inc(zeroed, 16)
            sp.wait_ge(zeroed, 32)

        @block.tensor
        def _(pe):
            pe.wait_ge(const_in, 48)

            def logits_of(g):
                pe.wait_ge(a_copied, g + 1)
                pe.wait_ge(d_copied, g + 1)
                if g >= 2:
                    pe.wait_ge(l_done, g - 1)
                for t in range(HALVES):
                    last = nc.tensor.matmul(lb[g % 2][:, :], wr[:, t, :], xT[:, g % 2, t, :],
                                            start=(t == 0), stop=(t == HALVES - 1))
                last.then_inc(l_full, 1)

            def back(g):
                pe.wait_ge(l_done, g + 1)
                if g >= 2:
                    pe.wait_ge(b_done, g - 1)
                for n in range(NB):
                    last = nc.tensor.matmul(bb[g % 2][:, n, :], lT[:, g % 2, n * P:(n + 1) * P], ident[0:E, 0:E],
                                            start=True, stop=True, is_transpose=True)
                last.then_inc(b_full, 1)

            for g in range(groups):
                pe.wait_ge(x_loaded[g % LOADS], 16 * (g // LOADS + 1))
                if g >= 2:
                    pe.wait_ge(a_copied, g - 1)
                    pe.wait_ge(d_copied, g - 1)
                for half in range(HALVES):
                    for n in range(NB):
                        last = nc.tensor.matmul(tb[2 * (g % 2) + half][:, n * P:(n + 1) * P],
                                                x2[:, g % LOADS, n, half * P:(half + 1) * P], ident[:],
                                                start=True, stop=True, is_transpose=True)
                last.then_inc(t_full, 1)
                if g >= 1:
                    logits_of(g - 1)
                if g >= 2:
                    back(g - 2)
            logits_of(groups - 1)
            back(groups - 2)
            back(groups - 1)

        @block.scalar
        def _(act):
            def take(g):
                act.wait_ge(b_full, g + 1)
                nc.scalar.copy(logits[:, g * NB:(g + 1) * NB, :], bb[g % 2][:, :, :]).then_inc(b_done, 1)
            for g in range(groups):
                act.wait_ge(t_full, g + 1)
                if g >= 2:
                    act.wait_ge(l_full, g - 1)
                nc.scalar.copy(xT[:, g % 2, 0, :], tb[2 * (g % 2)][:, :]).then_inc(a_copied, 1)
                if g >= 2:
                    take(g - 2)
            take(groups - 2)
            take(groups - 1)

        @block.vector
        def _(dve):
            def add_bias(g):
                dve.wait_ge(l_full, g + 1)
                if g >= 2:
                    dve.wait_ge(b_full, g - 1)
                nc.vector.tensor_scalar(lT[:, g % 2, :], lb[g % 2][:, :], br[:, 0:1], None, ALU.add).then_inc(l_done, 1)
            nc.vector.memset(zero[:], 0.0).then_inc(zero_made, 1)
            dve.wait_ge(const_in, 48)
            for g in range(groups):
                dve.wait_ge(t_full, g + 1)
                if g >= 2:
                    dve.wait_ge(l_full, g - 1)
                nc.vector.tensor_copy(xT[:, g % 2, 1, :], tb[2 * (g % 2) + 1][:, :]).then_inc(d_copied, 1)
                if g >= 1:
                    add_bias(g - 1)
            add_bias(groups - 1)


def route_block(nc, tiles, cap, logits, rows_dram, ids_dram, consts):
    LT = -(-cap // P)
    ROWS = E * LT
    dump = ROWS * P
    BATCH = 16
    Q = 2 * tiles
    CH = P // E
    F = tiles * P // CH
    TJ = F // P
    with ExitStack() as c:
        def sb(name, shape, dt=FP32):
            return c.enter_context(nc.sbuf_tensor("rt_" + name, shape, dt))

        def sem(name):
            return c.enter_context(nc.semaphore("rt_" + name))

        pr = sb("probs", [P, tiles, E])
        eq = sb("eq", [P, tiles, E])
        cand = sb("cand", [P, tiles, E])
        first = sb("first", [P, tiles, E])
        second = sb("second", [P, tiles, E])
        gm = sb("gm", [P, tiles, E])
        runs = sb("runs", [P, TJ, E, CH])
        st = sb("slot_t", [P, tiles, E])
        col = sb("col", [P, tiles])
        col2 = sb("col2", [P, tiles])
        ident = sb("ident", [P, P])
        same = sb("same", [P, P])
        before = sb("before", [P, P])
        ebase = sb("ebase", [P, 1])
        iota8 = sb("iota8", [P, E])
        gt = sb("gt", [P, F])
        above = sb("above", [P, F])
        equal = sb("equal", [P, F])
        ones = sb("ones", [P, F])
        sc_a = sb("sc_a", [P, F])
        sc_e = sb("sc_e", [P, F])
        junk = sb("junk", [P, F])
        thr = sb("thr", [P, 1], I32)
        tried = sb("tried", [P, 1], I32)
        next_bit = sb("next_bit", [P, 1], I32)
        bit = sb("bit", [P, 1], I32)
        off_bit = sb("off_bit", [P, 1], I32)
        cnt = sb("cnt", [P, 1])
        tot = sb("tot", [P, 2])
        off = sb("off", [P, 2])
        need = sb("need", [P, 1])
        gates = sb("gates", [P, 2, tiles])
        gate_rows = sb("gate_rows", [P, tiles, E])
        slots = sb("slots", [P, Q], I32)
        places = sb("places", [P, 2, Q], I32)
        lane_b = sb("lane_b", [P, Q], BF16)
        row_b = sb("row_b", [P, Q], BF16)
        iota_row = sb("iota_row", [P, P])
        iota_b = sb("iota_b", [P, P], BF16)
        tile_b = sb("tile_b", [P, tiles], BF16)
        lane = sb("lane", [P, 1])
        dummy = sb("dummy", [P, 1])
        hit_lane = sb("hit_lane", [P, Q, P], BF16)
        hit_row = sb("hit_row", [P, Q, ROWS], BF16)
        tagged = sb("tagged", [P, Q, 2, ROWS], BF16)
        id_parts = sb("id_parts", [P, 2, ROWS])
        empty = sb("empty", [P, ROWS])
        ids = sb("ids", [P, ROWS], I32)
        bi = c.enter_context(nc.psum_tensor("rt_I", [P, 2, ROWS], FP32))
        bt = c.enter_context(nc.psum_tensor("rt_T", [P, G], FP32))
        bc = c.enter_context(nc.psum_tensor("rt_C", [P, 8], FP32))
        const_in, dve_done, pe_done, act_done, counted, total = (
            sem(n) for n in ("const_in", "dve_done", "pe_done", "act_done", "counted", "total"))
        gates_stored, gates_made, ids_made, ids_stored = (
            sem(n) for n in ("gates_stored", "gates_made", "ids_made", "ids_stored"))
        lanes_hit = sem("lanes_hit")
        rows_hit = sem("rows_hit")
        lane_tagged = sem("lane_tagged")
        tile_tagged = sem("tile_tagged")
        routed = sem("routed")
        block = c.enter_context(nc.Block())

        @block.sync
        def _(sp):
            for dst, name in ((ident, "ident"), (same, "same_expert"), (before, "before"), (ebase, "ebase"), (iota8, "iota8"),
                              (iota_row, "iota_row"), (lane, "lane"), (dummy, "dummy_row")):
                sp.dma_start(dst[:], consts[name]).then_inc(const_in, 16)
            sp.wait_ge(gates_made, 1)
            sp.dma_start(rows_dram[0:tiles * P, D:D + E].rearrange("(t p) e -> p t e", p=P), gate_rows[:]).then_inc(gates_stored, 16)
            sp.wait_ge(ids_made, 1)
            sp.dma_start(ids_dram.rearrange("e p b -> p e b"), ids[:].rearrange("p (e b) -> p e b", e=E)).then_inc(ids_stored, 16)
            sp.wait_ge(gates_stored, 16)
            sp.wait_ge(ids_stored, 16)

        @block.scalar
        def _(act):
            act.wait_ge(routed, 1)
            nc.scalar.activation(pr[:, :, :], pr[:, :, :], ACT.Exp).then_inc(act_done, 1)
            for b in range(Q // BATCH):
                act.wait_ge(rows_hit, b + 1)
                qs = slice(b * BATCH, (b + 1) * BATCH)
                nc.scalar.activation(tagged[:, qs, 0, :], hit_row[:, qs, :], ACT.Copy, scale=lane[:, 0:1]).then_inc(lane_tagged, 1)

        @block.tensor
        def _(pe):
            pe.wait_ge(const_in, 128)
            pe.wait_ge(routed, 2)
            for j in range(TJ):
                last = nc.tensor.matmul(bt[:, j * P:(j + 1) * P], runs[:, j, :, :].rearrange("p e c -> p (e c)"),
                                        ident[:], start=True, stop=True, is_transpose=True)
            last.then_inc(pe_done, 1)
            with pe.Fori(0, BITS // BITS_TURN) as turn:
                for k in range(BITS_TURN):
                    pe.wait_ge(counted, turn * BITS_TURN + (k + 1))
                    nc.tensor.matmul(bc[:, 0:1], same[:], cnt[:], start=True, stop=True).then_inc(total, 1)
            pe.wait_ge(routed, 3)
            nc.tensor.matmul(bc[:, 2:4], before[:], tot[:], start=True, stop=True)
            nc.tensor.matmul(bc[:, 4:6], same[:], tot[:], start=True, stop=True).then_inc(pe_done, 1)
            pe.wait_ge(routed, 4)
            for j in range(TJ):
                last = nc.tensor.matmul(bt[:, j * P:(j + 1) * P], gt[:, j * P:(j + 1) * P], ident[:],
                                        start=True, stop=True, is_transpose=True)
            last.then_inc(pe_done, 1)
            for b in range(Q // BATCH):
                pe.wait_ge(lanes_hit, b + 1)
                pe.wait_ge(lane_tagged, b + 1)
                pe.wait_ge(tile_tagged, b + 1)
                for q in range(b * BATCH, (b + 1) * BATCH):
                    last = nc.tensor.matmul(bi[:, :, :].rearrange("p a r -> p (a r)"), hit_lane[:, q, :],
                                            tagged[:, q, :, :].rearrange("p a r -> p (a r)"),
                                            start=(q == 0), stop=(q == Q - 1))
            last.then_inc(pe_done, 1)

        @block.vector
        def _(dve):
            n = [0]

            def link(ins):
                n[0] += 1
                ins.then_inc(dve_done, 1)
                dve.wait_ge(dve_done, n[0])

            def wide(a):
                return a.unsqueeze(2).to_broadcast([P, tiles, E])

            v = nc.vector
            v.memset(ones[:], 1.0)
            v.memset(thr[:], 1 << (BITS - 1))
            link(v.memset(bit[:], 1 << (BITS - 1)))
            link(v.tensor_reduce(col[:], logits[:], AX, ALU.max))
            v.tensor_tensor(pr[:], logits[:], wide(col[:]), ALU.subtract).then_inc(routed, 1)
            dve.wait_ge(act_done, 1)
            link(v.tensor_reduce(col2[:], pr[:], AX, ALU.add))
            link(v.reciprocal(col[:], col2[:]))
            link(v.tensor_tensor(pr[:], pr[:], wide(col[:]), ALU.mult))
            dve.wait_ge(const_in, 128)
            link(v.tensor_reduce(gates[:, 0, :], pr[:], AX, ALU.max))
            lower = iota8[:].unsqueeze(1).to_broadcast([P, tiles, E])
            for kth, chosen in enumerate((first, second)):
                src = pr if kth == 0 else gm
                link(v.tensor_tensor(eq[:], src[:], wide(gates[:, kth, :]), ALU.is_equal))
                link(v.tensor_tensor(cand[:], eq[:], lower, ALU.mult))
                link(v.tensor_reduce(col[:], cand[:], AX, ALU.min))
                link(v.tensor_tensor(chosen[:], cand[:], wide(col[:]), ALU.is_equal))
                if kth == 0:
                    link(v.scalar_tensor_tensor(gm[:], chosen[:], -2.0, pr[:], ALU.mult, ALU.add))
                    link(v.tensor_reduce(gates[:, 1, :], gm[:], AX, ALU.max))
            link(v.tensor_tensor(eq[:], first[:], second[:], ALU.add))
            link(v.tensor_tensor(cand[:], pr[:], eq[:], ALU.mult))
            v.tensor_copy(gate_rows[:], cand[:]).then_inc(gates_made, 1)
            by_run = "p (c j) e -> p j e c"
            for j in range(TJ):
                ins = v.scalar_tensor_tensor(runs[:, j], eq[:].rearrange(by_run, j=TJ)[:, j], -1.0,
                                             cand[:].rearrange(by_run, j=TJ)[:, j], ALU.add, ALU.add)
            ins.then_inc(routed, 1)
            dve.wait_ge(pe_done, 1)
            link(v.tensor_copy(gt[:], bt[:]))
            base = n[0]
            def try_bit(i):
                v.tensor_scalar(junk[:], gt[:], thr[:].bitcast(FP32), 0.0, ALU.is_ge, ALU.add,
                                accum_out=cnt[:]).then_inc(counted, 1)
                v.tensor_scalar(next_bit[:], bit[:], 1, None, ALU.logical_shift_right).then_inc(dve_done, 1)
                dve.wait_ge(dve_done, i * 4 + (base + 1))
                v.tensor_tensor(tried[:], thr[:], next_bit[:], ALU.bitwise_or).then_inc(dve_done, 1)
                dve.wait_ge(total, i + 1)
                v.tensor_scalar(off_bit[:], bc[:, 0:1], float(cap), bit[:, 0:1], ALU.is_lt, ALU.mult).then_inc(dve_done, 1)
                dve.wait_ge(dve_done, i * 4 + (base + 3))
                v.tensor_copy(bit[:], next_bit[:])
                v.tensor_tensor(thr[:], tried[:], off_bit[:], ALU.bitwise_xor).then_inc(dve_done, 1)
                dve.wait_ge(dve_done, i * 4 + (base + 4))
            with dve.Fori(0, BITS // BITS_TURN) as turn:
                for k in range(BITS_TURN):
                    try_bit(turn * BITS_TURN + k)
            n[0] = base + 4 * BITS
            dve.wait_ge(counted, BITS)
            t = thr[:].bitcast(FP32)
            link(v.tensor_scalar(above[:], gt[:], t, None, ALU.is_gt))
            link(v.tensor_scalar(equal[:], gt[:], t, None, ALU.is_equal))
            link(v.tensor_tensor_scan(sc_a[:], ones[:], above[:], 0.0, ALU.mult, ALU.add))
            link(v.tensor_tensor_scan(sc_e[:], ones[:], equal[:], 0.0, ALU.mult, ALU.add))
            v.tensor_copy(tot[:, 0:1], sc_a[:, F - 1:F])
            link(v.tensor_copy(tot[:, 1:2], sc_e[:, F - 1:F]))
            v.memset(junk[:, 0:1], 0.0).then_inc(routed, 1)
            dve.wait_ge(pe_done, 2)
            link(v.tensor_copy(off[:], bc[:, 2:4]))
            link(v.tensor_scalar(need[:], bc[:, 4:5], -1.0, float(cap), ALU.mult, ALU.add))
            link(v.scalar_tensor_tensor(sc_e[:], sc_e[:], off[:, 1:2], equal[:], ALU.add, ALU.subtract))
            link(v.scalar_tensor_tensor(sc_a[:], sc_a[:], off[:, 0:1], above[:], ALU.add, ALU.subtract))
            link(v.scalar_tensor_tensor(equal[:], sc_e[:], need[:, 0:1], equal[:], ALU.is_lt, ALU.mult))
            link(v.scalar_tensor_tensor(sc_a[:], sc_e[:], need[:, 0:1], sc_a[:], ALU.min, ALU.add))
            link(v.tensor_tensor(equal[:], equal[:], above[:], ALU.add))
            v.scalar_tensor_tensor(gt[:], sc_a[:], ebase[:, 0:1], equal[:], ALU.add, ALU.mult).then_inc(routed, 1)
            dve.wait_ge(pe_done, 3)
            for j in range(TJ):
                ins = v.tensor_copy(st[:].rearrange(by_run, j=TJ)[:, j], bt[:].rearrange("p (j e c) -> p j e c", j=TJ, e=E)[:, j])
            link(ins)
            for kth, chosen in enumerate((first, second)):
                link(v.tensor_tensor(cand[:], chosen[:], st[:], ALU.mult))
                link(v.tensor_reduce(col[:], cand[:], AX, ALU.add))
                link(v.tensor_scalar(slots[:, kth * tiles:(kth + 1) * tiles], col[:], float(dump), None, ALU.add))
            v.tensor_scalar(places[:, 0, :], slots[:], P - 1, None, ALU.bitwise_and)
            v.tensor_copy(iota_b[:], iota_row[:])
            v.tensor_scalar(tile_b[:], iota_row[:, 0:tiles], 1.0, None, ALU.add)
            link(v.tensor_scalar(places[:, 1, :], slots[:], P.bit_length() - 1, None, ALU.logical_shift_right))
            v.tensor_copy(lane_b[:], places[:, 0, :])
            link(v.tensor_copy(row_b[:], places[:, 1, :]))
            v.memset(junk[:, 0:1], 0.0).then_inc(routed, 1)
            for b in range(Q // BATCH):
                qs = slice(b * BATCH, (b + 1) * BATCH)
                for out, mine, width, ready in ((hit_row, row_b, ROWS, rows_hit), (hit_lane, lane_b, P, lanes_hit)):
                    v.tensor_tensor(out[:, qs, :], mine[:, qs].unsqueeze(2).to_broadcast([P, BATCH, width]),
                                    iota_b[:, 0:width].unsqueeze(1).to_broadcast([P, BATCH, width]),
                                    ALU.is_equal).then_inc(ready, 1)
            dve.wait_ge(pe_done, 4)
            link(v.tensor_copy(id_parts[:], bi[:]))
            link(v.tensor_scalar(empty[:], id_parts[:, 1, :], 0.0, dummy[:, 0:1], ALU.is_equal, ALU.mult))
            link(v.scalar_tensor_tensor(id_parts[:, 0, :], id_parts[:, 1, :], float(P), id_parts[:, 0, :], ALU.mult, ALU.add))
            v.scalar_tensor_tensor(ids[:], id_parts[:, 0, :], -float(P), empty[:], ALU.add, ALU.add).then_inc(ids_made, 1)

        @block.gpsimd
        def _(pool):
            pool.wait_ge(routed, 5)
            for b in range(Q // BATCH):
                pool.wait_ge(rows_hit, b + 1)
                qs = slice(b * BATCH, (b + 1) * BATCH)
                t0 = b * BATCH % tiles
                nc.gpsimd.tensor_tensor(tagged[:, qs, 1, :], hit_row[:, qs, :],
                                        tile_b[:, t0:t0 + BATCH].unsqueeze(2).to_broadcast([P, BATCH, ROWS]),
                                        ALU.mult).then_inc(tile_tagged, 1)


def experts_block(nc, cap, rows_dram, ids_dram, sum_dram, w, consts):
    LT = -(-cap // P)
    NC = 3
    used = cap + cap % 2
    parts = [LT // NC] * (NC - 1) + [LT - (NC - 1) * (LT // NC)]
    starts = [sum(parts[:c]) for c in range(NC)]
    widths = [min(used, (starts[c] + parts[c]) * P) - starts[c] * P for c in range(NC)]
    tiles_of = [[(o, min(P, n - o)) for o in range(0, n, P)] for n in widths]
    W = max(widths)
    UP = 4
    HR = 4
    assert LT % 2 == 0 and W <= G
    with ExitStack() as c:
        def sb(name, shape, dt=FP32):
            return c.enter_context(nc.sbuf_tensor("ex_" + name, shape, dt))

        def sem(name):
            return c.enter_context(nc.semaphore("ex_" + name))

        w1 = sb("w1", [P, 2, 2, HALVES, HID], FP32R)
        w2 = sb("w2", [P, 2, 2, HT, D], FP32R)
        w1_in = sb("w1_in", [P, HALVES, HID])
        w2_in = sb("w2_in", [P, HT, D])
        b1 = sb("b1", [P, 2, HT])
        b2 = sb("b2", [P, 2, D])
        mask = sb("mask", [P, 2, E])
        ids = sb("ids", [P, 2, LT], I32)
        out_ids = sb("out_ids", [P, 2, NC, NB], I32)
        xg = sb("xg", [P, 2, NB, D + E])
        xT = sb("xT", [P, 2, 2, HALVES, W], FP32R)
        h = sb("h", [P, HR, W])
        hT = sb("hT", [P, 2, 2, HT, W], FP32R)
        chosen = sb("chosen", [P, NB, E])
        gate = sb("gate", [P, NC, NB])
        raw = sb("raw", [P, NB, D])
        o = sb("o", [P, 2, NB, D])
        ident = sb("ident", [P, P])
        scratch_p = (sb("scratch_p", [P, 65]), [0])
        T = [c.enter_context(nc.psum_tensor(f"ex_T{i}", [P, G], FP32)) for i in range(2)]
        U = [c.enter_context(nc.psum_tensor(f"ex_U{i}", [P, G], FP32)) for i in range(UP)]
        Dn = [c.enter_context(nc.psum_tensor(f"ex_D{i}", [P, D], FP32)) for i in range(2)]
        ident_in = sem("ident_in")
        w_in = sem("w_in")
        ids_in = sem("ids_in")
        small_in = sem("small_in")
        x_loaded = [sem(f"x_loaded{i}") for i in range(2)]
        ids_kept = sem("ids_kept")
        cleared = sem("cleared")
        t_full = sem("t_full")
        x_hi = sem("x_hi")
        x_lo = sem("x_lo")
        gate_ready = sem("gate_ready")
        chosen_ready = sem("chosen_ready")
        w_hi = sem("w_hi")
        w_lo = sem("w_lo")
        u_full = sem("u_full")
        u_done = sem("u_done")
        h_lo = sem("h_lo")
        d_full = sem("d_full")
        d_done = sem("d_done")
        o_ready = sem("o_ready")
        added = sem("added")
        block = c.enter_context(nc.Block())

        def pairwise(eng, body):
            def pair(e0):
                for j in range(2):
                    for ch in range(NC):
                        body(e0 + j, j, ch)
            pair(0)
            with eng.Fori(1, E // 2 - 1) as it:
                pair(it * 2)
            pair(E - 2)

        def par(j, ch):
            return (NC * j + ch) % 2

        def shifted(e, j, ch, by):
            turns, ch2 = divmod(ch + by, NC)
            return e + turns, (j + turns) % 2, ch2

        def exists(e, ch):
            return not isinstance(e, int) or 0 <= e < E

        def first_steps(e, ch, n):
            return isinstance(e, int) and e * NC + ch < n

        def tiles_before(e, ch):
            return e * LT + starts[ch]

        def gathered(e, j, ch):
            mine = [(j2, c2) for j2 in range(2) for c2 in range(NC) if par(j2, c2) == par(j, ch)]
            per_pair = sum(parts[c2] for _, c2 in mine)
            inside = sum(parts[c2] for j2, c2 in mine if NC * j2 + c2 <= NC * j + ch)
            assert per_pair % 2 == 0
            return (e - j) * (per_pair // 2 * 16) + inside * 16

        @block.sync
        def _(sp):
            sp.dma_start(ident[:], consts["ident"]).then_inc(ident_in, 16)

            def load_w(e):
                ix = bass.ds(e, 1)
                sp.dma_start(w1_in[:], w["w1"][ix].rearrange("a (t p) n -> p (a t) n", p=P)).then_inc(w_in, 16)
                sp.dma_start(w2_in[:], w["w2"][ix].rearrange("a (t p) n -> p (a t) n", p=P)).then_inc(w_in, 16)

            def load_ids(e, j):
                sp.dma_start(ids[:, j], ids_dram[bass.ds(e, 1)].rearrange("a p b -> p (a b)")).then_inc(ids_in, 16)

            def load_small(e, j):
                ix = bass.ds(e, 1)
                sp.dma_start(b1[:, j], w["b1"][ix].rearrange("a (t p) -> p (a t)", p=P),
                             allow_slow_non_contiguous=True).then_inc(small_in, 16)
                sp.dma_start(b2[:, j], w["b2"][ix].to_broadcast([P, D])).then_inc(small_in, 16)
                sp.dma_start(mask[:, j], consts["expert_mask"][ix].to_broadcast([P, E])).then_inc(small_in, 16)

            load_ids(0, 0)
            load_w(0)
            load_small(0, 0)

            def body(e, j, ch):
                if not exists(e + 1, 0):
                    return
                if ch == 0:
                    sp.wait_ge(w_lo, 2 * (e + 1))
                    load_ids(e + 1, 1 - j)
                    load_w(e + 1)
                if ch == 1:
                    if isinstance(e, int) and e == 0:
                        sp.wait_ge(small_in, 48)
                    else:
                        sp.wait_ge(o_ready, LT * e)
                    load_small(e + 1, 1 - j)
            pairwise(sp, body)

        @block.tensor
        def _(pe):
            pe.wait_ge(ident_in, 16)

            def transpose_x(e, j, ch):
                s = e * NC + ch
                pr = par(j, ch)
                pe.wait_ge(x_loaded[pr], gathered(e, j, ch))
                for half in range(HALVES):
                    wait(pe, x_lo, s * 2 + half - 1)
                    for b, (off, n) in enumerate(tiles_of[ch]):
                        last = nc.tensor.matmul(T[half][:, off:off + n], xg[0:n, pr, b, half * P:(half + 1) * P],
                                                ident[0:n, 0:n], start=True, stop=True, is_transpose=True)
                    last.then_inc(t_full, 1)

            def up(e, j, ch):
                s = e * NC + ch
                n = widths[ch]
                if ch == 0:
                    pe.wait_ge(w_lo, 2 * (e + 1))
                pe.wait_ge(x_lo, (s + 1) * 2)
                for m in range(HT):
                    wait(pe, u_done, s * HT + m - UP + 1)
                    for t in range(HALVES):
                        last = matmul3(nc, U[m % UP][:, 0:n], w1, xT, t == 0, t == HALVES - 1,
                                       lambda w_, a, t=t, m=m: w_[:, j, a, t, m * P:(m + 1) * P],
                                       lambda x_, a, t=t: x_[:, par(j, ch), a, t, 0:n])
                    last.then_inc(u_full, 1)

            def down(e, j, ch):
                s = e * NC + ch
                pe.wait_ge(h_lo, (s + 1) * HT)
                for b, (off, n) in enumerate(tiles_of[ch]):
                    wait(pe, d_done, tiles_before(e, ch) + b - 1)
                    for t in range(HT):
                        last = matmul3(nc, Dn[(starts[ch] + b) % 2][0:n, :], hT, w2, t == 0, t == HT - 1,
                                       lambda h_, a, t=t, off=off, n=n: h_[:, par(j, ch), a, t, off:off + n],
                                       lambda w_, a, t=t: w_[:, j, a, t, :])
                    last.then_inc(d_full, 1)

            transpose_x(0, 0, 0)

            def body(e, j, ch):
                nx = shifted(e, j, ch, 1)
                if exists(nx[0], 0):
                    transpose_x(*nx)
                up(e, j, ch)
                if not first_steps(e, ch, 1):
                    down(*shifted(e, j, ch, -1))
            pairwise(pe, body)
            down(E - 1, 1, NC - 1)

        @block.scalar
        def _(act):
            def round_x(e, j, ch):
                s = e * NC + ch
                for half in range(HALVES):
                    act.wait_ge(t_full, s * 2 + half + 1)
                    if half == 0 and not first_steps(e, ch, 2):
                        act.wait_ge(u_full, (s - 1) * HT)
                    nc.scalar.copy(xT[:, par(j, ch), 0, half, :widths[ch]], T[half][:, 0:widths[ch]]).then_inc(x_hi, 1)

            def round_w(e, j, which):
                if which == 0:
                    act.wait_ge(w_in, 32 * (e + 1))
                    if not (isinstance(e, int) and e < 2):
                        act.wait_ge(d_full, LT * (e - 1))
                src, dst = ((w1_in, w1), (w2_in, w2))[which]
                nc.scalar.copy(dst[:, j, 0], src[:]).then_inc(w_hi, 1)

            round_w(0, 0, 0)
            round_w(0, 0, 1)
            round_x(0, 0, 0)

            def body(e, j, ch):
                s = e * NC + ch
                n = widths[ch]
                nx = shifted(e, j, ch, 1)
                if exists(nx[0], 0):
                    round_x(*nx)
                if ch == 0:
                    act.wait_ge(small_in, 48 * (e + 1))
                for m in range(HT):
                    act.wait_ge(u_full, s * HT + m + 1)
                    if m == 0 and not first_steps(e, ch, 2):
                        act.wait_ge(d_full, tiles_before(*shifted(e, j, ch, -1)[::2]))
                    wait(act, h_lo, s * HT + m - HR + 1)
                    nc.scalar.activation(h[:, m % HR, 0:n], U[m % UP][:, 0:n], ACT.Silu, bias=b1[:, j, m:m + 1])
                    nc.scalar.activation(hT[:, par(j, ch), 0, m, 0:n], U[m % UP][:, 0:n], ACT.Silu,
                                         bias=b1[:, j, m:m + 1]).then_inc(u_done, 1)
                if ch > 0 and exists(e + 1, 0):
                    round_w(e + 1, 1 - j, ch - 1)
            pairwise(act, body)

        @block.vector
        def _(dve):
            def gates_of(e, j, ch):
                s = e * NC + ch
                if ch == 0:
                    dve.wait_ge(small_in, 48 * (e + 1))
                dve.wait_ge(x_loaded[par(j, ch)], gathered(e, j, ch))
                wait(dve, gate_ready, s)
                if not first_steps(e, ch, NC):
                    dve.wait_ge(o_ready, tiles_before(*shifted(e, j, ch, -NC + 1)[::2]))
                nt = parts[ch]
                nc.vector.tensor_tensor(chosen[:, 0:nt, :], xg[:, par(j, ch), 0:nt, D:D + E],
                                        mask[:, j, :].unsqueeze(1).to_broadcast([P, nt, E]), ALU.mult).then_inc(chosen_ready, 1)
                dve.wait_ge(chosen_ready, s + 1)
                nc.vector.tensor_reduce(gate[:, ch, 0:nt], chosen[:, 0:nt, :], AX, ALU.add).then_inc(gate_ready, 1)

            def rest_x(e, j, ch):
                s = e * NC + ch
                n = widths[ch]
                for half in range(HALVES):
                    dve.wait_ge(x_hi, s * 2 + half + 1)
                    nc.vector.tensor_tensor(xT[:, par(j, ch), 1, half, :n], T[half][:, 0:n],
                                            xT[:, par(j, ch), 0, half, :n].bitcast(FP32), ALU.subtract).then_inc(x_lo, 1)

            def rest_w(e, j, which):
                dve.wait_ge(w_hi, 2 * e + which + 1)
                src, dst = ((w1_in, w1), (w2_in, w2))[which]
                nc.vector.tensor_tensor(dst[:, j, 1], src[:], dst[:, j, 0].bitcast(FP32), ALU.subtract).then_inc(w_lo, 1)

            def rest_h(e, j, ch):
                s = e * NC + ch
                n = widths[ch]
                for m in range(HT):
                    dve.wait_ge(u_done, s * HT + m + 1)
                    nc.vector.tensor_tensor(hT[:, par(j, ch), 1, m, 0:n], h[:, m % HR, 0:n],
                                            hT[:, par(j, ch), 0, m, 0:n].bitcast(FP32), ALU.subtract).then_inc(h_lo, 1)

            def take_o(e, j, ch):
                pr = par(j, ch)
                wait(dve, o_ready, tiles_before(e, ch))
                if not first_steps(e, ch, 2):
                    dve.wait_ge(added, tiles_before(*shifted(e, j, ch, -1)[::2]) * 16)
                for b, (_, n) in enumerate(tiles_of[ch]):
                    dve.wait_ge(d_full, tiles_before(e, ch) + b + 1)
                    nc.vector.tensor_tensor(raw[0:n, b, :], Dn[(starts[ch] + b) % 2][0:n, :],
                                            b2[0:n, j, :], ALU.add).then_inc(d_done, 1)
                dve.wait_ge(gate_ready, e * NC + ch + 1)
                for b, (_, n) in enumerate(tiles_of[ch]):
                    dve.wait_ge(d_done, tiles_before(e, ch) + b + 1)
                    nc.vector.tensor_scalar(o[0:n, pr, b, :], raw[0:n, b, :], gate[0:n, ch, b:b + 1], None,
                                            ALU.mult).then_inc(o_ready, 1)

            nc.vector.memset(scratch_p[0][:], 0.0)
            nc.vector.memset(xg[:, :, parts[-1] - 1, :], 0.0).then_inc(cleared, 1)
            rest_w(0, 0, 0)
            rest_w(0, 0, 1)
            gates_of(0, 0, 0)
            rest_x(0, 0, 0)

            def body(e, j, ch):
                nx = shifted(e, j, ch, 1)
                if exists(nx[0], 0):
                    gates_of(*nx)
                    rest_x(*nx)
                rest_h(e, j, ch)
                if ch > 0 and exists(e + 1, 0):
                    rest_w(e + 1, 1 - j, ch - 1)
                if not first_steps(e, ch, 1):
                    take_o(*shifted(e, j, ch, -1))
            pairwise(dve, body)
            take_o(E - 1, 1, NC - 1)

        @block.gpsimd
        def _(pool):
            pool.wait_ge(cleared, 1)

            def gather(e, j, ch):
                s = e * NC + ch
                pr = par(j, ch)
                waits = []
                if not first_steps(e, ch, 2):
                    waits += [(t_full, (s - 1) * 2), (gate_ready, s - 1)]
                if not first_steps(e, ch, 2 * NC):
                    waits.append((added, tiles_before(*shifted(e, j, ch, -2 * NC + 1)[::2]) * 16))
                wait_apart(nc.gpsimd, scratch_p, (ids_in, 16 * (e + 1)), *waits)
                nc.gpsimd.tensor_copy(out_ids[:, j, ch, 0:parts[ch]], ids[:, j, starts[ch]:starts[ch] + parts[ch]]).then_inc(ids_kept, 1)
                wait_apart(nc.gpsimd, scratch_p, (ids_kept, s + 1))
                for b, (_, n) in enumerate(tiles_of[ch]):
                    at = starts[ch] + b
                    nc.gpsimd.indirect_dma_start(xg[0:n, pr, b, :], None, rows_dram,
                                                 bass.IndirectOffsetOnAxis(ap=ids[0:n, j, at:at + 1], axis=0),
                                                 bounds_check=rows_dram.shape[0] - 1).then_inc(x_loaded[pr], 16)

            def scatter(e, j, ch):
                pr = par(j, ch)
                for b, (_, n) in enumerate(tiles_of[ch]):
                    at = tiles_before(e, ch) + b
                    waits = [(o_ready, at + 1)]
                    if not (isinstance(at, int) and at == 0):
                        waits.append((added, 16 * at))
                    if b == 0:
                        waits.append((ids_kept, e * NC + ch + 1))
                    wait_apart(nc.gpsimd, scratch_p, *waits)
                    nc.gpsimd.indirect_dma_start(sum_dram, bass.IndirectOffsetOnAxis(ap=out_ids[0:n, j, ch, b:b + 1], axis=0),
                                                 o[0:n, pr, b, :], None, bounds_check=sum_dram.shape[0] - 1,
                                                 compute_op=ALU.add).then_inc(added, 16)

            gather(0, 0, 0)
            gather(0, 0, 1)

            def body(e, j, ch):
                nx = shifted(e, j, ch, 2)
                if exists(nx[0], 0):
                    gather(*nx)
                if not first_steps(e, ch, 1):
                    scatter(*shifted(e, j, ch, -1))
            pairwise(pool, body)
            scatter(E - 1, 1, NC - 1)
            pool.wait_ge(added, 16 * E * LT)


def norm_block(nc, tiles, sum_dram, out_dram):
    groups = tiles // NB
    with ExitStack() as c:
        def sb(name, shape, dt=FP32):
            return c.enter_context(nc.sbuf_tensor("nm_" + name, shape, dt))

        def sem(name):
            return c.enter_context(nc.semaphore("nm_" + name))

        x = sb("x", [P, tiles, D])
        stats = sb("stats", [P, tiles, 6])
        mv = sb("mv", [P, tiles, 2])
        rstd = sb("rstd", [P, tiles])
        shift = sb("shift", [P, tiles])
        minus_half = sb("minus_half", [P, NB])
        loaded = [sem(f"loaded{i}") for i in range(groups)]
        made, stats_done, rstd_done, y_ready, dve_chain, pool_chain, stored = (
            sem(n) for n in ("made", "stats_done", "rstd_done", "y_ready", "dve_chain", "pool_chain", "stored"))
        block = c.enter_context(nc.Block())

        @block.sync
        def _(sp):
            for g in range(groups):
                sp.dma_start(x[:, g * NB:(g + 1) * NB, :],
                             sum_dram[g * G:(g + 1) * G, :].rearrange("(b p) n -> p b n", p=P)).then_inc(loaded[g], 16)
            for g in range(groups):
                sp.wait_ge(y_ready, g + 1)
                sp.dma_start(out_dram[g * G:(g + 1) * G, :].rearrange("(b p) n -> p b n", p=P),
                             x[:, g * NB:(g + 1) * NB, :]).then_inc(stored, 16)
            sp.wait_ge(stored, 16 * groups)

        @block.gpsimd
        def _(pool):
            nc.gpsimd.memset(minus_half[:], -0.5).then_inc(made, 1)
            pool.wait_ge(made, 1)
            for g in range(groups):
                ts = slice(g * NB, (g + 1) * NB)
                pool.wait_ge(stats_done, g + 1)
                nc.gpsimd.tensor_scalar(shift[:, ts], mv[:, ts, 0], -1.0, None, ALU.mult)
                nc.gpsimd.tensor_scalar(rstd[:, ts], mv[:, ts, 1], EPS, None, ALU.add).then_inc(pool_chain, 1)
                pool.wait_ge(pool_chain, 2 * g + 1)
                nc.gpsimd.tensor_tensor(rstd[:, ts], rstd[:, ts], minus_half[:], ALU.pow).then_inc(pool_chain, 1)
                pool.wait_ge(pool_chain, 2 * g + 2)
                nc.gpsimd.tensor_tensor(shift[:, ts], shift[:, ts], rstd[:, ts], ALU.mult).then_inc(rstd_done, 1)

        @block.vector
        def _(dve):
            def aggregate(g):
                dve.wait_ge(dve_chain, g + 1)
                for t in range(g * NB, (g + 1) * NB):
                    ins = nc.vector.bn_aggr(mv[:, t, :], stats[:, t, :])
                ins.then_inc(stats_done, 1)
            for g in range(groups):
                dve.wait_ge(loaded[g], 16)
                for t in range(g * NB, (g + 1) * NB):
                    ins = nc.vector.bn_stats(stats[:, t, :], x[:, t, :])
                ins.then_inc(dve_chain, 1)
                aggregate(g)

        @block.scalar
        def _(act):
            for g in range(groups):
                act.wait_ge(rstd_done, g + 1)
                for t in range(g * NB, (g + 1) * NB):
                    ins = nc.scalar.activation(x[:, t, :], x[:, t, :], ACT.Identity, bias=shift[:, t:t + 1], scale=rstd[:, t:t + 1])
                ins.then_inc(y_ready, 1)


def decoder_layer(nc, ins, out):
    tokens = ins["x"].shape[0]
    cap = -(-tokens * 12 // (10 * E))
    groups = tokens // G
    x1 = nc.dram_tensor("x1", [tokens, D], FP32, kind="Internal").ap()
    rows = nc.dram_tensor("rows", [tokens + P, D + E], FP32, kind="Internal").ap()
    total = nc.dram_tensor("total", [tokens + P, D], FP32, kind="Internal").ap()
    qk = nc.dram_tensor("qk", [2, 2, 2, HALVES, P, G], FP32, kind="Internal").ap()
    lists = nc.dram_tensor("lists", [E, P, -(-cap // P)], I32, kind="Internal").ap()
    attention_block(nc, True, groups, ins["x"], None, [x1], qk,
                    {k: ins["attn_" + k] for k in ("wq", "wk", "wv", "wo")}, ins)
    attention_block(nc, False, groups, x1, ins["ctx"], [rows[:, 0:D], total], qk,
                    {k: ins["xattn_" + k] for k in ("wq", "wk", "wv", "wo", "bq", "bk", "bv", "bo")}, ins)
    moe(nc, tokens, cap, ins, rows, total, lists, out)


def moe(nc, tokens, cap, ins, rows, total, lists, out):
    tiles = tokens // P
    with ExitStack() as c:
        logits = c.enter_context(nc.sbuf_tensor("logits", [P, tiles, E], FP32))
        logits_block(nc, tiles, rows, total, ins["wr"], ins["br"], ins["ident"], logits)
        route_block(nc, tiles, cap, logits, rows, lists, ins)
    experts_block(nc, cap, rows, lists, total, {k: ins[k] for k in ("w1", "w2", "b1", "b2")}, ins)
    norm_block(nc, tiles, total, out)


def tables(tokens):
    import numpy as np
    cap = -(-tokens * 12 // (10 * E))
    pos = np.arange(P)
    slopes = (2.0 ** (-8.0 / H * (np.arange(H, dtype=np.float32) + 1.0))).astype(np.float32)
    sel = np.zeros((P, H, P), np.float32)
    for h in range(H):
        sel[h, h, :] = sel[H + h, h, :] = -1.0
    sel_causal = sel.copy()
    for h in range(H):
        rest = slopes[h] * pos.astype(np.float32)
        for j in range(3):
            bits = rest.astype(np.float32).view(np.uint32)
            part = (bits & np.uint32(0xFFFF0000)).view(np.float32)
            sel_causal[2 * H + j, h, :] = part
            rest = rest - part
    coarse_mask = np.zeros((P, NB, P), np.float32)
    coarse_mask[2 * H:2 * H + 3] = 1.0
    for j in range(P // 2):
        sel_causal[P // 2 + j, :, 2 * j:2 * j + 2] = 1.0
        coarse_mask[P // 2 + j] = np.where(j > pos // 2, -1e30, 0.0)
    bias_tab = np.where(pos[None, None, :] > pos[:, None, None], -1e30,
                        slopes[None, :, None] * pos[None, None, :]).astype(np.float32)
    ch = P // E
    same = (pos[:, None] // ch == pos[None, :] // ch).astype(np.float32)
    before = same * (pos[:, None] < pos[None, :])
    slots = -(-cap // P) * P
    ebase = (pos // ch * slots - E * slots).astype(np.float32).reshape(P, 1)
    iota8 = np.tile(np.arange(E, dtype=np.float32) - E, (P, 1))
    return {"ident": np.eye(P, dtype=np.float32), "sel": sel.reshape(P, 4, G),
            "sel_causal": sel_causal.reshape(P, 4, G), "coarse_mask": coarse_mask.reshape(P, G),
            "bias_tab": bias_tab.astype(np.float32).reshape(P, 4, G), "same_expert": same,
            "before": before.astype(np.float32), "ebase": ebase, "iota8": iota8.astype(np.float32),
            "iota_row": np.tile(np.arange(P, dtype=np.float32), (P, 1)), "lane": pos.astype(np.float32).reshape(P, 1),
            "dummy_row": (tokens + P + pos).astype(np.float32).reshape(P, 1), "expert_mask": np.eye(E, dtype=np.float32)}


def kernel(**inputs):
    import numpy as _np
    import concourse.bacc as _bacc
    from concourse import mybir as _mybir
    from concourse.bass_utils import run_bass_kernel_spmd as _run

    a = {n: _np.asarray(v) for n, v in inputs.items()}
    b, s, d = a["x"].shape
    w_in = a["L0_attn_w_in"]
    arrays = {
        "x": a["x"].reshape(b * s, d), "ctx": a["ctx_1024"].reshape(b * s, d),
        "attn_wq": w_in[0:d].T, "attn_wk": w_in[d:2 * d].T, "attn_wv": w_in[2 * d:3 * d].T,
        "attn_wo": a["L0_attn_w_out"].T,
        "xattn_wq": a["L0_xattn_Wq"], "xattn_wk": a["L0_xattn_Wk"], "xattn_wv": a["L0_xattn_Wv"],
        "xattn_wo": a["L0_xattn_Wo"], "xattn_bq": a["L0_xattn_bq"], "xattn_bk": a["L0_xattn_bk"],
        "xattn_bv": a["L0_xattn_bv"], "xattn_bo": a["L0_xattn_bo"],
        "wr": a["L0_ffn_Wr"], "br": a["L0_ffn_br"], "w1": a["L0_ffn_W1"], "b1": a["L0_ffn_b1"],
        "w2": a["L0_ffn_W2"], "b2": a["L0_ffn_b2"], **tables(b * s)}
    nc = _bacc.Bacc("TRN2", target_bir_lowering=False, num_devices=1)
    ins, feed = {}, {}
    for name, v in arrays.items():
        v = _np.ascontiguousarray(v)
        feed["in_" + name] = v
        ins[name] = nc.dram_tensor("in_" + name, v.shape, _mybir.dt.from_np(v.dtype), kind="ExternalInput").ap()
    out = nc.dram_tensor("out", (b * s, d), _mybir.dt.float32, kind="ExternalOutput").ap()
    decoder_layer(nc, ins, out)
    r = _run(nc, [feed], core_ids=[0])
    return _np.asarray(r.results[0]["out"]).reshape(b, s, d)
```
